# Optimizing a Trainium2 kernel written in Bass

```python
import numpy as np
import jax
import jax.numpy as jnp

def _softmax(x, axis=-1):
    return jax.nn.softmax(x, axis=axis)

def _gelu(x):
    return jax.nn.gelu(x, approximate=True)

def _silu(x):
    return jax.nn.silu(x)

def _sigmoid(x):
    return jax.nn.sigmoid(x)

def _layernorm(x, axis=-1, eps=1e-05):
    m = jnp.mean(x, axis=axis, keepdims=True)
    v = jnp.var(x, axis=axis, keepdims=True)
    return (x - m) / jnp.sqrt(v + eps)

def _scatter_add(tgt, idx, src, axis=0):
    return tgt.at[idx].add(src)

def _segment_sum(src, seg, n):
    return jax.ops.segment_sum(src, seg, n)
kernel_name = 'mk_macaron_d2_jaxref_r4_bed7a2'

def setup_inputs(seed: int=0):
    np.random.seed(seed)
    _w = jnp.asarray

    def _L0_attn_setup():
        import jax, jax.numpy as jnp
        import numpy as np
        B, N, D = (4, 512, 256)
        H = 8
        DK = D // H
        DV = D // H
        DF = 2 * DK
        CHUNK = 64
        RMS_EPS = 1e-05

        def _hedgehog(x, w, b):
            y = jnp.einsum('bhnd,ed->bhne', x, w) + b
            return jnp.concatenate([jnp.exp(y), jnp.exp(-y)], axis=-1)

        def _fused_chunk_linear_attn(q, k, v):
            b, h, n, df = q.shape
            dv = v.shape[-1]
            nc = n // CHUNK

            def to_chunks(t):
                d = t.shape[-1]
                return t.reshape(b, h, nc, CHUNK, d).transpose(2, 0, 1, 3, 4)
            qc, kc, vc = (to_chunks(q), to_chunks(k), to_chunks(v))
            mask = jnp.tril(jnp.ones((CHUNK, CHUNK), dtype=bool))

            def step(S, inp):
                qi, ki, vi = inp
                attn = jnp.einsum('bhcd,bhed->bhce', qi, ki)
                attn = jnp.where(mask, attn, 0.0)
                intra = jnp.einsum('bhce,bhev->bhcv', attn, vi)
                inter = jnp.einsum('bhcd,bhdv->bhcv', qi, S)
                S = S + jnp.einsum('bhcd,bhcv->bhdv', ki, vi)
                return (S, intra + inter)
            S0 = jnp.zeros((b, h, df, dv), dtype=q.dtype)
            _, oc = jax.lax.scan(step, S0, (qc, kc, vc))
            return oc.transpose(1, 2, 0, 3, 4).reshape(b, h, n, dv)
        key = jax.random.key(seed)
        ks = jax.random.split(key, 10)
        s = D ** (-0.5)
        x = jax.random.normal(ks[0], (B, N, D), dtype=jnp.float32)
        Wq = jax.random.normal(ks[1], (D, D), dtype=jnp.float32) * s
        Wk = jax.random.normal(ks[2], (D, D), dtype=jnp.float32) * s
        Wv = jax.random.normal(ks[3], (D, D), dtype=jnp.float32) * s
        Wo = jax.random.normal(ks[4], (D, D), dtype=jnp.float32) * s
        eye = jnp.eye(DK, dtype=jnp.float32)
        fmq_w = eye + 0.02 * jax.random.normal(ks[5], (DK, DK), dtype=jnp.float32)
        fmq_b = 0.02 * jax.random.normal(ks[6], (DK,), dtype=jnp.float32)
        fmk_w = eye + 0.02 * jax.random.normal(ks[7], (DK, DK), dtype=jnp.float32)
        fmk_b = 0.02 * jax.random.normal(ks[8], (DK,), dtype=jnp.float32)
        rms_w = 1.0 + 0.1 * jax.random.normal(ks[9], (DV,), dtype=jnp.float32)
        return {'x': x, 'Wq': Wq, 'Wk': Wk, 'Wv': Wv, 'Wo': Wo, 'fmq_w': fmq_w, 'fmq_b': fmq_b, 'fmk_w': fmk_w, 'fmk_b': fmk_b, 'rms_w': rms_w}
    _L0_attn_in = _L0_attn_setup()

    def _L0_ffn_setup():
        import jax, jax.numpy as jnp
        import numpy as np
        QMAX = 127.0

        def _quant_dequant(w):
            scale = jnp.max(jnp.abs(w), axis=-1, keepdims=True) / QMAX
            scale = jnp.maximum(scale, 1e-08)
            q = jnp.clip(jnp.round(w / scale), -QMAX, QMAX)
            return q * scale
        key = jax.random.key(seed)
        ks = jax.random.split(key, 7)
        B, S, D, F, E, NS = (2, 512, 256, 512, 8, 1)
        std = 1.0 / np.sqrt(D)
        x = jax.random.normal(ks[0], (B, S, D), dtype=jnp.float32)
        router_w = _quant_dequant(jax.random.normal(ks[1], (E, D), dtype=jnp.float32) * std)
        router_b = jnp.zeros((E,), dtype=jnp.float32)
        w_up = _quant_dequant(jax.random.normal(ks[2], (E, F, D), dtype=jnp.float32) * std)
        w_down = _quant_dequant(jax.random.normal(ks[3], (E, D, F), dtype=jnp.float32) / np.sqrt(F))
        shared_w_up = _quant_dequant(jax.random.normal(ks[4], (NS, F, D), dtype=jnp.float32) * std)
        shared_w_down = _quant_dequant(jax.random.normal(ks[5], (NS, D, F), dtype=jnp.float32) / np.sqrt(F))
        return {'x': x, 'router_w': router_w, 'router_b': router_b, 'w_up': w_up, 'w_down': w_down, 'shared_w_up': shared_w_up, 'shared_w_down': shared_w_down}
    _L0_ffn_in = _L0_ffn_setup()

    def _L1_attn_setup():
        import math
        import jax, jax.numpy as jnp
        import numpy as np
        B, S, D, H = (2, 512, 256, 16)
        HD = D // H
        key = jax.random.key(seed)
        k1, k2, k3 = jax.random.split(key, 3)
        h = jax.random.normal(k1, (B, S, D), dtype=jnp.float32)
        Wqvk = jax.random.normal(k2, (D, 3 * D), dtype=jnp.float32) * (1.0 / math.sqrt(D))
        Wo = jax.random.normal(k3, (D, D), dtype=jnp.float32) * (1.0 / math.sqrt(D))
        return {'h': h, 'Wqvk': Wqvk, 'Wo': Wo}
    _L1_attn_in = _L1_attn_setup()

    def _L1_ffn_setup():
        import jax, jax.numpy as jnp
        import numpy as np
        import math
        BETA = 0.9
        THRESHOLD = 1.0
        NUM_STEPS = 5
        ALPHA = 2.0

        @jax.custom_vjp
        def spike_fn(u):
            return (u > 0).astype(u.dtype)

        def _spike_fwd(u):
            return (spike_fn(u), u)

        def _spike_bwd(u, g):
            s = jnp.pi / 2.0 * ALPHA * u
            return (g * (ALPHA / 2.0) / (1.0 + s * s),)
        spike_fn.defvjp(_spike_fwd, _spike_bwd)
        key = jax.random.key(seed)
        k1, k2, k3 = jax.random.split(key, 3)
        n_embd = 256
        x = jax.random.normal(k1, (4, 512, n_embd), dtype=jnp.float32)
        W_fc = jax.random.normal(k2, (4 * n_embd, n_embd), dtype=jnp.float32) / math.sqrt(n_embd)
        W_proj = jax.random.normal(k3, (n_embd, 4 * n_embd), dtype=jnp.float32) / math.sqrt(4 * n_embd)
        return {'x': x, 'W_fc': W_fc, 'W_proj': W_proj}
    _L1_ffn_in = _L1_ffn_setup()
    _d = {'L0_attn_x': _L0_attn_in['x'], 'L0_attn_Wq': _L0_attn_in['Wq'], 'L0_attn_Wk': _L0_attn_in['Wk'], 'L0_attn_Wv': _L0_attn_in['Wv'], 'L0_attn_Wo': _L0_attn_in['Wo'], 'L0_attn_fmq_w': _L0_attn_in['fmq_w'], 'L0_attn_fmq_b': _L0_attn_in['fmq_b'], 'L0_attn_fmk_w': _L0_attn_in['fmk_w'], 'L0_attn_fmk_b': _L0_attn_in['fmk_b'], 'L0_attn_rms_w': _L0_attn_in['rms_w'], 'L0_ffn_router_w': _L0_ffn_in['router_w'], 'L0_ffn_router_b': _L0_ffn_in['router_b'], 'L0_ffn_w_up': _L0_ffn_in['w_up'], 'L0_ffn_w_down': _L0_ffn_in['w_down'], 'L0_ffn_shared_w_up': _L0_ffn_in['shared_w_up'], 'L0_ffn_shared_w_down': _L0_ffn_in['shared_w_down'], 'L1_attn_Wqvk': _L1_attn_in['Wqvk'], 'L1_attn_Wo': _L1_attn_in['Wo'], 'L1_ffn_W_fc': _L1_ffn_in['W_fc'], 'L1_ffn_W_proj': _L1_ffn_in['W_proj']}
    _x0 = _d['L0_attn_x']
    _d['L0_attn_x'] = jax.random.normal(jax.random.fold_in(jax.random.key(seed), 1), (1, 4096, 256), dtype=_x0.dtype)
    del _x0
    return _d

def reference(L0_attn_x, L0_attn_Wq, L0_attn_Wk, L0_attn_Wv, L0_attn_Wo, L0_attn_fmq_w, L0_attn_fmq_b, L0_attn_fmk_w, L0_attn_fmk_b, L0_attn_rms_w, L0_ffn_router_w, L0_ffn_router_b, L0_ffn_w_up, L0_ffn_w_down, L0_ffn_shared_w_up, L0_ffn_shared_w_down, L1_attn_Wqvk, L1_attn_Wo, L1_ffn_W_fc, L1_ffn_W_proj):

    def _L0_attn_ref(x, Wq, Wk, Wv, Wo, fmq_w, fmq_b, fmk_w, fmk_b, rms_w):
        import jax, jax.numpy as jnp
        import numpy as np
        B, N, D = (4, 512, 256)
        H = 8
        DK = D // H
        DV = D // H
        DF = 2 * DK
        CHUNK = 64
        RMS_EPS = 1e-05

        def _hedgehog(x, w, b):
            y = jnp.einsum('bhnd,ed->bhne', x, w) + b
            return jnp.concatenate([jnp.exp(y), jnp.exp(-y)], axis=-1)

        def _fused_chunk_linear_attn(q, k, v):
            b, h, n, df = q.shape
            dv = v.shape[-1]
            nc = n // CHUNK

            def to_chunks(t):
                d = t.shape[-1]
                return t.reshape(b, h, nc, CHUNK, d).transpose(2, 0, 1, 3, 4)
            qc, kc, vc = (to_chunks(q), to_chunks(k), to_chunks(v))
            mask = jnp.tril(jnp.ones((CHUNK, CHUNK), dtype=bool))

            def step(S, inp):
                qi, ki, vi = inp
                attn = jnp.einsum('bhcd,bhed->bhce', qi, ki)
                attn = jnp.where(mask, attn, 0.0)
                intra = jnp.einsum('bhce,bhev->bhcv', attn, vi)
                inter = jnp.einsum('bhcd,bhdv->bhcv', qi, S)
                S = S + jnp.einsum('bhcd,bhcv->bhdv', ki, vi)
                return (S, intra + inter)
            S0 = jnp.zeros((b, h, df, dv), dtype=q.dtype)
            _, oc = jax.lax.scan(step, S0, (qc, kc, vc))
            return oc.transpose(1, 2, 0, 3, 4).reshape(b, h, n, dv)
        b, n, d = x.shape
        split = lambda t: t.reshape(b, n, H, -1).transpose(0, 2, 1, 3)
        q = split(x @ Wq.T)
        k = split(x @ Wk.T)
        v = split(x @ Wv.T)
        q = _hedgehog(q, fmq_w, fmq_b)
        k = _hedgehog(k, fmk_w, fmk_b)
        scale = q.shape[-1] ** (-0.5)
        o = _fused_chunk_linear_attn(q * scale, k, v)
        o = o * jax.lax.rsqrt(jnp.mean(o * o, axis=-1, keepdims=True) + RMS_EPS) * rms_w
        o = o.transpose(0, 2, 1, 3).reshape(b, n, H * DV)
        return o @ Wo.T

    def _L0_ffn_ref(x, router_w, router_b, w_up, w_down, shared_w_up, shared_w_down):
        import jax, jax.numpy as jnp
        import numpy as np
        QMAX = 127.0

        def _quant_dequant(w):
            scale = jnp.max(jnp.abs(w), axis=-1, keepdims=True) / QMAX
            scale = jnp.maximum(scale, 1e-08)
            q = jnp.clip(jnp.round(w / scale), -QMAX, QMAX)
            return q * scale
        B, S, D = x.shape
        E = router_w.shape[0]
        TOPK = 2
        xt = x.reshape(-1, D)
        logits = xt @ router_w.T + router_b
        probs = jax.nn.softmax(logits, axis=-1)
        top_vals, top_idx = jax.lax.top_k(probs, TOPK)
        top_vals = top_vals / jnp.sum(top_vals, axis=-1, keepdims=True)
        combine = jnp.sum(jax.nn.one_hot(top_idx, E, dtype=xt.dtype) * top_vals[..., None], axis=1)
        h = jnp.einsum('td,efd->tef', xt, w_up)
        y = jnp.einsum('tef,edf->ted', jax.nn.silu(h), w_down)
        out = jnp.einsum('ted,te->td', y, combine)
        hs = jnp.einsum('td,sfd->tsf', xt, shared_w_up)
        out = out + jnp.einsum('tsf,sdf->td', jax.nn.silu(hs), shared_w_down)
        return out.reshape(B, S, D)

    def _L1_attn_ref(h, Wqvk, Wo):
        import math
        import jax, jax.numpy as jnp
        import numpy as np
        B, S, D, H = (2, 512, 256, 16)
        HD = D // H
        b, s, d = h.shape
        qvk = (h @ Wqvk).reshape(b, s, 3, H, HD)
        q, v, k = (qvk[:, :, 0], qvk[:, :, 1], qvk[:, :, 2])
        scores = jnp.einsum('bshi,bthi->bsth', q, k)
        mask = jnp.where(jnp.arange(s)[None, :] > jnp.arange(s)[:, None], jnp.float32(-jnp.inf), jnp.float32(0.0))
        scores = scores + mask[None, :, :, None]
        scores = scores / math.sqrt(d)
        weights = jax.nn.softmax(scores, axis=2)
        wv = jnp.einsum('bsth,bthi->bshi', weights, v).reshape(b, s, d)
        return wv @ Wo

    def _L1_ffn_ref(x, W_fc, W_proj):
        import jax, jax.numpy as jnp
        import numpy as np
        import math
        BETA = 0.9
        THRESHOLD = 1.0
        NUM_STEPS = 5
        ALPHA = 2.0

        @jax.custom_vjp
        def spike_fn(u):
            return (u > 0).astype(u.dtype)

        def _spike_fwd(u):
            return (spike_fn(u), u)

        def _spike_bwd(u, g):
            s = jnp.pi / 2.0 * ALPHA * u
            return (g * (ALPHA / 2.0) / (1.0 + s * s),)
        spike_fn.defvjp(_spike_fwd, _spike_bwd)
        h = jnp.square(jax.nn.relu(jnp.einsum('bsd,fd->bsf', x, W_fc)))
        y = jnp.einsum('bsf,df->bsd', h, W_proj)

        def step(mem, _):
            reset = jax.lax.stop_gradient(spike_fn(mem - THRESHOLD))
            mem_new = BETA * mem + y - reset * THRESHOLD
            spk = spike_fn(mem_new - THRESHOLD)
            return (mem_new, spk)
        mem0 = jnp.zeros_like(y)
        _, spks = jax.lax.scan(step, mem0, None, length=NUM_STEPS)
        return jnp.sum(spks, axis=0) / NUM_STEPS
    x = L0_attn_x
    x = x + 0.5 * _L0_ffn_ref(_layernorm(x, axis=-1), L0_ffn_router_w, L0_ffn_router_b, L0_ffn_w_up, L0_ffn_w_down, L0_ffn_shared_w_up, L0_ffn_shared_w_down)
    x = x + _L0_attn_ref(_layernorm(x, axis=-1), L0_attn_Wq, L0_attn_Wk, L0_attn_Wv, L0_attn_Wo, L0_attn_fmq_w, L0_attn_fmq_b, L0_attn_fmk_w, L0_attn_fmk_b, L0_attn_rms_w)
    x = x + 0.5 * _L0_ffn_ref(_layernorm(x, axis=-1), L0_ffn_router_w, L0_ffn_router_b, L0_ffn_w_up, L0_ffn_w_down, L0_ffn_shared_w_up, L0_ffn_shared_w_down)
    x = x + 0.5 * _L1_ffn_ref(_layernorm(x, axis=-1), L1_ffn_W_fc, L1_ffn_W_proj)
    x = x + _L1_attn_ref(_layernorm(x, axis=-1), L1_attn_Wqvk, L1_attn_Wo)
    x = x + 0.5 * _L1_ffn_ref(_layernorm(x, axis=-1), L1_ffn_W_fc, L1_ffn_W_proj)
    return x

_drawn_inputs = setup_inputs


def setup_inputs(seed=0):
    import zlib

    import numpy as np

    out = dict(_drawn_inputs(seed))
    spreads = {'L0_ffn_router_b': (0.0, 0.1)}
    factors = {'L0_attn_fmq_b': 8.0, 'L0_attn_fmk_b': 8.0}
    for name, (base, spread) in spreads.items():
        noise = np.random.default_rng([zlib.crc32(name.encode()), seed]).standard_normal(out[name].shape)
        drawn = base * np.exp(spread * noise) if base else spread * noise
        out[name] = jnp.asarray(drawn.astype(out[name].dtype))
    for name, factor in factors.items():
        out[name] = (out[name] * factor).astype(out[name].dtype)
    return out
```

```python
from contextlib import ExitStack

import concourse.bass as bass
from concourse import mybir

P = 128
D = 256
DC = D // P
EPS = 1e-5
F32 = mybir.dt.float32
F32R = mybir.dt.float32r
BF16 = mybir.dt.bfloat16
U32 = mybir.dt.uint32
ALU = mybir.AluOpType
ACT = mybir.ActivationFunctionType
AX_X = mybir.AxisListType.X


class Scope:

    def __init__(self, nc, ctx, stage):
        self.nc, self.ctx, self.stage = nc, ctx, stage
        self.sems = []
        ctx.callback(self.release)

    def release(self):
        if self.sems:
            self.nc.clear_and_free_semaphores(self.sems)
            self.nc.all_engine_barrier()

    def sb(self, name, shape, dt=F32):
        return self.ctx.enter_context(self.nc.sbuf_tensor(f"{self.stage}_{name}", shape, dt))

    def ps(self, name, shape, dt=F32):
        return self.ctx.enter_context(self.nc.psum_tensor(f"{self.stage}_{name}", shape, dt))

    def sem(self, name):
        self.sems.append(self.nc.alloc_semaphore(name=f"{self.stage}_{name}"))
        return self.sems[-1]


def stats_buffers(s, T):
    return dict(
        raw=s.sb("ln_raw", [P, T, 6]), tmp=s.sb("ln_tmp", [P, 4, T]), mean=s.sb("ln_mean", [P, T]),
        var=s.sb("ln_var", [P, T]), std=s.sb("ln_std", [P, T]), rstd=s.sb("ln_rstd", [P, T]),
        raw_done=s.sem("ln_raw_done"), step=s.sem("ln_step"), var_done=s.sem("ln_var_done"),
        std_done=s.sem("ln_std_done"), rstd_done=s.sem("ln_rstd_done"))


def dve_stats(dve, x, T, ln):
    unroll = 4
    with dve.Fori(0, T // unroll) as i:
        for k in range(unroll):
            dve.bn_stats(ln["raw"][:, i * unroll + k, :], x[:, i * unroll + k, :]).then_inc(ln["raw_done"], 1)
    raw, tmp, step = ln["raw"], ln["tmp"], ln["step"]
    mean_sum, mean_diff, dev_sum, diff_sq = (tmp[:, k, :] for k in range(4))
    dve.wait_ge(ln["raw_done"], T)
    dve.tensor_tensor(mean_sum, raw[:, :, 1], raw[:, :, 4], ALU.add).then_inc(step, 1)
    dve.tensor_tensor(mean_diff, raw[:, :, 1], raw[:, :, 4], ALU.subtract).then_inc(step, 1)
    dve.tensor_tensor(dev_sum, raw[:, :, 2], raw[:, :, 5], ALU.add).then_inc(step, 1)
    dve.wait_ge(step, 3)
    dve.tensor_scalar(ln["mean"][:, :], mean_sum, 0.5, None, ALU.mult).then_inc(step, 1)
    dve.scalar_tensor_tensor(out=diff_sq, in0=mean_diff, scalar=0.25, in1=mean_diff,
                             op0=ALU.mult, op1=ALU.mult).then_inc(step, 1)
    dve.wait_ge(step, 5)
    dve.scalar_tensor_tensor(out=ln["var"][:, :], in0=dev_sum, scalar=1.0 / D, in1=diff_sq,
                             op0=ALU.mult, op1=ALU.add).then_inc(ln["var_done"], 1)
    dve.wait_ge(ln["std_done"], 1)
    dve.reciprocal(ln["rstd"][:, :], ln["std"][:, :]).then_inc(ln["rstd_done"], 1)
    dve.wait_ge(ln["rstd_done"], 1)


def act_std(act, ln, eps_col):
    act.wait_ge(ln["var_done"], 1)
    act.activation(ln["std"][:, :], ln["var"][:, :], ACT.Sqrt, bias=eps_col).then_inc(ln["std_done"], 1)


def dve_normalise(dve, out, x, ln, t):
    return dve.tensor_scalar(out, x[:, t, :], ln["mean"][:, bass.ds(t, 1)], ln["rstd"][:, bass.ds(t, 1)],
                             ALU.subtract, ALU.mult)


def stage_load(nc, core, x_dram, const_dram):
    with ExitStack() as ctx:
        s = Scope(nc, ctx, "load")
        arrived = s.sem("arrived")
        block = ctx.enter_context(nc.Block())

        @block.sync
        def _(sp):
            xv = x_dram.rearrange("(t p) d -> p t d", p=P)
            T = core["T"]
            for q in range(4):
                sp.dma_start(core["x"][:, q * T // 4:(q + 1) * T // 4, :],
                             xv[:, q * T // 4:(q + 1) * T // 4, :]).then_inc(arrived, 16)
            for name in ("ident", "cols", "iota8"):
                sp.dma_start(core[name][:, :], const_dram[name]).then_inc(arrived, 16)
            sp.wait_ge(arrived, 16 * 7)


def stage_store(nc, core, out_dram):
    with ExitStack() as ctx:
        s = Scope(nc, ctx, "store")
        stored = s.sem("stored")
        block = ctx.enter_context(nc.Block())

        @block.sync
        def _(sp):
            ov = out_dram.rearrange("(t p) d -> p t d", p=P)
            T = core["T"]
            for q in range(4):
                sp.dma_start(ov[:, q * T // 4:(q + 1) * T // 4, :],
                             core["x"][:, q * T // 4:(q + 1) * T // 4, :]).then_inc(stored, 16)
            sp.wait_ge(stored, 16 * 4)


def stage_norm(nc, core, stage, x1, x2, router):
    T, x = core["T"], core["x"]
    with ExitStack() as ctx:
        s = Scope(nc, ctx, stage)
        ln = stats_buffers(s, T)
        xn = s.sb("xn", [P, 2, D])
        tr = [s.ps(f"tr{k}", [P, DC, P]) for k in range(2)]
        xn_ready, tr_done = s.sem("xn_ready"), s.sem("tr_done")
        x1_done, x2_done = s.sem("x1_done"), s.sem("x2_done")
        if router:
            E = router["E"]
            rw = s.sb("rw", [P, DC, E])
            rb = s.sb("rb", [P, E])
            xs = s.sb("xs", [P, 2, DC, P])
            lg = s.sb("lg", [P, T, E])
            top = s.sb("top", [P, T, 8])
            top_at = s.sb("top_at", [P, T, 8], U32)
            at_f = s.sb("at_f", [P, T, 2])
            gap = s.sb("gap", [P, T])
            ex = s.sb("ex", [P, T])
            den = s.sb("den", [P, T])
            wt = s.sb("wt", [P, 3, T])
            pick = s.sb("pick", [P, 2, T, E])
            lgp = [s.ps(f"lgp{k}", [P, E]) for k in range(2)]
            rw_in, xs_done, router_done = s.sem("rw_in"), s.sem("xs_done"), s.sem("router_done")
            lg_done, top_done, at_done = s.sem("lg_done"), s.sem("top_done"), s.sem("at_done")
            gap_done, ex_done, wstep = s.sem("gap_done"), s.sem("ex_done"), s.sem("wstep")
        block = ctx.enter_context(nc.Block())

        if router:
            @block.sync
            def _(sp):
                sp.dma_start(rw[:, :, :], router["w"]).then_inc(rw_in, 16)
                sp.dma_start(rb[:, :], router["b"]).then_inc(rw_in, 16)
                sp.wait_ge(rw_in, 32)

        def pairs(eng, step):
            with eng.Fori(0, T // 2 - 1) as i:
                for k in range(2):
                    step(i * 2 + k, k, True)
            for k in range(2):
                step(T - 2 + k, k, False)

        @block.vector
        def _(dve):
            dve_stats(dve, x, T, ln)
            for k in range(2):
                dve_normalise(dve, xn[:, k, :], x, ln, k).then_inc(xn_ready, 1)

            def step(t, k, has_next):
                dve.wait_ge(x1_done, t + 1)
                if router:
                    dve.wait_ge(xs_done, t + 1)
                dve.tensor_tensor(x2[:, :, bass.ts(t, P)], tr[k][:, :, :],
                                  x1[:, :, bass.ts(t, P)].bitcast(F32), ALU.subtract).then_inc(x2_done, 1)
                if has_next:
                    dve_normalise(dve, xn[:, k, :], x, ln, t + 2).then_inc(xn_ready, 1)
                if router:
                    dve.wait_ge(router_done, t + 3)
                    dve.tensor_tensor(lg[:, t, :], lgp[k][:, :], rb[:, :], ALU.add).then_inc(lg_done, 1)

            if router:
                dve.sem_inc(lg_done, 2)
                dve.wait_ge(rw_in, 32)
            pairs(dve, step)
            if not router:
                return
            dve.wait_ge(lg_done, T + 2)
            for t in range(T):
                dve.max(top[:, t, :], lg[:, t, :]).then_inc(top_done, 1)
            dve.wait_ge(top_done, T)
            for t in range(T):
                dve.max_index(top_at[:, t, :], top[:, t, :], lg[:, t, :]).then_inc(at_done, 1)
            dve.tensor_tensor(gap[:, :], top[:, :, 1], top[:, :, 0], ALU.subtract).then_inc(gap_done, 1)
            dve.wait_ge(at_done, T)
            dve.tensor_copy(at_f[:, :, :], top_at[:, :, 0:2]).then_inc(wstep, 1)
            dve.wait_ge(ex_done, 1)
            dve.tensor_scalar(den[:, :], ex[:, :], 1.0, None, ALU.add).then_inc(wstep, 1)
            dve.wait_ge(wstep, 2)
            dve.reciprocal(wt[:, 2, :], den[:, :]).then_inc(wstep, 1)
            dve.wait_ge(wstep, 3)
            dve.tensor_scalar(wt[:, 0, :], wt[:, 2, :], 0.5, None, ALU.mult).then_inc(wstep, 1)
            dve.wait_ge(wstep, 4)
            dve.tensor_tensor(wt[:, 1, :], ex[:, :], wt[:, 0, :], ALU.mult).then_inc(wstep, 1)
            for k in range(2):
                dve.tensor_tensor(pick[:, k, :, :], core["iota8"][:, :].unsqueeze(1).broadcast_to([P, T, E]),
                                  at_f[:, :, k:k + 1].broadcast_to([P, T, E]), ALU.is_equal).then_inc(wstep, 1)
            dve.wait_ge(wstep, 7)
            for k in range(2):
                dve.tensor_tensor(pick[:, k, :, :], pick[:, k, :, :],
                                  wt[:, k, :].unsqueeze(2).broadcast_to([P, T, E]), ALU.mult).then_inc(wstep, 1)
            dve.wait_ge(wstep, 9)
            dve.tensor_tensor(core["comb"][:, :, 0:E], pick[:, 0, :, :], pick[:, 1, :, :],
                              ALU.add).then_inc(wstep, 1)
            dve.memset(core["comb"][:, :, E:E + 1], 0.5).then_inc(wstep, 1)

        @block.scalar
        def _(act):
            act_std(act, ln, core["cols"][:, 0:1])

            def step(t, k, has_next):
                act.wait_ge(tr_done, t + 1)
                act.activation(x1[:, :, bass.ts(t, P)], tr[k][:, :, :], ACT.Copy).then_inc(x1_done, 1)
                if router:
                    act.wait_ge(router_done, t + 1)
                    act.activation(xs[:, k, :, :], tr[k][:, :, :], ACT.Copy).then_inc(xs_done, 1)

            pairs(act, step)
            if router:
                act.wait_ge(gap_done, 1)
                act.activation(ex[:, :], gap[:, :], ACT.Exp).then_inc(ex_done, 1)

        @block.tensor
        def _(pe):
            def transposes(t, k):
                pe.wait_ge(xn_ready, t + 1)
                for c in range(DC):
                    mm = pe.transpose(tr[k][:, c, :], xn[:, k, c * P:(c + 1) * P], core["ident"][:, :])
                mm.then_inc(tr_done, 1)

            def logits(t, k):
                pe.wait_ge(xs_done, t + 1)
                pe.wait_ge(lg_done, t + 1)
                for c in range(DC):
                    mm = pe.matmul(lgp[k][:, :], xs[:, k, c, :], rw[:, c, :], start=(c == 0), stop=(c == DC - 1))
                mm.then_inc(router_done, 1)

            if router:
                pe.sem_inc(router_done, 2)
                pe.wait_ge(rw_in, 32)
            for k in range(2):
                transposes(k, k)

            def step(t, k, has_next):
                if router:
                    logits(t, k)
                if has_next:
                    pe.wait_ge(x2_done, t + 1)
                    transposes(t + 2, k)

            pairs(pe, step)


def stage_experts(nc, core, stage, x1, x2, up_dram, dn_dram, NE):
    T, x, comb = core["T"], core["x"], core["comb"]
    F = up_dram.shape[2] // DC
    FT = F // P
    TT = 4
    G = T // TT
    N = TT * P
    with ExitStack() as ctx:
        s = Scope(nc, ctx, stage)
        raw_up, raw_dn = s.sb("raw_up", [P, DC * F]), s.sb("raw_dn", [P, FT * D])
        up1, up2 = s.sb("up1", [P, DC * F], F32R), s.sb("up2", [P, DC * F], F32R)
        dn1, dn2 = s.sb("dn1", [P, FT * D], F32R), s.sb("dn2", [P, FT * D], F32R)
        h = s.sb("h", [P, FT, N])
        h1, h2 = s.sb("h1", [P, FT, N], F32R), s.sb("h2", [P, FT, N], F32R)
        hp = [s.ps(f"hp{f}", [P, N]) for f in range(FT)]
        yp = [s.ps(f"yp{t}", [P, D]) for t in range(TT)]
        up_in, dn_in = s.sem("up_in"), s.sem("dn_in")
        up1_done, up_split, dn1_done, dn_split = (s.sem(n) for n in ("up1_done", "up_split", "dn1_done", "dn_split"))
        ups_done, hp_ready, act_done, h_split = (s.sem(n) for n in ("ups_done", "hp_ready", "act_done", "h_split"))
        h_used, yp_ready, y_added = s.sem("h_used"), s.sem("yp_ready"), s.sem("y_added")
        block = ctx.enter_context(nc.Block())
        up_parts = ((up1, x1), (up1, x2), (up2, x1))

        @block.sync
        def _(sp):
            with sp.Fori(0, NE) as e:
                sp.wait_ge(up_split, e + 1)
                sp.dma_start(raw_up[:, :], up_dram[e, :, :]).then_inc(up_in, 16)
                sp.wait_ge(dn_split, e + 1)
                sp.dma_start(raw_dn[:, :], dn_dram[e, :, :]).then_inc(dn_in, 16)

        @block.tensor
        def _(pe):
            with pe.Fori(0, NE) as e:
                with pe.Fori(0, G) as g:
                    n = e * G + g
                    pe.wait_ge(up_split, e + 2)
                    for f in range(FT):
                        pe.wait_ge(act_done, n * FT + f + 1)
                        k = 0
                        for w, v in up_parts:
                            for c in range(DC):
                                mm = pe.matmul(hp[f][:, :], w[:, c * F + f * P:c * F + (f + 1) * P],
                                               v[:, c, bass.ts(g, N)], start=(k == 0), stop=(k == 5))
                                k += 1
                        mm.then_inc(hp_ready, 1)
                    pe.sem_inc(ups_done, 1)
                    pe.wait_ge(dn_split, e + 2)
                    for f in range(FT):
                        pe.wait_ge(h_split, n * FT + f + 1 + FT)
                        for t in range(TT):
                            if f == 0:
                                pe.wait_ge(y_added, n * TT + t + 1 + T - TT)
                            for k, (a, b) in enumerate(((h1, dn1), (h1, dn2), (h2, dn1))):
                                mm = pe.matmul(yp[t][:, :], a[:, f, t * P:(t + 1) * P], b[:, f * D:(f + 1) * D],
                                               start=(f == 0 and k == 0), stop=(f == FT - 1 and k == 2))
                            if f == FT - 1:
                                mm.then_inc(yp_ready, 1)
                        if f < FT - 1:
                            mm.then_inc(h_used, 1)
                        else:
                            pe.sem_inc(h_used, 1)

        @block.scalar
        def _(act):
            act.sem_inc(act_done, FT)
            with act.Fori(0, NE) as e:
                with act.Fori(0, G) as g:
                    n = e * G + g
                    for f in range(FT):
                        act.wait_ge(hp_ready, n * FT + f + 1)
                        act.wait_ge(h_split, n * FT + f + 1)
                        act.activation(h[:, f, :], hp[f][:, :], ACT.Silu)
                        act.wait_ge(h_used, n * FT + f + 1)
                        act.activation(h1[:, f, :], hp[f][:, :], ACT.Silu).then_inc(act_done, 1)

        @block.vector
        def _(dve):
            dve.sem_inc(up_split, 1)
            dve.sem_inc(dn_split, 1)
            dve.sem_inc(h_split, FT)
            dve.sem_inc(h_used, FT)
            dve.sem_inc(y_added, T)

            def split_up(e):
                dve.wait_ge(up_in, e * 16 + 16)
                dve.tensor_copy(up1[:, :], raw_up[:, :]).then_inc(up1_done, 1)
                dve.wait_ge(up1_done, e + 1)
                dve.tensor_tensor(up2[:, :], raw_up[:, :], up1[:, :].bitcast(F32), ALU.subtract).then_inc(up_split, 1)

            def split_dn(e):
                dve.wait_ge(dn_in, e * 16 + 16)
                dve.tensor_copy(dn1[:, :], raw_dn[:, :]).then_inc(dn1_done, 1)
                dve.wait_ge(dn1_done, e + 1)
                dve.tensor_tensor(dn2[:, :], raw_dn[:, :], dn1[:, :].bitcast(F32), ALU.subtract).then_inc(dn_split, 1)

            def group(e, g, last_of_expert):
                n = e * G + g
                for f in range(FT):
                    dve.wait_ge(act_done, n * FT + f + 1 + FT)
                    dve.wait_ge(h_used, n * FT + f + 1)
                    dve.tensor_tensor(h2[:, f, :], h[:, f, :], h1[:, f, :].bitcast(F32),
                                      ALU.subtract).then_inc(h_split, 1)
                if last_of_expert:
                    dve.wait_ge(ups_done, n + 1)
                    split_up(e + 1)
                for t in range(TT):
                    dve.wait_ge(yp_ready, n * TT + t + 1)
                    dve.wait_ge(y_added, n * TT + t + 1)
                    tile = g * TT + t
                    dve.scalar_tensor_tensor(out=x[:, tile, :], in0=yp[t][:, :],
                                             scalar=comb[:, tile, bass.ds(e, 1)], in1=x[:, tile, :],
                                             op0=ALU.mult, op1=ALU.add).then_inc(y_added, 1)
                if last_of_expert:
                    dve.wait_ge(h_used, n * FT + FT + FT)
                    split_dn(e + 1)

            split_up(0)
            split_dn(0)
            with dve.Fori(0, NE - 1) as e:
                with dve.Fori(0, G - 1) as g:
                    group(e, g, False)
                group(e, G - 1, True)
            with dve.Fori(0, G) as g:
                group(NE - 1, g, False)


def stage_spikes(nc, core, stage, x1, x2, fc_dram, proj_dram):
    T, x = core["T"], core["x"]
    STEPS, BETA, THRESHOLD = 5, 0.9, 1.0
    F = fc_dram.shape[1] // DC
    FT = F // P
    HT = 4
    TT = 4
    G = T // TT
    N = TT * P
    with ExitStack() as ctx:
        s = Scope(nc, ctx, stage)
        raw = s.sb("raw", [P, DC * F])
        fc1, fc2 = s.sb("fc1", [P, DC * F], F32R), s.sb("fc2", [P, DC * F], F32R)
        pj1, pj2 = s.sb("pj1", [P, FT * D], F32R), s.sb("pj2", [P, FT * D], F32R)
        r = s.sb("r", [P, 2, N])
        h = s.sb("h", [P, HT, N])
        h1, h2 = s.sb("h1", [P, HT, N], F32R), s.sb("h2", [P, HT, N], F32R)
        y, mem, leak, spk = s.sb("y", [P, TT, D]), s.sb("mem", [P, TT, D]), s.sb("leak", [P, TT, D]), s.sb("spk", [P, TT, D])
        hp = [s.ps(f"hp{f}", [P, N]) for f in range(HT)]
        yp = s.ps("yp", [P, TT, N])
        w_in, w1_done, w_split = s.sem("w_in"), s.sem("w1_done"), s.sem("w_split")
        hp_ready, relu_done, act_done, h_split = (s.sem(n) for n in ("hp_ready", "relu_done", "act_done", "h_split"))
        h_used, yp_ready, y_ready, y_free, neuron = (s.sem(n) for n in ("h_used", "yp_ready", "y_ready", "y_free", "neuron"))
        block = ctx.enter_context(nc.Block())

        @block.sync
        def _(sp):
            sp.dma_start(raw[:, :], fc_dram).then_inc(w_in, 16)
            sp.wait_ge(w_split, 1)
            sp.dma_start(raw[:, :], proj_dram).then_inc(w_in, 16)

        @block.tensor
        def _(pe):
            pe.wait_ge(w_split, 2)
            with pe.Fori(0, G) as g:
                for half in range(FT // HT):
                    for f in range(HT):
                        n = g * FT + half * HT + f
                        pe.wait_ge(act_done, n + 1)
                        k = 0
                        for w, v in ((fc1, x1), (fc1, x2), (fc2, x1)):
                            for c in range(DC):
                                at = c * F + (half * HT + f) * P
                                mm = pe.matmul(hp[f][:, :], w[:, at:at + P], v[:, c, bass.ts(g, N)],
                                               start=(k == 0), stop=(k == 5))
                                k += 1
                        mm.then_inc(hp_ready, 1)
                    for f in range(HT):
                        pe.wait_ge(h_split, g * FT + half * HT + f + 1 + HT)
                        if half == 0 and f == 0:
                            pe.wait_ge(y_ready, g + 1)
                        at = (half * HT + f) * D
                        for t in range(TT):
                            for k, (a, b) in enumerate(((h1, pj1), (h1, pj2), (h2, pj1))):
                                mm = pe.matmul(yp[:, t, 0:D], a[:, f, t * P:(t + 1) * P], b[:, at:at + D],
                                               start=(half == 0 and f == 0 and k == 0),
                                               stop=(half == 1 and f == HT - 1 and k == 2))
                        mm.then_inc(h_used, 1)

        @block.scalar
        def _(act):
            act.sem_inc(act_done, HT)
            act.sem_inc(relu_done, 2)
            act.sem_inc(y_ready, 1)

            def copy_y(g):
                act.wait_ge(h_used, g * FT + FT + HT)
                act.wait_ge(y_free, g + 1)
                act.activation(y[:, :, :], yp[:, :, 0:D], ACT.Copy).then_inc(y_ready, 1)

            def half_of(g, half):
                for f in range(HT):
                    n = g * FT + half * HT + f
                    act.wait_ge(hp_ready, n + 1)
                    act.wait_ge(act_done, n + HT - 1)
                    act.activation(r[:, f % 2, :], hp[f][:, :], ACT.Relu).then_inc(relu_done, 1)
                    act.wait_ge(relu_done, n + 3)
                    act.wait_ge(h_split, n + 1)
                    act.activation(h[:, f, :], r[:, f % 2, :], ACT.Square)
                    act.wait_ge(h_used, n + 1)
                    act.activation(h1[:, f, :], r[:, f % 2, :], ACT.Square).then_inc(act_done, 1)

            half_of(0, 0)
            half_of(0, 1)
            with act.Fori(0, G - 1) as i:
                copy_y(i)
                half_of(i + 1, 0)
                half_of(i + 1, 1)
            copy_y(G - 1)

        @block.vector
        def _(dve):
            dve.sem_inc(h_split, HT)
            dve.sem_inc(h_used, HT)
            dve.sem_inc(y_free, 1)
            for k, (a, b) in enumerate(((fc1, fc2), (pj1, pj2))):
                dve.wait_ge(w_in, 16 * (k + 1))
                dve.tensor_copy(a[:, :], raw[:, :]).then_inc(w1_done, 1)
                dve.wait_ge(w1_done, k + 1)
                dve.tensor_tensor(b[:, :], raw[:, :], a[:, :].bitcast(F32), ALU.subtract).then_inc(w_split, 1)

            def split(n, f):
                dve.wait_ge(act_done, n + 1 + HT)
                dve.wait_ge(h_used, n + 1)
                dve.tensor_tensor(h2[:, f, :], h[:, f, :], h1[:, f, :].bitcast(F32), ALU.subtract).then_inc(h_split, 1)

            def first(g):
                dve.wait_ge(y_ready, g + 2)
                return dve.tensor_scalar(spk[:, :, :], y[:, :, :], THRESHOLD, None, ALU.is_gt)

            def decay(src):
                return lambda g: dve.scalar_tensor_tensor(out=leak[:, :, :], in0=src[:, :, :], scalar=BETA,
                                                          in1=y[:, :, :], op0=ALU.mult, op1=ALU.add)

            def reset(src):
                return lambda g: dve.scalar_tensor_tensor(out=mem[:, :, :], in0=src[:, :, :], scalar=THRESHOLD,
                                                          in1=leak[:, :, :], op0=ALU.is_gt, op1=ALU.subtract,
                                                          reverse1=True)

            def count(g):
                return dve.scalar_tensor_tensor(out=spk[:, :, :], in0=mem[:, :, :], scalar=THRESHOLD,
                                                in1=spk[:, :, :], op0=ALU.is_gt, op1=ALU.add)

            def add_to_x(g):
                xg = x[:, bass.ts(g, TT), :]
                return dve.scalar_tensor_tensor(out=xg, in0=spk[:, :, :], scalar=0.5 / STEPS, in1=xg,
                                                op0=ALU.mult, op1=ALU.add)

            chain = [first]
            for k in range(1, STEPS):
                chain += [decay(y if k == 1 else mem), reset(y if k == 1 else mem), count]
            chain.append(add_to_x)
            L = len(chain)

            def neuron_steps(g, todo):
                for k in todo:
                    if k:
                        dve.wait_ge(neuron, g * L + k)
                    chain[k](g).then_inc(neuron, 1)
                if L - 1 in todo:
                    dve.wait_ge(neuron, g * L + L)
                    dve.sem_inc(y_free, 1)

            for f in range(FT):
                split(f, f % HT)
            share = [[] for _ in range(FT)]
            for k in range(L):
                share[HT * (k // (L // 2)) + min(HT - 1, k % (L // 2))].append(k)
            with dve.Fori(0, G - 1) as i:
                for f in range(FT):
                    split((i + 1) * FT + f, f % HT)
                    neuron_steps(i, share[f])
            neuron_steps(G - 1, range(L))


def wait_if(eng, sem, value):
    if not isinstance(value, int) or value > 0:
        eng.wait_ge(sem, value)


def stage_linear_attention(nc, core, stage, ins):
    T, x = core["T"], core["x"]
    H, DV, DF = 8, 32, 64
    NP = H // 2
    SCALE = DF ** -0.5
    with ExitStack() as ctx:
        s = Scope(nc, ctx, stage)
        ln = stats_buffers(s, T)
        w_nat = [s.sb(f"w{n}_nat", [P, DC, D]) for n in "qk"]
        blocks = [s.sb(f"fm{n}", [P, P]) for n in "qk"]
        b_raw = [s.sb(f"b{n}_raw", [P, 1]) for n in "qk"]
        b_col = [s.sb(f"b{n}", [P, 1]) for n in "qk"]
        w_feat = [s.sb(f"w{n}_feat", [P, DC, H, 2, 32]) for n in "qk"]
        wv, wo_raw, wo, rms = s.sb("wv", [P, DC, D]), s.sb("wo_raw", [P, DC, D]), s.sb("wo", [P, DC, D]), s.sb("rms", [P, 1])
        keep = s.sb("keep", [P, P])
        xn, xT = s.sb("xn", [P, 2, D]), s.sb("xT", [P, 2, DC, P])
        qf, kf, kt = s.sb("qf", [P, 2, NP, P]), s.sb("kf", [P, 2, NP, P]), s.sb("kt", [P, 2, NP, P])
        v = s.sb("v", [P, 2, D])
        am = s.sb("am", [P, 2, H, P])
        S = s.sb("S", [P, NP, 2 * DV])
        o, sq, on, oT = s.sb("o", [P, 2, D]), s.sb("sq", [P, 2, D]), s.sb("on", [P, 2, D]), s.sb("oT", [P, DC, P])
        ss, ms, rs = s.sb("ss", [P, 2, H]), s.sb("ms", [P, 2, H]), s.sb("rs", [P, 2, H])
        half_neg = s.sb("half_neg", [P, H])
        bank0, bank4 = s.ps("bank0", [P, 512]), s.ps("bank4", [P, 512])
        trp, vp = bank0[:, 0:D].rearrange("p (c q) -> p c q", c=DC), bank0[:, D:2 * D]
        qp, kp = s.ps("qp", [P, NP, P]), s.ps("kp", [P, NP, P])
        ktp = s.ps("ktp", [P, NP, P])
        sp_new = ktp[:, 0:2, :].rearrange("p a q -> p (a q)")
        ap = [s.ps(f"ap{k}", [P, 4, P]) for k in range(2)]
        op = s.ps("op", [P, D])
        oTp, yp = bank4[:, 0:D].rearrange("p (c q) -> p c q", c=DC), bank4[:, D:2 * D]
        w_in, fm_in, zeroed, prep, half_set = (s.sem(n) for n in ("w_in", "fm_in", "zeroed", "prep", "half_set"))
        wf_ready, wf_done = s.sem("wf_ready"), s.sem("wf_done")
        names = ("xn_ready", "tr_done", "xT_done", "q_ready", "k_ready", "v_ready", "q_done", "k_done", "v_done",
                 "kt_ready", "kt_done", "a_ready", "masked", "o_ready", "o_done", "sq_done", "S_done", "ss_done",
                 "ms_done", "rs_done", "on_done", "oT_ready", "oT_done", "y_ready", "x_done")
        m = {n: s.sem(n) for n in names}
        block = ctx.enter_context(nc.Block())

        def chunks(eng, step):
            for t in range(2):
                step(t, t, True, True)
            with eng.Fori(0, (T - 4) // 2) as i:
                for k in range(2):
                    step(i * 2 + (2 + k), k, True, True)
            step(T - 2, 0, True, False)
            step(T - 1, 1, False, False)

        @block.sync
        def _(sp):
            for dst, src in ((w_nat[0], ins["lwq"]), (w_nat[1], ins["lwk"]), (wv, ins["lwv"]), (wo_raw, ins["lwo"])):
                sp.dma_start(dst[:, :, :], src.rearrange("p (c n) -> p c n", c=DC)).then_inc(w_in, 16)
            for dst, src in ((b_raw[0], ins["lbq"]), (b_raw[1], ins["lbk"]), (rms, ins["lrms"]), (keep, ins["keep_kq"])):
                sp.dma_start(dst[:, :], src).then_inc(w_in, 16)
            sp.wait_ge(zeroed, 2)
            for n, src in enumerate((ins["lfq"], ins["lfk"])):
                for j in range(4):
                    sp.dma_start(blocks[n][32 * j:32 * j + 32, 32 * j:32 * j + 32], src).then_inc(fm_in, 16)
            sp.wait_ge(w_in, 16 * 8)
            sp.wait_ge(fm_in, 16 * 2 * 4)

        @block.gpsimd
        def _(pool):
            pool.memset(half_neg[:, :], -0.5).then_inc(half_set, 1)
            pool.wait_ge(half_set, 1)

            def step(t, k, *_):
                pool.wait_ge(m["ms_done"], t + 1)
                wait_if(pool, m["on_done"], t - 1)
                pool.tensor_tensor(rs[:, k, :], ms[:, k, :], half_neg[:, :], ALU.pow).then_inc(m["rs_done"], 1)

            chunks(pool, step)

        @block.tensor
        def _(pe):
            pe.wait_ge(w_in, 16 * 8)
            pe.wait_ge(fm_in, 16 * 2 * 4)
            for n, dst in enumerate((qp, kp)):
                for c in range(DC):
                    for j in range(DC):
                        mm = pe.matmul(dst[:, c * DC + j, :], w_nat[n][:, j, c * P:(c + 1) * P], blocks[n][:, :],
                                       start=True, stop=True)
                mm.then_inc(wf_ready, 1)
            pe.wait_ge(wf_done, 4)

            def x_transposes(t, k):
                pe.wait_ge(m["xn_ready"], t + 1)
                wait_if(pe, m["v_done"], t)
                for c in range(DC):
                    mm = pe.transpose(trp[:, c, :], xn[:, k, c * P:(c + 1) * P], core["ident"][:, :])
                mm.then_inc(m["tr_done"], 1)

            def qk(t, k):
                pe.wait_ge(m["xT_done"], t + 1)
                for n, (dst, read, ready) in enumerate(((qp, "q_done", "q_ready"), (kp, "k_done", "k_ready"))):
                    wait_if(pe, m[read], t)
                    wf = w_feat[n][:, :, :, :, :].rearrange("p c h s e -> p c (h s e)")
                    for f in range(NP):
                        for c in range(DC):
                            mm = pe.matmul(dst[:, f, :], wf[:, c, f * P:(f + 1) * P], xT[:, k, c, :],
                                           start=(c == 0), stop=(c == DC - 1))
                    mm.then_inc(m[ready], 1)

            def values(t, k):
                for c in range(DC):
                    mm = pe.matmul(vp, xT[:, k, c, :], wv[:, c, :], start=(c == 0), stop=(c == DC - 1))
                mm.then_inc(m["v_ready"], 1)

            def k_transposes(t, k):
                pe.wait_ge(m["k_done"], t + 1)
                pe.wait_ge(m["S_done"], t * 2 + 2)
                for f in range(NP):
                    mm = pe.transpose(ktp[:, f, :], kf[:, k, f, :], core["ident"][:, :])
                mm.then_inc(m["kt_ready"], 1)

            def inside(t, k):
                pe.wait_ge(m["q_done"], t + 1)
                pe.wait_ge(m["k_done"], t + 1)
                wait_if(pe, m["masked"], t * 2)
                for f in range(NP):
                    for odd in range(2):
                        r = slice(DF * odd, DF * odd + DF)
                        mm = pe.matmul(ap[odd][:, f, :], kf[r, k, f, :], qf[r, k, f, :], start=True, stop=True)
                        if f == NP - 1:
                            mm.then_inc(m["a_ready"], 1)

            def outputs(t, k):
                pe.wait_ge(m["masked"], t * 2 + 2)
                pe.wait_ge(m["v_done"], t + 1)
                pe.wait_ge(m["kt_done"], t + 1)
                pe.wait_ge(m["S_done"], t * 2 + 2)
                wait_if(pe, m["sq_done"], t)
                for f in range(NP):
                    pe.matmul(op[:, f * 64:(f + 1) * 64], qf[:, k, f, :], S[:, f, :], start=True, stop=True)
                    for j in range(2):
                        h = 2 * f + j
                        pe.matmul(op[:, h * DV:(h + 1) * DV], am[:, k, j * NP + f, :], v[:, k, h * DV:(h + 1) * DV],
                                  start=False, stop=True, skip_group_check=True)
                for f in range(NP):
                    mm = pe.matmul(sp_new[:, f * 64:(f + 1) * 64], kt[:, k, f, :], v[:, k, f * 64:(f + 1) * 64],
                                   start=True, stop=True)
                mm.then_inc(m["o_ready"], 1)

            def o_transposes(t, k):
                pe.wait_ge(m["on_done"], t + 1)
                wait_if(pe, m["x_done"], t)
                for c in range(DC):
                    mm = pe.transpose(oTp[:, c, :], on[:, k, c * P:(c + 1) * P], core["ident"][:, :])
                mm.then_inc(m["oT_ready"], 1)

            def project(t):
                pe.wait_ge(m["oT_done"], t + 1)
                for c in range(DC):
                    mm = pe.matmul(yp, oT[:, c, :], wo[:, c, :], start=(c == 0), stop=(c == DC - 1))
                mm.then_inc(m["y_ready"], 1)

            x_transposes(0, 0)
            qk(0, 0)
            values(0, 0)
            k_transposes(0, 0)

            def step(t, k, has_next, _):
                if has_next:
                    x_transposes(t + 1, 1 - k)
                inside(t, k)
                if has_next:
                    qk(t + 1, 1 - k)
                first = isinstance(t, int) and t == 0
                if not first:
                    o_transposes(t - 1, 1 - k)
                if has_next:
                    values(t + 1, 1 - k)
                outputs(t, k)
                if not first:
                    project(t - 1)
                if has_next:
                    k_transposes(t + 1, 1 - k)

            chunks(pe, step)
            o_transposes(T - 1, 1)
            project(T - 1)

        @block.scalar
        def _(act):
            act_std(act, ln, core["cols"][:, 0:1])
            for n, src in enumerate((qp, kp)):
                act.wait_ge(wf_ready, n + 1)
                act.activation(w_feat[n][:, :, :, 0, :], src[:, :, :].rearrange("p (c j) (h e) -> p c (j h) e", c=DC, e=32),
                               ACT.Copy).then_inc(wf_done, 1)
                act.activation(w_feat[n][:, :, :, 1, :], src[:, :, :].rearrange("p (c j) (h e) -> p c (j h) e", c=DC, e=32),
                               ACT.Copy, scale=-1.0).then_inc(wf_done, 1)
            act.wait_ge(prep, 3)

            def front(t, k):
                act.wait_ge(m["tr_done"], t + 1)
                wait_if(act, m["v_ready"], t - 1)
                act.activation(xT[:, k, :, :], trp, ACT.Copy).then_inc(m["xT_done"], 1)
                wait_if(act, m["o_ready"], t - 1)
                act.wait_ge(m["q_ready"], t + 1)
                act.activation(qf[:, k, :, :], qp[:, :, :], ACT.Exp, bias=b_col[0][:, 0:1]).then_inc(m["q_done"], 1)
                act.wait_ge(m["k_ready"], t + 1)
                act.activation(kf[:, k, :, :], kp[:, :, :], ACT.Exp, bias=b_col[1][:, 0:1]).then_inc(m["k_done"], 1)

            def k_rows(t, k):
                act.wait_ge(m["kt_ready"], t + 1)
                act.activation(kt[:, k, :, :], ktp[:, :, :], ACT.Copy).then_inc(m["kt_done"], 1)

            def o_out(t, k):
                act.wait_ge(m["o_ready"], t + 1)
                wait_if(act, m["on_done"], t - 1)
                act.activation(o[:, k, :], op[:, :], ACT.Copy, scale=SCALE).then_inc(m["o_done"], 1)
                act.activation(sq[:, k, :], op[:, :], ACT.Square, scale=SCALE).then_inc(m["sq_done"], 1)

            front(0, 0)
            k_rows(0, 0)

            def step(t, k, has_next, _):
                if has_next:
                    front(t + 1, 1 - k)
                o_out(t, k)
                if has_next:
                    k_rows(t + 1, 1 - k)

            chunks(act, step)

        @block.vector
        def _(dve):
            for n in range(2):
                dve.memset(blocks[n][:, :], 0.0).then_inc(zeroed, 1)
            dve.memset(S[:, :, :], 0.0).then_inc(m["S_done"], 1)
            dve.sem_inc(m["S_done"], 1)
            dve_stats(dve, x, T, ln)
            for k in range(2):
                dve_normalise(dve, xn[:, k, :], x, ln, k).then_inc(m["xn_ready"], 1)
            dve.wait_ge(w_in, 16 * 8)
            for n in range(2):
                dve.tensor_tensor(b_col[n][:, :], b_raw[n][:, :], core["cols"][:, 1:2], ALU.mult).then_inc(prep, 1)
            dve.tensor_scalar(wo[:, :, :], wo_raw[:, :, :], rms[:, 0:1], None, ALU.mult).then_inc(prep, 1)
            dve.wait_ge(m["S_done"], 2)

            def v_out(t, k):
                dve.wait_ge(m["v_ready"], t + 1)
                wait_if(dve, m["o_ready"], t - 1)
                dve.tensor_copy(v[:, k, :], vp).then_inc(m["v_done"], 1)

            def mask(t, k):
                wait_if(dve, m["o_ready"], t - 1)
                for half in range(2):
                    dve.wait_ge(m["a_ready"], t * 2 + half + 1)
                    dve.tensor_tensor(am[:, k, 4 * half:4 * half + 4, :], ap[half][:, :, :],
                                      keep[:, :].unsqueeze(1).broadcast_to([P, 4, P]), ALU.mult).then_inc(m["masked"], 1)

            def oT_out(t):
                dve.wait_ge(m["oT_ready"], t + 1)
                wait_if(dve, m["y_ready"], t)
                dve.tensor_copy(oT[:, :, :], oTp).then_inc(m["oT_done"], 1)

            def add_y(t):
                dve.wait_ge(m["y_ready"], t + 1)
                dve.tensor_tensor(x[:, t, :], yp, x[:, t, :], ALU.add).then_inc(m["x_done"], 1)

            def add_S(t):
                dve.wait_ge(m["o_ready"], t + 1)
                for j in range(2):
                    r, c = slice(DF * j, DF * j + DF), slice(DV * j, DV * j + DV)
                    new = sp_new.rearrange("p (f n) -> p f n", f=NP)
                    dve.tensor_tensor(S[r, :, c], new[r, :, c], S[r, :, c], ALU.add).then_inc(m["S_done"], 1)

            def norm_a(t, k):
                dve.wait_ge(m["sq_done"], t + 1)
                dve.reduce_sum(ss[:, k, :], sq[:, k, :].rearrange("p (h e) -> p h e", e=DV), AX_X).then_inc(m["ss_done"], 1)
                dve.wait_ge(m["ss_done"], t + 1)
                dve.tensor_scalar(ms[:, k, :], ss[:, k, :], 1.0 / DV, EPS, ALU.mult, ALU.add).then_inc(m["ms_done"], 1)

            def norm_b(t, k):
                dve.wait_ge(m["rs_done"], t + 1)
                dve.tensor_tensor(on[:, k, :].rearrange("p (h e) -> p h e", e=DV),
                                  o[:, k, :].rearrange("p (h e) -> p h e", e=DV),
                                  rs[:, k, :].unsqueeze(2).broadcast_to([P, H, DV]), ALU.mult).then_inc(m["on_done"], 1)

            v_out(0, 0)

            def step(t, k, has_next, has_two):
                first = isinstance(t, int) and t == 0
                mask(t, k)
                if not first:
                    oT_out(t - 1)
                if has_next:
                    v_out(t + 1, 1 - k)
                if not first:
                    add_y(t - 1)
                add_S(t)
                norm_a(t, k)
                if has_two:
                    dve_normalise(dve, xn[:, k, :], x, ln, t + 2).then_inc(m["xn_ready"], 1)
                norm_b(t, k)

            chunks(dve, step)
            oT_out(T - 1)
            add_y(T - 1)


def stage_softmax_attention(nc, core, stage, ins):
    T = core["T"]
    Tok = T * P
    H, HD = 16, 16
    qk_parts = nc.dram_tensor(f"{stage}_qk_parts", (2, 3, H * HD, Tok), BF16, kind="Internal").ap()
    m_parts = nc.dram_tensor(f"{stage}_m_parts", (3 * T, P), BF16, kind="Internal").ap()
    oT_dram = nc.dram_tensor(f"{stage}_oT", (H * HD, Tok), F32, kind="Internal").ap()
    with ExitStack() as ctx:
        s = Scope(nc, ctx, stage)
        v_ones = s.sb("v_ones", [P, T, H, HD + 1])
        softmax_project(nc, core, f"{stage}p", ins, qk_parts, v_ones, H, HD)
        softmax_heads(nc, core, f"{stage}h", ins, qk_parts, m_parts, v_ones, oT_dram, H, HD)
    softmax_output(nc, core, f"{stage}o", ins, oT_dram)


def softmax_project(nc, core, stage, ins, qk_parts, v_ones, H, HD):
    T, x = core["T"], core["x"]
    TT = 4
    G = T // TT
    N = TT * P
    with ExitStack() as ctx:
        s = Scope(nc, ctx, stage)
        ln = stats_buffers(s, T)
        w = s.sb("w", [P, DC, 3 * D])
        xn, xT = s.sb("xn", [P, 2, D]), s.sb("xT", [P, 2, DC, N])
        rest = s.sb("rest", [P, 2, N])
        parts = [s.sb(f"parts{j}", [P, 3, N], BF16) for j in range(4)]
        trp = [s.ps(f"trp{k}", [P, DC, P]) for k in range(2)]
        qp = [s.ps(f"qp{j}", [P, N]) for j in range(4)]
        vp = [s.ps(f"vp{k}", [P, H, HD]) for k in range(2)]
        w_in = s.sem("w_in")
        stored = [s.sem(f"stored{j}") for j in range(4)]
        names = ("ones_set", "xn_ready", "tr_done", "xT_done", "q_ready", "part1", "rest_done", "part2", "part3",
                 "v_ready", "v_done")
        m = {n: s.sem(n) for n in names}
        block = ctx.enter_context(nc.Block())
        columns = (0, P, 2 * D, 2 * D + P)

        def groups(eng, step):
            step(0, 0, "first")
            with eng.Fori(0, (G - 2) // 2) as i:
                step(i * 2 + 1, 1, "inside")
                step(i * 2 + 2, 0, "inside")
            step(G - 1, 1, "last")

        @block.sync
        def _(sp):
            sp.dma_start(w[:, :, :], ins["swqvk"].rearrange("p (c n) -> p c n", c=DC)).then_inc(w_in, 16)
            with sp.Fori(0, G) as g:
                for j in range(4):
                    sp.wait_ge(m["part3"], g * 4 + (j + 1))
                    dst = qk_parts[j // 2, :, (j % 2) * P:(j % 2 + 1) * P, bass.ts(g, N)]
                    sp.dma_start(dst.rearrange("a p n -> p a n"), parts[j][:, :, :]).then_inc(stored[j], 16)
            for j in range(4):
                sp.wait_ge(stored[j], 16 * G)

        @block.tensor
        def _(pe):
            pe.wait_ge(w_in, 16)

            def transposes(t, k):
                pe.wait_ge(m["xn_ready"], t + 1)
                wait_if(pe, m["xT_done"], t - 1)
                for c in range(DC):
                    mm = pe.transpose(trp[k][:, c, :], xn[:, k, c * P:(c + 1) * P], core["ident"][:, :])
                mm.then_inc(m["tr_done"], 1)

            for t in range(TT):
                transposes(t, t % 2)

            def step(g, k, position):
                pe.wait_ge(m["xT_done"], g * TT + TT)
                for j in range(4):
                    n = g * 4 + j
                    if position != "last":
                        transposes(g * TT + (TT + j), j % 2)
                    wait_if(pe, m["rest_done"], n - 3)
                    for c in range(DC):
                        mm = pe.matmul(qp[j][:, :], w[:, c, columns[j]:columns[j] + P], xT[:, k, c, :],
                                       start=(c == 0), stop=(c == DC - 1))
                    mm.then_inc(m["q_ready"], 1)
                for j in range(TT):
                    t = g * TT + j
                    wait_if(pe, m["v_done"], t - 1)
                    for c in range(DC):
                        mm = pe.matmul(vp[j % 2][:, :, :].rearrange("p h e -> p (h e)"), xT[:, k, c, j * P:(j + 1) * P],
                                       w[:, c, D:2 * D], start=(c == 0), stop=(c == DC - 1))
                    mm.then_inc(m["v_ready"], 1)

            groups(pe, step)

        @block.scalar
        def _(act):
            act_std(act, ln, core["cols"][:, 0:1])

            def xT_out(t, k, gk, j):
                act.wait_ge(m["tr_done"], t + 1)
                act.activation(xT[:, gk, :, j * P:(j + 1) * P], trp[k][:, :, :], ACT.Copy).then_inc(m["xT_done"], 1)

            def second_part(n, j):
                act.wait_ge(m["rest_done"], n + 1)
                act.activation(parts[j][:, 1, :], rest[:, j % 2, :], ACT.Copy).then_inc(m["part2"], 1)

            for t in range(TT):
                xT_out(t, t % 2, 0, t)

            def step(g, k, position):
                if position != "last":
                    wait_if(act, m["v_ready"], g * TT)
                for j in range(4):
                    n = g * 4 + j
                    if position != "last":
                        xT_out(g * TT + (TT + j), j % 2, 1 - k, j)
                    act.wait_ge(m["q_ready"], n + 1)
                    wait_if(act, stored[j], g * 16)
                    act.activation(parts[j][:, 0, :], qp[j][:, :], ACT.Copy).then_inc(m["part1"], 1)
                    if not (position == "first" and j == 0):
                        second_part(n - 1, (j + 3) % 4)

            groups(act, step)
            second_part(G * 4 - 1, 3)

        @block.vector
        def _(dve):
            dve.memset(v_ones[:, :, :, HD:HD + 1], 1.0).then_inc(m["ones_set"], 1)
            dve_stats(dve, x, T, ln)

            def normalise(t, k):
                wait_if(dve, m["tr_done"], t - 1)
                dve_normalise(dve, xn[:, k, :], x, ln, t).then_inc(m["xn_ready"], 1)

            def third_part(n, j):
                dve.wait_ge(m["part2"], n + 1)
                dve.tensor_tensor(parts[j][:, 2, :], rest[:, j % 2, :], parts[j][:, 1, :],
                                  ALU.subtract).then_inc(m["part3"], 1)

            for t in range(TT):
                normalise(t, t % 2)

            def step(g, k, position):
                for j in range(4):
                    n = g * 4 + j
                    if position != "last":
                        normalise(g * TT + (TT + j), j % 2)
                    dve.wait_ge(m["part1"], n + 1)
                    wait_if(dve, m["part3"], n - 1)
                    dve.tensor_tensor(rest[:, j % 2, :], qp[j][:, :], parts[j][:, 0, :],
                                      ALU.subtract).then_inc(m["rest_done"], 1)
                    if not (position == "first" and j == 0):
                        third_part(n - 1, (j + 3) % 4)
                for j in range(TT):
                    t = g * TT + j
                    dve.wait_ge(m["v_ready"], t + 1)
                    dve.tensor_copy(v_ones[:, t, :, 0:HD], vp[j % 2][:, :, :]).then_inc(m["v_done"], 1)

            groups(dve, step)
            third_part(G * 4 - 1, 3)


def softmax_heads(nc, core, stage, ins, qk_parts, m_parts, v_ones, oT_dram, H, HD):
    T = core["T"]
    Tok = T * P
    Q_PARTS, K_PARTS = (0, 0, 0, 1, 1, 2), (0, 1, 2, 0, 1, 0)
    R = HD * len(Q_PARTS)
    TG = 4
    G = T // TG
    N = TG * P
    HALF = N // 2
    M = 2 * (HD + 1)
    SCALE = float(D) ** -0.5

    chunks = [(t, c) for t in range(T) for c in range(t // TG + 1)]
    NA = len(chunks) + 1
    units = [(g, p) for g in range(G) for p in range(2 * g + 2)]
    NB = len(units)
    last_unit = [sum(2 * a + 2 for a in range(g + 1)) - 1 for g in range(G)]
    RING = 4
    LAG = 3
    FIRST_A, LAST_A = 3, NB - 8
    share = [[] for _ in range(NB)]
    for n in range(NA - 1):
        share[FIRST_A + n * (LAST_A - FIRST_A) // (NA - 1)].append(n)

    def unit_tiles(u):
        g, pair = units[u]
        return [(2 * pair + kk, max(0, 2 * pair + kk - TG * g) * P) for kk in range(2)]

    with ExitStack() as ctx:
        s = Scope(nc, ctx, stage)
        qs = [s.sb(f"qs{k}", [P, Tok], BF16) for k in range(2)]
        ks = [s.sb(f"ks{k}", [P, Tok], BF16) for k in range(2)]
        vh = [s.sb(f"vh{k}", [P, T, M], F32R) for k in range(2)]
        p = [s.sb(f"p{k}", [P, 2 * N]) for k in range(RING)]
        p1 = [s.sb(f"p1{k}", [P, N + HALF], F32R) for k in range(RING)]
        p2 = [s.sb(f"p2{k}", [P, N + HALF], F32R) for k in range(RING)]
        top = [s.sb(f"top{k}", [P, T, G]) for k in range(2)]
        neg, rest = s.sb("neg", [P, 2, T]), s.sb("rest", [P, 2, T])
        neg_parts = s.sb("neg_parts", [P, 3 * T], BF16)
        neg_rows = s.sb("neg_rows", [3 * T, P], BF16)
        hide_raw = s.sb("hide_raw", [P, 3, P])
        hide_kq, hide_qk, ident = s.sb("hide_kq", [P, P], BF16), s.sb("hide_qk", [P, P], BF16), s.sb("identb", [P, P], BF16)
        v_head = s.sb("v_head", [P, T, HD + 1])
        fold = s.sb("fold", [M, P])
        raw_o = [s.sb(f"raw_o{k}", [M, N]) for k in range(2)]
        rden = [s.sb(f"rden{k}", [HD, N]) for k in range(2)]
        oh = [s.sb(f"oh{k}", [HD, N]) for k in range(2)]
        ap = [s.ps(f"ap{k}", [P, N]) for k in range(2)]
        st = [s.ps(f"st{k}", [P, 2 * N]) for k in range(2)]
        op = [s.ps(f"op{k}", [P, N]) for k in range(2)]
        hide_in, const_done, m_out, m_in = (s.sem(n) for n in ("hide_in", "const_done", "m_out", "m_in"))
        qk_in = [s.sem(f"qk_in{k}") for k in range(2)]
        oh_out = [s.sem(f"oh_out{k}") for k in range(2)]
        names = ("a_ready", "a_free", "max_step", "max_parts", "s_ready", "p_ready", "p2_ready", "pv_done",
                 "vh_step", "vh_ready", "raw_done", "fold_done", "rden_done", "o_done")
        m = {n: s.sem(n) for n in names}
        block = ctx.enter_context(nc.Block())
        LOAD = 16 * 9

        def heads(eng, step):
            step(0, 0, 0, False, True)
            step(1, 1, 0, True, True)
            with eng.Fori(0, H // 2 - 2) as i:
                step(i * 2 + 2, 0, i + 1, True, True)
                step(i * 2 + 3, 1, i + 1, True, True)
            step(H - 2, 0, H // 2 - 1, True, True)
            step(H - 1, 1, H // 2 - 1, True, False)

        def behind(h, k, has_prev, u, lag):
            if u >= lag:
                return h, k, u - lag
            return (h - 1, 1 - k, NB + u - lag) if has_prev else None

        @block.sync
        def _(sp):
            for k, name in enumerate(("hide_kq", "hide_qk", "ident")):
                sp.dma_start(hide_raw[:, k, :], ins[name]).then_inc(hide_in, 16)
            sp.dma_start(fold[:, :], ins["fold"]).then_inc(hide_in, 16)

            def load(h, k):
                for n, part in enumerate(Q_PARTS):
                    sp.dma_start(qs[k][n * HD:(n + 1) * HD, :],
                                 qk_parts[0, part, bass.ts(h, HD), :]).then_inc(qk_in[k], 16)
                row = 0
                for count in (3, 2, 1):
                    src = qk_parts[1, 0:count, bass.ts(h, HD), :]
                    sp.dma_start(ks[k][row:row + count * HD, :], src).then_inc(qk_in[k], 16)
                    row += count * HD

            def maxima(h, k):
                sp.wait_ge(m["a_free"], h * NA + (NA + 2))
                sp.dma_start(m_parts, neg_rows[:, :]).then_inc(m_out, 16)
                sp.wait_ge(m_out, h * 16 + 16)
                sp.dma_start(qs[k][R:R + 3, :], m_parts.rearrange("(a t) p -> a (t p)", a=3)).then_inc(m_in, 16)

            def store(h, g):
                sp.wait_ge(m["o_done"], h * G + (g + 3))
                sp.dma_start(oT_dram[bass.ts(h, HD), g * N:(g + 1) * N], oh[g % 2][:, :]).then_inc(oh_out[g % 2], 16)

            load(0, 0)
            load(1, 1)
            maxima(0, 0)

            def step(h, k, half, has_prev, has_next):
                if has_prev:
                    store(h - 1, G - 1)
                for g in range(G - 1):
                    store(h, g)
                if has_next:
                    maxima(h + 1, 1 - k)
                    if not (isinstance(h, int) and h == H - 2):
                        sp.wait_ge(m["s_ready"], h * NB + NB)
                        load(h + 2, k)

            heads(sp, step)
            store(H - 1, G - 1)
            sp.wait_ge(m_in, 16 * H)
            for k in range(2):
                sp.wait_ge(oh_out[k], 16 * H * G // 2)

        @block.gpsimd
        def _(pool):
            def take_v(h, k, head_before=None):
                pool.tensor_copy(v_head[:, :, :], v_ones[:, :, h, :]).then_inc(m["vh_step"], 1)
                if head_before is not None:
                    pool.wait_ge(m["pv_done"], head_before * NB + (NB + RING))
                pool.wait_ge(m["vh_step"], h * 2 + 1)
                ones = v_head[:, :, HD:HD + 1].broadcast_to([P, T, HD + 1])
                pool.tensor_tensor(vh[k][:, :, 0:HD + 1], v_head[:, :, :], ones,
                                   ALU.mult).then_inc(m["vh_step"], 1)
                pool.wait_ge(m["vh_step"], h * 2 + 2)
                pool.tensor_tensor(vh[k][:, :, HD + 1:M], v_head[:, :, :], vh[k][:, :, 0:HD + 1].bitcast(F32),
                                   ALU.subtract).then_inc(m["vh_ready"], 1)

            take_v(0, 0)

            def step(h, k, half, has_prev, has_next):
                for u in range(NB):
                    b = h * NB + u
                    (_, lo0), (_, lo1) = unit_tiles(u)
                    ranges = [(0, N + HALF)] if lo1 == 0 else [(lo0, N)] + ([(N + lo1, N + HALF)] if lo1 < HALF else [])
                    pool.wait_ge(m["p_ready"], b + 3)
                    for lo, hi in ranges:
                        sub = pool.tensor_tensor(p2[u % RING][:, lo:hi], p[u % RING][:, lo:hi],
                                                 p1[u % RING][:, lo:hi].bitcast(F32), ALU.subtract)
                    sub.then_inc(m["p2_ready"], 1)
                    if u == LAG + 3 and has_next:
                        take_v(h + 1, 1 - k, h - 1 if has_prev else None)

            heads(pool, step)

        @block.tensor
        def _(pe):
            def pass_a(h, k, n):
                t, c = chunks[n]
                width = min(N, (t + 1) * P - c * N)
                bank = ap[(k + n) % 2]
                pe.wait_ge(m["a_free"], h * NA + (n + 1))
                diagonal = c == t // TG
                mm = pe.matmul(bank[:, 0:width], qs[k][0:R, t * P:(t + 1) * P], ks[k][0:R, c * N:c * N + width],
                               start=True, stop=not diagonal)
                if diagonal:
                    mm = pe.matmul(bank[:, width - P:width], ident[:, :], hide_qk[:, :], start=False, stop=True)
                mm.then_inc(m["a_ready"], 1)

            def transpose_maxima(h, k):
                pe.wait_ge(m["max_parts"], h + 1)
                pe.wait_ge(m["a_free"], h * NA + NA)
                pe.transpose(ap[(k + NA - 1) % 2][0:3 * T, 0:P // 2].bitcast(BF16), neg_parts[:, :],
                             ident[:, :]).then_inc(m["a_ready"], 1)

            def scores(h, k, u):
                g, pair = units[u]
                pe.wait_ge(m["p_ready"], h * NB + (u + 1))
                for kk, (tile, lo) in enumerate(unit_tiles(u)):
                    diagonal = tile >= TG * g
                    mm = pe.matmul(st[u % 2][:, kk * N + lo:(kk + 1) * N], ks[k][0:R + 3, tile * P:(tile + 1) * P],
                                   qs[k][0:R + 3, g * N + lo:(g + 1) * N], start=True, stop=not diagonal)
                    if diagonal:
                        mm = pe.matmul(st[u % 2][:, kk * N + lo:kk * N + lo + P], ident[:, :], hide_kq[:, :],
                                       start=False, stop=True)
                mm.then_inc(m["s_ready"], 1)

            def values(h, k, u):
                g, pair = units[u]
                if u == 0:
                    pe.wait_ge(m["vh_ready"], h + 1)
                pe.wait_ge(m["p2_ready"], h * NB + (u + 1))
                if pair == 0:
                    pe.wait_ge(m["o_done"], h * G + (g + 1))
                (tile0, lo0), (tile1, lo1) = unit_tiles(u)
                r = u % RING
                steps = [(p1, tile0, lo0, N, 0), (p2, tile0, lo0, N, 0)]
                if lo1 < HALF:
                    steps += [(p1, tile1, lo1, HALF, N), (p2, tile1, lo1, HALF, N)]
                steps.append((p, tile1, max(lo1, HALF), N, N))
                for n, (src, tile, lo, hi, base) in enumerate(steps):
                    w = vh[k][:, tile, :] if src is not p else vh[k][:, tile, :].bitcast(F32)
                    mm = pe.matmul(op[g % 2][0:M, lo:hi], w, src[r][:, base + lo:base + hi],
                                   start=(pair == 0 and n == 0), stop=(tile >= TG * g), skip_group_check=True)
                mm.then_inc(m["pv_done"], 1)

            def fold_output(h, g):
                pe.wait_ge(m["raw_done"], h * G + (g + 1))
                pe.matmul(op[g % 2][:, :], fold[:, :], raw_o[g % 2][:, :], start=True,
                          stop=True).then_inc(m["fold_done"], 1)

            pe.wait_ge(const_done, 7)
            pe.wait_ge(hide_in, 64)
            pe.wait_ge(qk_in[0], LOAD)
            for n in range(NA - 1):
                pass_a(0, 0, n)
            transpose_maxima(0, 0)

            def step(h, k, half, has_prev, has_next):
                pe.wait_ge(m_in, h * 16 + 16)
                for u in range(NB):
                    scores(h, k, u)
                    if has_next:
                        if u == FIRST_A:
                            pe.wait_ge(qk_in[1 - k], (half + 1 + k) * LOAD)
                        for n in share[u]:
                            pass_a(h + 1, 1 - k, n)
                        if u == LAST_A + 2:
                            transpose_maxima(h + 1, 1 - k)
                    if (at := behind(h, k, has_prev, u, LAG)) is not None:
                        values(*at)
                    if (at := behind(h, k, has_prev, u, LAG + 1)) is not None and at[2] in last_unit:
                        fold_output(at[0], last_unit.index(at[2]))

            heads(pe, step)
            for u in range(NB - LAG, NB):
                values(H - 1, 1, u)
            fold_output(H - 1, G - 1)

        @block.scalar
        def _(act):
            act.wait_ge(hide_in, 64)
            for k, dst in enumerate((hide_kq, hide_qk, ident)):
                act.activation(dst[:, :], hide_raw[:, k, :], ACT.Copy).then_inc(const_done, 1)
            act.sem_inc(m["p_ready"], 2)
            act.sem_inc(m["pv_done"], RING)

            def step(h, k, half, has_prev, has_next):
                for u in range(NB):
                    b = h * NB + u
                    (_, lo0), (_, lo1) = unit_tiles(u)
                    if lo1 == 0:
                        whole, split = [(0, 2 * N)], [(0, N + HALF)]
                    else:
                        whole = [(lo0, N), (N + lo1, 2 * N)]
                        split = [(lo0, N)] + ([(N + lo1, N + HALF)] if lo1 < HALF else [])
                    act.wait_ge(m["s_ready"], b + 1)
                    act.wait_ge(m["pv_done"], b + 1)
                    for dst, ranges in ((p, whole), (p1, split)):
                        for lo, hi in ranges:
                            ex = act.activation(dst[u % RING][:, lo:hi], st[u % 2][:, lo:hi], ACT.Exp, scale=SCALE)
                    ex.then_inc(m["p_ready"], 1)

            heads(act, step)

        @block.vector
        def _(dve):
            for k in range(2):
                dve.memset(ks[k][R:R + 3, :], 1.0).then_inc(const_done, 1)
                dve.memset(top[k][:, :, :], -3.0e38).then_inc(const_done, 1)
            dve.sem_inc(m["a_free"], 2)
            dve.sem_inc(m["o_done"], 2)
            dve.wait_ge(const_done, 7)

            def reduce(h, k, n):
                t, c = chunks[n]
                width = min(N, (t + 1) * P - c * N)
                dve.wait_ge(m["a_ready"], h * NA + (n + 1))
                dve.reduce_max(top[k][:, t, c:c + 1], ap[(k + n) % 2][:, 0:width], AX_X).then_inc(m["a_free"], 1)

            def split_maxima(h, k):
                step = m["max_step"]
                dve.wait_ge(m["a_free"], h * NA + (NA + 1))
                dve.tensor_reduce(neg[:, 0, :], top[k][:, :, :], AX_X, ALU.max).then_inc(step, 1)
                dve.wait_ge(step, h * 6 + 1)
                dve.tensor_scalar(neg[:, 1, :], neg[:, 0, :], -1.0, None, ALU.mult).then_inc(step, 1)
                src = neg[:, 1, :]
                for k3 in range(2):
                    part = neg_parts[:, k3 * T:(k3 + 1) * T]
                    dve.wait_ge(step, h * 6 + (2 + 2 * k3))
                    dve.tensor_copy(part, src).then_inc(step, 1)
                    dve.wait_ge(step, h * 6 + (3 + 2 * k3))
                    dve.tensor_tensor(rest[:, k3, :], src, part, ALU.subtract).then_inc(step, 1)
                    src = rest[:, k3, :]
                dve.wait_ge(step, h * 6 + 6)
                dve.tensor_copy(neg_parts[:, 2 * T:3 * T], src).then_inc(m["max_parts"], 1)

            def maxima_out(h, k):
                dve.wait_ge(m["a_ready"], h * NA + NA)
                wait_if(dve, m_out, h * 16)
                dve.tensor_copy(neg_rows[:, :], ap[(k + NA - 1) % 2][0:3 * T, 0:P // 2].bitcast(BF16)
                                ).then_inc(m["a_free"], 1)

            def raw_output(h, g):
                dve.wait_ge(m["pv_done"], h * NB + (last_unit[g] + 1 + RING))
                dve.tensor_copy(raw_o[g % 2][:, :], op[g % 2][0:M, :]).then_inc(m["raw_done"], 1)

            def output(h, half, g):
                n = h * G + g
                dve.wait_ge(m["fold_done"], n + 1)
                dve.reciprocal(rden[g % 2][:, :], op[g % 2][32:32 + HD, :]).then_inc(m["rden_done"], 1)
                dve.wait_ge(m["rden_done"], n + 1)
                wait_if(dve, oh_out[g % 2], h * (16 * G // 2) + 16 * (g // 2))
                dve.tensor_tensor(oh[g % 2][:, :], op[g % 2][0:HD, :], rden[g % 2][:, :],
                                  ALU.mult).then_inc(m["o_done"], 1)

            for n in range(NA - 1):
                reduce(0, 0, n)
            split_maxima(0, 0)
            maxima_out(0, 0)

            def step(h, k, half, has_prev, has_next):
                for u in range(NB):
                    if has_next:
                        for n in share[u]:
                            reduce(h + 1, 1 - k, n)
                        if share[u] and share[u][-1] == NA - 2:
                            split_maxima(h + 1, 1 - k)
                        if u == LAST_A + 2:
                            maxima_out(h + 1, 1 - k)
                    if (at := behind(h, k, has_prev, u, LAG)) is not None and at[2] in last_unit:
                        raw_output(at[0], last_unit.index(at[2]))
                    if (at := behind(h, k, has_prev, u, LAG + 1)) is not None and at[2] in last_unit:
                        output(at[0], half, last_unit.index(at[2]))

            heads(dve, step)
            raw_output(H - 1, G - 1)
            output(H - 1, H // 2 - 1, G - 1)


def softmax_output(nc, core, stage, ins, oT_dram):
    T, x = core["T"], core["x"]
    TG = 4
    G = T // TG
    N = TG * P
    with ExitStack() as ctx:
        s = Scope(nc, ctx, stage)
        wo = s.sb("wo", [P, DC, D])
        oT = [s.sb(f"oT{k}", [P, DC, N]) for k in range(2)]
        yp = [s.ps(f"yp{k}", [P, D]) for k in range(4)]
        w_in = s.sem("w_in")
        oT_in = [s.sem(f"oT_in{k}") for k in range(2)]
        y_ready, x_done = s.sem("y_ready"), s.sem("x_done")
        block = ctx.enter_context(nc.Block())

        @block.sync
        def _(sp):
            sp.dma_start(wo[:, :, :], ins["swo"].rearrange("p (c n) -> p c n", c=DC)).then_inc(w_in, 16)
            view = oT_dram.rearrange("(c p) n -> p c n", p=P)

            def load(g, k):
                sp.dma_start(oT[k][:, :, :], view[:, :, bass.ts(g, N)]).then_inc(oT_in[k], 16)

            load(0, 0)
            load(1, 1)
            with sp.Fori(0, G // 2 - 1) as i:
                for k in range(2):
                    sp.wait_ge(y_ready, (i * 2 + (k + 1)) * TG)
                    load(i * 2 + (2 + k), k)

        @block.tensor
        def _(pe):
            pe.wait_ge(w_in, 16)
            with pe.Fori(0, G // 2) as i:
                for k in range(2):
                    pe.wait_ge(oT_in[k], i * 16 + 16)
                    for t in range(TG):
                        pe.wait_ge(x_done, (i * 2 + k) * TG + (t + 1))
                        for c in range(DC):
                            mm = pe.matmul(yp[t][:, :], oT[k][:, c, t * P:(t + 1) * P], wo[:, c, :],
                                           start=(c == 0), stop=(c == DC - 1))
                        mm.then_inc(y_ready, 1)

        @block.vector
        def _(dve):
            dve.sem_inc(x_done, TG)
            with dve.Fori(0, G) as g:
                for t in range(TG):
                    dve.wait_ge(y_ready, g * TG + (t + 1))
                    dve.tensor_tensor(x[:, g * TG + t, :], yp[t][:, :], x[:, g * TG + t, :], ALU.add).then_inc(x_done, 1)


STAGES = ['moe', 'lin', 'moe', 'spike', 'soft', 'spike']


def build(nc, ins, out_dram):
    Tok = ins["x"].shape[0]
    T = Tok // P
    with ExitStack() as ctx:
        s = Scope(nc, ctx, "core")
        NE = ins["up"].shape[0]
        core = dict(T=T, x=s.sb("x", [P, T, D]), ident=s.sb("ident", [P, P]), cols=s.sb("cols", [P, 4]),
                    iota8=s.sb("iota8", [P, 8]), comb=s.sb("comb", [P, T, NE]))
        stage_load(nc, core, ins["x"], ins)
        for n, kind in enumerate(STAGES):
            if kind in ("moe", "spike"):
                with ExitStack() as parts:
                    sp = Scope(nc, parts, f"{kind}{n}")
                    x1 = sp.sb("xT1", [P, DC, Tok], F32R)
                    x2 = sp.sb("xT2", [P, DC, Tok], F32R)
                    router = dict(E=NE - 1, w=ins["rw"], b=ins["rb"]) if kind == "moe" else None
                    stage_norm(nc, core, f"norm{n}", x1, x2, router)
                    if kind == "moe":
                        stage_experts(nc, core, f"experts{n}", x1, x2, ins["up"], ins["dn"], NE)
                    else:
                        stage_spikes(nc, core, f"spikes{n}", x1, x2, ins["fc"], ins["proj"])
            if kind == "lin":
                stage_linear_attention(nc, core, f"lin{n}", ins)
            if kind == "soft":
                stage_softmax_attention(nc, core, f"soft{n}", ins)
        stage_store(nc, core, out_dram)


def kernel(**inputs):
    import numpy as np
    import concourse.bacc as _bacc
    from concourse.bass_utils import run_bass_kernel_spmd as _run

    a = {k: np.asarray(v) for k, v in inputs.items()}

    def by_rows(w):
        r, n = w.shape
        return np.ascontiguousarray(w.reshape(r // P, P, n).transpose(1, 0, 2).reshape(P, -1))

    x = a["L0_attn_x"]
    up = np.concatenate([a["L0_ffn_w_up"], a["L0_ffn_shared_w_up"]])
    dn = np.concatenate([a["L0_ffn_w_down"], a["L0_ffn_shared_w_down"]])
    H0, H1 = 8, 16
    cols = np.zeros((P, 4), np.float32)
    cols[:, 0] = EPS
    sign = np.where((np.arange(P) // 32) % 2 == 0, 1.0, -1.0)
    cols[:, 1] = sign
    cols[:, 2] = 1.0
    cols[:, 3] = -0.5
    k_after_q = np.arange(P)[:, None] > np.arange(P)[None, :]
    fold = np.zeros((34, P), np.float32)
    for part in range(2):
        fold[17 * part + np.arange(16), np.arange(16)] = 1.0
        fold[17 * part + 16, 32:48] = 1.0
    arrays = {
        "fold": fold,
        "x": x.reshape(-1, D),
        "up": np.stack([by_rows(w.T) for w in up]),
        "dn": np.stack([by_rows(w.T) for w in dn]),
        "rw": by_rows(a["L0_ffn_router_w"].T).reshape(P, DC, -1),
        "rb": np.broadcast_to(a["L0_ffn_router_b"], (P, a["L0_ffn_router_b"].shape[0])),
        "ident": np.eye(P, dtype=np.float32),
        "cols": cols,
        "iota8": np.broadcast_to(np.arange(8, dtype=np.float32), (P, 8)),
        "keep_kq": (~k_after_q).astype(np.float32),
        "hide_kq": np.where(k_after_q, -1e30, 0.0).astype(np.float32),
        "hide_qk": np.where(k_after_q.T, -1e30, 0.0).astype(np.float32),
        "fc": by_rows(a["L1_ffn_W_fc"].T),
        "proj": by_rows(a["L1_ffn_W_proj"].T),
        "lwq": by_rows(a["L0_attn_Wq"]),
        "lwk": by_rows(a["L0_attn_Wk"]),
        "lwv": by_rows(a["L0_attn_Wv"].T),
        "lwo": by_rows(a["L0_attn_Wo"].T),
        "lfq": np.ascontiguousarray(a["L0_attn_fmq_w"].T),
        "lfk": np.ascontiguousarray(a["L0_attn_fmk_w"].T),
        "lbq": np.tile(a["L0_attn_fmq_b"], 4)[:, None],
        "lbk": np.tile(a["L0_attn_fmk_b"], 4)[:, None],
        "lrms": np.tile(a["L0_attn_rms_w"], 4)[:, None],
        "swqvk": by_rows(a["L1_attn_Wqvk"]),
        "swo": by_rows(a["L1_attn_Wo"]),
    }
    nc = _bacc.Bacc("TRN2", target_bir_lowering=False, num_devices=1)
    ins = {}
    used = {f"in_{k}": np.ascontiguousarray(v) for k, v in arrays.items()}
    for name, v in arrays.items():
        ins[name] = nc.dram_tensor(f"in_{name}", v.shape, mybir.dt.from_np(v.dtype), kind="ExternalInput").ap()
    out = nc.dram_tensor("out_0", (x.shape[0] * x.shape[1], D), F32, kind="ExternalOutput").ap()
    build(nc, ins, out)
    r = _run(nc, [used], core_ids=[0])
    return r.results[0]["out_0"].reshape(x.shape)
```

```python
from contextlib import ExitStack

import concourse.bass as bass
from concourse import mybir

P = 128
D = 256
DC = D // P
EPS = 1e-5
F32 = mybir.dt.float32
F32R = mybir.dt.float32r
BF16 = mybir.dt.bfloat16
U32 = mybir.dt.uint32
ALU = mybir.AluOpType
ACT = mybir.ActivationFunctionType
AX_X = mybir.AxisListType.X


class Scope:

    def __init__(self, nc, ctx, stage):
        self.nc, self.ctx, self.stage = nc, ctx, stage
        self.sems = []
        ctx.callback(self.release)

    def release(self):
        if self.sems:
            self.nc.clear_and_free_semaphores(self.sems)
            self.nc.all_engine_barrier()

    def sb(self, name, shape, dt=F32):
        return self.ctx.enter_context(self.nc.sbuf_tensor(f"{self.stage}_{name}", shape, dt))

    def ps(self, name, shape, dt=F32):
        return self.ctx.enter_context(self.nc.psum_tensor(f"{self.stage}_{name}", shape, dt))

    def sem(self, name):
        self.sems.append(self.nc.alloc_semaphore(name=f"{self.stage}_{name}"))
        return self.sems[-1]


def stats_buffers(s, T):
    return dict(
        raw=s.sb("ln_raw", [P, T, 6]), tmp=s.sb("ln_tmp", [P, 4, T]), mean=s.sb("ln_mean", [P, T]),
        var=s.sb("ln_var", [P, T]), std=s.sb("ln_std", [P, T]), rstd=s.sb("ln_rstd", [P, T]),
        raw_done=s.sem("ln_raw_done"), step=s.sem("ln_step"), var_done=s.sem("ln_var_done"),
        std_done=s.sem("ln_std_done"), rstd_done=s.sem("ln_rstd_done"))


def dve_stats(dve, x, T, ln):
    unroll = 8
    with dve.Fori(0, T // unroll) as i:
        for k in range(unroll):
            dve.bn_stats(ln["raw"][:, i * unroll + k, :], x[:, i * unroll + k, :]).then_inc(ln["raw_done"], 1)
    raw, tmp, step = ln["raw"], ln["tmp"], ln["step"]
    mean_sum, mean_diff, dev_sum, diff_sq = (tmp[:, k, :] for k in range(4))
    dve.wait_ge(ln["raw_done"], T)
    dve.tensor_tensor(mean_sum, raw[:, :, 1], raw[:, :, 4], ALU.add).then_inc(step, 1)
    dve.tensor_tensor(mean_diff, raw[:, :, 1], raw[:, :, 4], ALU.subtract).then_inc(step, 1)
    dve.tensor_tensor(dev_sum, raw[:, :, 2], raw[:, :, 5], ALU.add).then_inc(step, 1)
    dve.wait_ge(step, 3)
    dve.tensor_scalar(ln["mean"][:, :], mean_sum, 0.5, None, ALU.mult).then_inc(step, 1)
    dve.scalar_tensor_tensor(out=diff_sq, in0=mean_diff, scalar=0.25, in1=mean_diff,
                             op0=ALU.mult, op1=ALU.mult).then_inc(step, 1)
    dve.wait_ge(step, 5)
    dve.scalar_tensor_tensor(out=ln["var"][:, :], in0=dev_sum, scalar=1.0 / D, in1=diff_sq,
                             op0=ALU.mult, op1=ALU.add).then_inc(ln["var_done"], 1)
    dve.wait_ge(ln["std_done"], 1)
    dve.reciprocal(ln["rstd"][:, :], ln["std"][:, :]).then_inc(ln["rstd_done"], 1)
    dve.wait_ge(ln["rstd_done"], 1)


def act_std(act, ln, eps_col):
    act.wait_ge(ln["var_done"], 1)
    act.activation(ln["std"][:, :], ln["var"][:, :], ACT.Sqrt, bias=eps_col).then_inc(ln["std_done"], 1)


def dve_normalise(dve, out, x, ln, t):
    return dve.tensor_scalar(out, x[:, t, :], ln["mean"][:, bass.ds(t, 1)], ln["rstd"][:, bass.ds(t, 1)],
                             ALU.subtract, ALU.mult)


def stage_load(nc, core, x_dram, const_dram):
    with ExitStack() as ctx:
        s = Scope(nc, ctx, "load")
        arrived = s.sem("arrived")
        block = ctx.enter_context(nc.Block())

        @block.sync
        def _(sp):
            xv = x_dram.rearrange("(t p) d -> p t d", p=P)
            T = core["T"]
            for q in range(4):
                sp.dma_start(core["x"][:, q * T // 4:(q + 1) * T // 4, :],
                             xv[:, q * T // 4:(q + 1) * T // 4, :]).then_inc(arrived, 16)
            for name in ("ident", "cols", "iota8"):
                sp.dma_start(core[name][:, :], const_dram[name]).then_inc(arrived, 16)
            sp.wait_ge(arrived, 16 * 7)


def stage_store(nc, core, out_dram):
    with ExitStack() as ctx:
        s = Scope(nc, ctx, "store")
        stored = s.sem("stored")
        block = ctx.enter_context(nc.Block())

        @block.sync
        def _(sp):
            ov = out_dram.rearrange("(t p) d -> p t d", p=P)
            T = core["T"]
            for q in range(4):
                sp.dma_start(ov[:, q * T // 4:(q + 1) * T // 4, :],
                             core["x"][:, q * T // 4:(q + 1) * T // 4, :]).then_inc(stored, 16)
            sp.wait_ge(stored, 16 * 4)


def stage_norm(nc, core, stage, x1, x2, router, weights):
    T, x = core["T"], core["x"]
    RING = 4
    with ExitStack() as ctx:
        s = Scope(nc, ctx, stage)
        ln = stats_buffers(s, T)
        xn = s.sb("xn", [P, RING, D])
        tr = [s.ps(f"tr{k}", [P, DC, P]) for k in range(RING)]
        xn_ready, tr_done = s.sem("xn_ready"), s.sem("tr_done")
        x1_done, x2_done = s.sem("x1_done"), s.sem("x2_done")
        if router:
            E = router["E"]
            rw = s.sb("rw", [P, DC, E])
            rb = s.sb("rb", [P, E])
            xs = s.sb("xs", [P, RING, DC, P])
            lg = s.sb("lg", [P, T, E])
            top = s.sb("top", [P, T, 8])
            top_at = s.sb("top_at", [P, T, 8], U32)
            at_f = s.sb("at_f", [P, T, 2])
            gap = s.sb("gap", [P, T])
            ex = s.sb("ex", [P, T])
            den = s.sb("den", [P, T])
            wt = s.sb("wt", [P, 3, T])
            pick = s.sb("pick", [P, 2, T, E])
            lgp = [s.ps(f"lgp{k}", [P, E]) for k in range(RING)]
            rw_in, xs_done, router_done = s.sem("rw_in"), s.sem("xs_done"), s.sem("router_done")
            lg_done, top_done, at_done = s.sem("lg_done"), s.sem("top_done"), s.sem("at_done")
            gap_done, ex_done, wstep = s.sem("gap_done"), s.sem("ex_done"), s.sem("wstep")
        weights_in = s.sem("weights_in")
        block = ctx.enter_context(nc.Block())

        @block.sync
        def _(sp):
            if router:
                sp.dma_start(rw[:, :, :], router["w"]).then_inc(rw_in, 16)
                sp.dma_start(rb[:, :], router["b"]).then_inc(rw_in, 16)
            for dst, src in weights:
                sp.dma_start(dst[:, :], src).then_inc(weights_in, 16)
            if router:
                sp.wait_ge(rw_in, 32)
            sp.wait_ge(weights_in, 16 * len(weights))

        def tiles(eng, step):
            with eng.Fori(0, T // RING - 1) as i:
                for k in range(RING):
                    step(i * RING + k, k, True)
            for k in range(RING):
                step(T - RING + k, k, False)

        @block.vector
        def _(dve):
            dve_stats(dve, x, T, ln)
            for k in range(RING):
                dve_normalise(dve, xn[:, k, :], x, ln, k).then_inc(xn_ready, 1)

            def step(t, k, has_next):
                dve.wait_ge(x1_done, t + 1)
                if router:
                    dve.wait_ge(xs_done, t + 1)
                dve.tensor_tensor(x2[:, :, bass.ts(t, P)], tr[k][:, :, :],
                                  x1[:, :, bass.ts(t, P)].bitcast(F32), ALU.subtract).then_inc(x2_done, 1)
                if has_next:
                    dve_normalise(dve, xn[:, k, :], x, ln, t + RING).then_inc(xn_ready, 1)
                if router and k == RING - 1:
                    for j in range(RING):
                        at = t - (RING - 1 - j)
                        dve.wait_ge(router_done, at + (1 + RING))
                        dve.tensor_tensor(lg[:, at, :], lgp[j][:, :], rb[:, :], ALU.add).then_inc(lg_done, 1)

            if router:
                dve.sem_inc(lg_done, RING)
                dve.wait_ge(rw_in, 32)
            tiles(dve, step)
            if not router:
                return
            dve.wait_ge(lg_done, T + RING)
            for t in range(T):
                dve.max(top[:, t, :], lg[:, t, :]).then_inc(top_done, 1)
            dve.wait_ge(top_done, T)
            for t in range(T):
                dve.max_index(top_at[:, t, :], top[:, t, :], lg[:, t, :]).then_inc(at_done, 1)
            dve.tensor_tensor(gap[:, :], top[:, :, 1], top[:, :, 0], ALU.subtract).then_inc(gap_done, 1)
            dve.wait_ge(at_done, T)
            dve.tensor_copy(at_f[:, :, :], top_at[:, :, 0:2]).then_inc(wstep, 1)
            dve.wait_ge(ex_done, 1)
            dve.tensor_scalar(den[:, :], ex[:, :], 1.0, None, ALU.add).then_inc(wstep, 1)
            dve.wait_ge(wstep, 2)
            dve.reciprocal(wt[:, 2, :], den[:, :]).then_inc(wstep, 1)
            dve.wait_ge(wstep, 3)
            dve.tensor_scalar(wt[:, 0, :], wt[:, 2, :], 0.5, None, ALU.mult).then_inc(wstep, 1)
            dve.wait_ge(wstep, 4)
            dve.tensor_tensor(wt[:, 1, :], ex[:, :], wt[:, 0, :], ALU.mult).then_inc(wstep, 1)
            for k in range(2):
                dve.tensor_tensor(pick[:, k, :, :], core["iota8"][:, :].unsqueeze(1).broadcast_to([P, T, E]),
                                  at_f[:, :, k:k + 1].broadcast_to([P, T, E]), ALU.is_equal).then_inc(wstep, 1)
            dve.wait_ge(wstep, 7)
            for k in range(2):
                dve.tensor_tensor(pick[:, k, :, :], pick[:, k, :, :],
                                  wt[:, k, :].unsqueeze(2).broadcast_to([P, T, E]), ALU.mult).then_inc(wstep, 1)
            dve.wait_ge(wstep, 9)
            dve.tensor_tensor(core["comb"][:, :, 0:E], pick[:, 0, :, :], pick[:, 1, :, :],
                              ALU.add).then_inc(wstep, 1)
            dve.memset(core["comb"][:, :, E:E + 1], 0.5).then_inc(wstep, 1)

        @block.scalar
        def _(act):
            act_std(act, ln, core["cols"][:, 0:1])

            def step(t, k, has_next):
                act.wait_ge(tr_done, t + 1)
                act.activation(x1[:, :, bass.ts(t, P)], tr[k][:, :, :], ACT.Copy).then_inc(x1_done, 1)
                if router:
                    act.wait_ge(router_done, t + 1)
                    act.activation(xs[:, k, :, :], tr[k][:, :, :], ACT.Copy).then_inc(xs_done, 1)

            tiles(act, step)
            if router:
                act.wait_ge(gap_done, 1)
                act.activation(ex[:, :], gap[:, :], ACT.Exp).then_inc(ex_done, 1)

        @block.tensor
        def _(pe):
            def transposes(t, k):
                pe.wait_ge(xn_ready, t + 1)
                for c in range(DC):
                    mm = pe.transpose(tr[k][:, c, :], xn[:, k, c * P:(c + 1) * P], core["ident"][:, :])
                mm.then_inc(tr_done, 1)

            def logits(t, k):
                pe.wait_ge(xs_done, t + 1)
                pe.wait_ge(lg_done, t + 1)
                for c in range(DC):
                    mm = pe.matmul(lgp[k][:, :], xs[:, k, c, :], rw[:, c, :], start=(c == 0), stop=(c == DC - 1))
                mm.then_inc(router_done, 1)

            if router:
                pe.sem_inc(router_done, RING)
                pe.wait_ge(rw_in, 32)
            for k in range(RING):
                transposes(k, k)

            def step(t, k, has_next):
                if router:
                    logits(t, k)
                if has_next:
                    pe.wait_ge(x2_done, t + 1)
                    transposes(t + RING, k)

            tiles(pe, step)


def stage_experts(nc, core, stage, x1, x2, raw_up, raw_dn, up_dram, dn_dram, NE):
    T, x, comb = core["T"], core["x"], core["comb"]
    F = up_dram.shape[2] // DC
    FT = F // P
    TT = 4
    G = T // TT
    N = TT * P
    with ExitStack() as ctx:
        s = Scope(nc, ctx, stage)
        up1, up2 = s.sb("up1", [P, DC * F], F32R), s.sb("up2", [P, DC * F], F32R)
        dn1, dn2 = s.sb("dn1", [P, FT * D], F32R), s.sb("dn2", [P, FT * D], F32R)
        h = s.sb("h", [P, FT, N])
        h1, h2 = s.sb("h1", [P, FT, N], F32R), s.sb("h2", [P, FT, N], F32R)
        hp = [s.ps(f"hp{f}", [P, N]) for f in range(FT)]
        yp = [s.ps(f"yp{t}", [P, D]) for t in range(TT)]
        up_in, dn_in = s.sem("up_in"), s.sem("dn_in")
        up1_done, up_split, dn1_done, dn_split = (s.sem(n) for n in ("up1_done", "up_split", "dn1_done", "dn_split"))
        ups_done, hp_ready, act_done, h_split = (s.sem(n) for n in ("ups_done", "hp_ready", "act_done", "h_split"))
        h_used, yp_ready, y_added = s.sem("h_used"), s.sem("yp_ready"), s.sem("y_added")
        block = ctx.enter_context(nc.Block())
        up_parts = ((up1, x1), (up1, x2), (up2, x1))

        @block.sync
        def _(sp):
            with sp.Fori(0, NE - 1) as e:
                sp.wait_ge(up_split, e + 2)
                sp.dma_start(raw_up[:, :], up_dram[e + 1, :, :]).then_inc(up_in, 16)
                sp.wait_ge(dn_split, e + 2)
                sp.dma_start(raw_dn[:, :], dn_dram[e + 1, :, :]).then_inc(dn_in, 16)

        @block.tensor
        def _(pe):
            with pe.Fori(0, NE) as e:
                with pe.Fori(0, G) as g:
                    n = e * G + g
                    pe.wait_ge(up_split, e + 2)
                    for f in range(FT):
                        pe.wait_ge(act_done, n * FT + f + 1)
                        k = 0
                        for w, v in up_parts:
                            for c in range(DC):
                                mm = pe.matmul(hp[f][:, :], w[:, c * F + f * P:c * F + (f + 1) * P],
                                               v[:, c, bass.ts(g, N)], start=(k == 0), stop=(k == 5))
                                k += 1
                        mm.then_inc(hp_ready, 1)
                    pe.sem_inc(ups_done, 1)
                    pe.wait_ge(dn_split, e + 2)
                    for f in range(FT):
                        pe.wait_ge(h_split, n * FT + f + 1 + FT)
                        for t in range(TT):
                            if f == 0:
                                pe.wait_ge(y_added, n * TT + t + 1 + T - TT)
                            for k, (a, b) in enumerate(((h1, dn1), (h1, dn2), (h2, dn1))):
                                mm = pe.matmul(yp[t][:, :], a[:, f, t * P:(t + 1) * P], b[:, f * D:(f + 1) * D],
                                               start=(f == 0 and k == 0), stop=(f == FT - 1 and k == 2))
                            if f == FT - 1:
                                mm.then_inc(yp_ready, 1)
                        if f < FT - 1:
                            mm.then_inc(h_used, 1)
                        else:
                            pe.sem_inc(h_used, 1)

        @block.scalar
        def _(act):
            act.sem_inc(act_done, FT)
            with act.Fori(0, NE) as e:
                with act.Fori(0, G) as g:
                    n = e * G + g
                    for f in range(FT):
                        act.wait_ge(hp_ready, n * FT + f + 1)
                        act.wait_ge(h_split, n * FT + f + 1)
                        act.activation(h[:, f, :], hp[f][:, :], ACT.Silu)
                        act.wait_ge(h_used, n * FT + f + 1)
                        act.activation(h1[:, f, :], hp[f][:, :], ACT.Silu).then_inc(act_done, 1)

        @block.vector
        def _(dve):
            dve.sem_inc(up_split, 1)
            dve.sem_inc(dn_split, 1)
            dve.sem_inc(h_split, FT)
            dve.sem_inc(h_used, FT)
            dve.sem_inc(y_added, T)

            def split_up(e):
                if not isinstance(e, int):
                    dve.wait_ge(up_in, e * 16)
                dve.tensor_copy(up1[:, :], raw_up[:, :]).then_inc(up1_done, 1)
                dve.wait_ge(up1_done, e + 1)
                dve.tensor_tensor(up2[:, :], raw_up[:, :], up1[:, :].bitcast(F32), ALU.subtract).then_inc(up_split, 1)

            def split_dn(e):
                if not isinstance(e, int):
                    dve.wait_ge(dn_in, e * 16)
                dve.tensor_copy(dn1[:, :], raw_dn[:, :]).then_inc(dn1_done, 1)
                dve.wait_ge(dn1_done, e + 1)
                dve.tensor_tensor(dn2[:, :], raw_dn[:, :], dn1[:, :].bitcast(F32), ALU.subtract).then_inc(dn_split, 1)

            def group(e, g, last_of_expert):
                n = e * G + g
                for f in range(FT):
                    dve.wait_ge(act_done, n * FT + f + 1 + FT)
                    dve.wait_ge(h_used, n * FT + f + 1)
                    dve.tensor_tensor(h2[:, f, :], h[:, f, :], h1[:, f, :].bitcast(F32),
                                      ALU.subtract).then_inc(h_split, 1)
                if last_of_expert:
                    dve.wait_ge(ups_done, n + 1)
                    split_up(e + 1)
                for t in range(TT):
                    dve.wait_ge(yp_ready, n * TT + t + 1)
                    dve.wait_ge(y_added, n * TT + t + 1)
                    tile = g * TT + t
                    dve.scalar_tensor_tensor(out=x[:, tile, :], in0=yp[t][:, :],
                                             scalar=comb[:, tile, bass.ds(e, 1)], in1=x[:, tile, :],
                                             op0=ALU.mult, op1=ALU.add).then_inc(y_added, 1)
                if last_of_expert:
                    dve.wait_ge(h_used, n * FT + FT + FT)
                    split_dn(e + 1)

            split_up(0)
            split_dn(0)
            with dve.Fori(0, NE - 1) as e:
                with dve.Fori(0, G - 1) as g:
                    group(e, g, False)
                group(e, G - 1, True)
            with dve.Fori(0, G) as g:
                group(NE - 1, g, False)


def stage_spikes(nc, core, stage, x1, x2, raw_fc, raw_pj):
    T, x = core["T"], core["x"]
    STEPS, BETA, THRESHOLD = 5, 0.9, 1.0
    F = raw_fc.shape[1] // DC
    FT = F // P
    HT = 4
    TT = 4
    G = T // TT
    N = TT * P
    with ExitStack() as ctx:
        s = Scope(nc, ctx, stage)
        fc1, fc2 = s.sb("fc1", [P, DC * F], F32R), s.sb("fc2", [P, DC * F], F32R)
        pj1, pj2 = s.sb("pj1", [P, FT * D], F32R), s.sb("pj2", [P, FT * D], F32R)
        r = s.sb("r", [P, 2, N])
        h = s.sb("h", [P, HT, N])
        h1, h2 = s.sb("h1", [P, HT, N], F32R), s.sb("h2", [P, HT, N], F32R)
        y, mem, leak, spk = s.sb("y", [P, TT, D]), s.sb("mem", [P, TT, D]), s.sb("leak", [P, TT, D]), s.sb("spk", [P, TT, D])
        hp = [s.ps(f"hp{f}", [P, N]) for f in range(HT)]
        yp = s.ps("yp", [P, TT, N])
        fc1_done, fc_split, pj1_done, pj_split = (s.sem(n) for n in ("fc1_done", "fc_split", "pj1_done", "pj_split"))
        hp_ready, relu_done, act_done, h_split = (s.sem(n) for n in ("hp_ready", "relu_done", "act_done", "h_split"))
        h_used, yp_ready, y_ready, y_free, neuron = (s.sem(n) for n in ("h_used", "yp_ready", "y_ready", "y_free", "neuron"))
        block = ctx.enter_context(nc.Block())

        @block.tensor
        def _(pe):
            pe.wait_ge(fc_split, 1)
            with pe.Fori(0, G) as g:
                for half in range(FT // HT):
                    for f in range(HT):
                        n = g * FT + half * HT + f
                        pe.wait_ge(act_done, n + 1)
                        k = 0
                        for w, v in ((fc1, x1), (fc1, x2), (fc2, x1)):
                            for c in range(DC):
                                at = c * F + (half * HT + f) * P
                                mm = pe.matmul(hp[f][:, :], w[:, at:at + P], v[:, c, bass.ts(g, N)],
                                               start=(k == 0), stop=(k == 5))
                                k += 1
                        mm.then_inc(hp_ready, 1)
                    if half == 0:
                        pe.wait_ge(pj_split, 1)
                    for f in range(HT):
                        pe.wait_ge(h_split, g * FT + half * HT + f + 1 + HT)
                        if half == 0 and f == 0:
                            pe.wait_ge(y_ready, g + 1)
                        at = (half * HT + f) * D
                        for t in range(TT):
                            for k, (a, b) in enumerate(((h1, pj1), (h1, pj2), (h2, pj1))):
                                mm = pe.matmul(yp[:, t, 0:D], a[:, f, t * P:(t + 1) * P], b[:, at:at + D],
                                               start=(half == 0 and f == 0 and k == 0),
                                               stop=(half == 1 and f == HT - 1 and k == 2))
                        mm.then_inc(h_used, 1)

        @block.scalar
        def _(act):
            act.activation(pj1[:, :], raw_pj[:, :], ACT.Copy).then_inc(pj1_done, 1)
            act.sem_inc(act_done, HT)
            act.sem_inc(relu_done, 2)
            act.sem_inc(y_ready, 1)

            def copy_y(g):
                act.wait_ge(h_used, g * FT + FT + HT)
                act.wait_ge(y_free, g + 1)
                act.activation(y[:, :, :], yp[:, :, 0:D], ACT.Copy).then_inc(y_ready, 1)

            def half_of(g, half):
                for f in range(HT):
                    n = g * FT + half * HT + f
                    act.wait_ge(hp_ready, n + 1)
                    act.wait_ge(act_done, n + HT - 1)
                    act.activation(r[:, f % 2, :], hp[f][:, :], ACT.Relu).then_inc(relu_done, 1)
                    act.wait_ge(relu_done, n + 3)
                    act.wait_ge(h_split, n + 1)
                    act.activation(h[:, f, :], r[:, f % 2, :], ACT.Square)
                    act.wait_ge(h_used, n + 1)
                    act.activation(h1[:, f, :], r[:, f % 2, :], ACT.Square).then_inc(act_done, 1)

            half_of(0, 0)
            half_of(0, 1)
            with act.Fori(0, G - 1) as i:
                copy_y(i)
                half_of(i + 1, 0)
                half_of(i + 1, 1)
            copy_y(G - 1)

        @block.vector
        def _(dve):
            dve.sem_inc(h_split, HT)
            dve.sem_inc(h_used, HT)
            dve.sem_inc(y_free, 1)
            dve.tensor_copy(fc1[:, :], raw_fc[:, :]).then_inc(fc1_done, 1)
            dve.wait_ge(fc1_done, 1)
            dve.tensor_tensor(fc2[:, :], raw_fc[:, :], fc1[:, :].bitcast(F32), ALU.subtract).then_inc(fc_split, 1)
            dve.wait_ge(pj1_done, 1)
            dve.tensor_tensor(pj2[:, :], raw_pj[:, :], pj1[:, :].bitcast(F32), ALU.subtract).then_inc(pj_split, 1)

            def split(n, f):
                dve.wait_ge(act_done, n + 1 + HT)
                dve.wait_ge(h_used, n + 1)
                dve.tensor_tensor(h2[:, f, :], h[:, f, :], h1[:, f, :].bitcast(F32), ALU.subtract).then_inc(h_split, 1)

            def first(g):
                dve.wait_ge(y_ready, g + 2)
                return dve.tensor_scalar(spk[:, :, :], y[:, :, :], THRESHOLD, None, ALU.is_gt)

            def decay(src):
                return lambda g: dve.scalar_tensor_tensor(out=leak[:, :, :], in0=src[:, :, :], scalar=BETA,
                                                          in1=y[:, :, :], op0=ALU.mult, op1=ALU.add)

            def reset(src):
                return lambda g: dve.scalar_tensor_tensor(out=mem[:, :, :], in0=src[:, :, :], scalar=THRESHOLD,
                                                          in1=leak[:, :, :], op0=ALU.is_gt, op1=ALU.subtract,
                                                          reverse1=True)

            def count(g):
                return dve.scalar_tensor_tensor(out=spk[:, :, :], in0=mem[:, :, :], scalar=THRESHOLD,
                                                in1=spk[:, :, :], op0=ALU.is_gt, op1=ALU.add)

            def add_to_x(g):
                xg = x[:, bass.ts(g, TT), :]
                return dve.scalar_tensor_tensor(out=xg, in0=spk[:, :, :], scalar=0.5 / STEPS, in1=xg,
                                                op0=ALU.mult, op1=ALU.add)

            chain = [first]
            for k in range(1, STEPS):
                chain += [decay(y if k == 1 else mem), reset(y if k == 1 else mem), count]
            chain.append(add_to_x)
            L = len(chain)

            def neuron_steps(g, todo):
                for k in todo:
                    if k:
                        dve.wait_ge(neuron, g * L + k)
                    chain[k](g).then_inc(neuron, 1)
                if L - 1 in todo:
                    dve.wait_ge(neuron, g * L + L)
                    dve.sem_inc(y_free, 1)

            for f in range(FT):
                split(f, f % HT)
            share = [[] for _ in range(FT)]
            for k in range(L):
                share[HT * (k // (L // 2)) + min(HT - 1, k % (L // 2))].append(k)
            with dve.Fori(0, G - 1) as i:
                for f in range(FT):
                    split((i + 1) * FT + f, f % HT)
                    neuron_steps(i, share[f])
            neuron_steps(G - 1, range(L))


def wait_if(eng, sem, value):
    if not isinstance(value, int) or value > 0:
        eng.wait_ge(sem, value)


def stage_linear_attention(nc, core, stage, ins):
    T, x = core["T"], core["x"]
    H, DV, DF = 8, 32, 64
    NP = H // 2
    SCALE = DF ** -0.5
    with ExitStack() as ctx:
        s = Scope(nc, ctx, stage)
        ln = stats_buffers(s, T)
        w_nat = [s.sb(f"w{n}_nat", [P, DC, D]) for n in "qk"]
        blocks = [s.sb(f"fm{n}", [P, P]) for n in "qk"]
        b_raw = [s.sb(f"b{n}_raw", [P, 1]) for n in "qk"]
        b_col = [s.sb(f"b{n}", [P, 1]) for n in "qk"]
        w_feat = [s.sb(f"w{n}_feat", [P, DC, H, 2, 32]) for n in "qk"]
        wv, wo_raw, wo, rms = s.sb("wv", [P, DC, D]), s.sb("wo_raw", [P, DC, D]), s.sb("wo", [P, DC, D]), s.sb("rms", [P, 1])
        keep = s.sb("keep", [P, P])
        xn, xT = s.sb("xn", [P, 2, D]), s.sb("xT", [P, 2, DC, P])
        qf, kf, kt = s.sb("qf", [P, 2, NP, P]), s.sb("kf", [P, 2, NP, P]), s.sb("kt", [P, 2, NP, P])
        v = s.sb("v", [P, 2, D])
        am = s.sb("am", [P, 2, H, P])
        S = s.sb("S", [P, NP, 2 * DV])
        o, sq, on, oT = s.sb("o", [P, 2, D]), s.sb("sq", [P, 2, D]), s.sb("on", [P, 2, D]), s.sb("oT", [P, DC, P])
        ss, ms, rs = s.sb("ss", [P, 2, H]), s.sb("ms", [P, 2, H]), s.sb("rs", [P, 2, H])
        half_neg = s.sb("half_neg", [P, H])
        bank0, bank4 = s.ps("bank0", [P, 512]), s.ps("bank4", [P, 512])
        trp, vp = bank0[:, 0:D].rearrange("p (c q) -> p c q", c=DC), bank0[:, D:2 * D]
        qp, kp = s.ps("qp", [P, NP, P]), s.ps("kp", [P, NP, P])
        ktp = s.ps("ktp", [P, NP, P])
        sp_new = ktp[:, 0:2, :].rearrange("p a q -> p (a q)")
        ap = [s.ps(f"ap{k}", [P, 4, P]) for k in range(2)]
        op = s.ps("op", [P, D])
        oTp, yp = bank4[:, 0:D].rearrange("p (c q) -> p c q", c=DC), bank4[:, D:2 * D]
        w_in, fm_in, zeroed, prep, half_set = (s.sem(n) for n in ("w_in", "fm_in", "zeroed", "prep", "half_set"))
        wf_ready, wf_done = s.sem("wf_ready"), s.sem("wf_done")
        names = ("xn_ready", "tr_done", "xT_done", "q_ready", "k_ready", "v_ready", "q_done", "k_done", "v_done",
                 "kt_ready", "kt_done", "a_ready", "masked", "o_ready", "o_done", "sq_done", "S_done", "ss_done",
                 "ms_done", "rs_done", "on_done", "oT_ready", "oT_done", "y_ready", "x_done")
        m = {n: s.sem(n) for n in names}
        block = ctx.enter_context(nc.Block())

        def chunks(eng, step):
            for t in range(2):
                step(t, t, True, True)
            with eng.Fori(0, (T - 4) // 2) as i:
                for k in range(2):
                    step(i * 2 + (2 + k), k, True, True)
            step(T - 2, 0, True, False)
            step(T - 1, 1, False, False)

        @block.sync
        def _(sp):
            for dst, src in ((w_nat[0], ins["lwq"]), (w_nat[1], ins["lwk"]), (wv, ins["lwv"]), (wo_raw, ins["lwo"])):
                sp.dma_start(dst[:, :, :], src.rearrange("p (c n) -> p c n", c=DC)).then_inc(w_in, 16)
            for dst, src in ((b_raw[0], ins["lbq"]), (b_raw[1], ins["lbk"]), (rms, ins["lrms"]), (keep, ins["keep_kq"])):
                sp.dma_start(dst[:, :], src).then_inc(w_in, 16)
            sp.wait_ge(zeroed, 2)
            for n, src in enumerate((ins["lfq"], ins["lfk"])):
                for j in range(4):
                    sp.dma_start(blocks[n][32 * j:32 * j + 32, 32 * j:32 * j + 32], src).then_inc(fm_in, 16)
            sp.wait_ge(w_in, 16 * 8)
            sp.wait_ge(fm_in, 16 * 2 * 4)

        @block.gpsimd
        def _(pool):
            pool.memset(half_neg[:, :], -0.5).then_inc(half_set, 1)
            pool.wait_ge(half_set, 1)

            def step(t, k, *_):
                pool.wait_ge(m["ms_done"], t + 1)
                wait_if(pool, m["on_done"], t - 1)
                pool.tensor_tensor(rs[:, k, :], ms[:, k, :], half_neg[:, :], ALU.pow).then_inc(m["rs_done"], 1)

            chunks(pool, step)

        @block.tensor
        def _(pe):
            pe.wait_ge(w_in, 16 * 8)
            pe.wait_ge(fm_in, 16 * 2 * 4)
            for n, dst in enumerate((qp, kp)):
                for c in range(DC):
                    for j in range(DC):
                        mm = pe.matmul(dst[:, c * DC + j, :], w_nat[n][:, j, c * P:(c + 1) * P], blocks[n][:, :],
                                       start=True, stop=True)
                mm.then_inc(wf_ready, 1)
            pe.wait_ge(wf_done, 4)

            def x_transposes(t, k):
                pe.wait_ge(m["xn_ready"], t + 1)
                wait_if(pe, m["v_done"], t)
                for c in range(DC):
                    mm = pe.transpose(trp[:, c, :], xn[:, k, c * P:(c + 1) * P], core["ident"][:, :])
                mm.then_inc(m["tr_done"], 1)

            def qk(t, k):
                pe.wait_ge(m["xT_done"], t + 1)
                for n, (dst, read, ready) in enumerate(((qp, "q_done", "q_ready"), (kp, "k_done", "k_ready"))):
                    wait_if(pe, m[read], t)
                    wf = w_feat[n][:, :, :, :, :].rearrange("p c h s e -> p c (h s e)")
                    for f in range(NP):
                        for c in range(DC):
                            mm = pe.matmul(dst[:, f, :], wf[:, c, f * P:(f + 1) * P], xT[:, k, c, :],
                                           start=(c == 0), stop=(c == DC - 1))
                    mm.then_inc(m[ready], 1)

            def values(t, k):
                for c in range(DC):
                    mm = pe.matmul(vp, xT[:, k, c, :], wv[:, c, :], start=(c == 0), stop=(c == DC - 1))
                mm.then_inc(m["v_ready"], 1)

            def k_transposes(t, k):
                pe.wait_ge(m["k_done"], t + 1)
                pe.wait_ge(m["S_done"], t * 2 + 2)
                for f in range(NP):
                    mm = pe.transpose(ktp[:, f, :], kf[:, k, f, :], core["ident"][:, :])
                mm.then_inc(m["kt_ready"], 1)

            def inside(t, k):
                pe.wait_ge(m["q_done"], t + 1)
                pe.wait_ge(m["k_done"], t + 1)
                wait_if(pe, m["masked"], t * 2)
                for f in range(NP):
                    for odd in range(2):
                        r = slice(DF * odd, DF * odd + DF)
                        mm = pe.matmul(ap[odd][:, f, :], kf[r, k, f, :], qf[r, k, f, :], start=True, stop=True)
                        if f == NP - 1:
                            mm.then_inc(m["a_ready"], 1)

            def outputs(t, k):
                pe.wait_ge(m["masked"], t * 2 + 2)
                pe.wait_ge(m["v_done"], t + 1)
                pe.wait_ge(m["kt_done"], t + 1)
                pe.wait_ge(m["S_done"], t * 2 + 2)
                wait_if(pe, m["sq_done"], t)
                for f in range(NP):
                    pe.matmul(op[:, f * 64:(f + 1) * 64], qf[:, k, f, :], S[:, f, :], start=True, stop=True)
                    for j in range(2):
                        h = 2 * f + j
                        pe.matmul(op[:, h * DV:(h + 1) * DV], am[:, k, j * NP + f, :], v[:, k, h * DV:(h + 1) * DV],
                                  start=False, stop=True, skip_group_check=True)
                for f in range(NP):
                    mm = pe.matmul(sp_new[:, f * 64:(f + 1) * 64], kt[:, k, f, :], v[:, k, f * 64:(f + 1) * 64],
                                   start=True, stop=True)
                mm.then_inc(m["o_ready"], 1)

            def o_transposes(t, k):
                pe.wait_ge(m["on_done"], t + 1)
                wait_if(pe, m["x_done"], t)
                for c in range(DC):
                    mm = pe.transpose(oTp[:, c, :], on[:, k, c * P:(c + 1) * P], core["ident"][:, :])
                mm.then_inc(m["oT_ready"], 1)

            def project(t):
                pe.wait_ge(m["oT_done"], t + 1)
                for c in range(DC):
                    mm = pe.matmul(yp, oT[:, c, :], wo[:, c, :], start=(c == 0), stop=(c == DC - 1))
                mm.then_inc(m["y_ready"], 1)

            x_transposes(0, 0)
            qk(0, 0)
            values(0, 0)
            k_transposes(0, 0)

            def step(t, k, has_next, _):
                if has_next:
                    x_transposes(t + 1, 1 - k)
                inside(t, k)
                if has_next:
                    qk(t + 1, 1 - k)
                first = isinstance(t, int) and t == 0
                if not first:
                    o_transposes(t - 1, 1 - k)
                if has_next:
                    values(t + 1, 1 - k)
                outputs(t, k)
                if not first:
                    project(t - 1)
                if has_next:
                    k_transposes(t + 1, 1 - k)

            chunks(pe, step)
            o_transposes(T - 1, 1)
            project(T - 1)

        @block.scalar
        def _(act):
            act_std(act, ln, core["cols"][:, 0:1])
            for n, src in enumerate((qp, kp)):
                act.wait_ge(wf_ready, n + 1)
                act.activation(w_feat[n][:, :, :, 0, :], src[:, :, :].rearrange("p (c j) (h e) -> p c (j h) e", c=DC, e=32),
                               ACT.Copy).then_inc(wf_done, 1)
                act.activation(w_feat[n][:, :, :, 1, :], src[:, :, :].rearrange("p (c j) (h e) -> p c (j h) e", c=DC, e=32),
                               ACT.Copy, scale=-1.0).then_inc(wf_done, 1)
            act.wait_ge(prep, 3)

            def front(t, k):
                act.wait_ge(m["tr_done"], t + 1)
                wait_if(act, m["v_ready"], t - 1)
                act.activation(xT[:, k, :, :], trp, ACT.Copy).then_inc(m["xT_done"], 1)
                wait_if(act, m["o_ready"], t - 1)
                act.wait_ge(m["q_ready"], t + 1)
                act.activation(qf[:, k, :, :], qp[:, :, :], ACT.Exp, bias=b_col[0][:, 0:1]).then_inc(m["q_done"], 1)
                act.wait_ge(m["k_ready"], t + 1)
                act.activation(kf[:, k, :, :], kp[:, :, :], ACT.Exp, bias=b_col[1][:, 0:1]).then_inc(m["k_done"], 1)

            def k_rows(t, k):
                act.wait_ge(m["kt_ready"], t + 1)
                act.activation(kt[:, k, :, :], ktp[:, :, :], ACT.Copy).then_inc(m["kt_done"], 1)

            def o_out(t, k):
                act.wait_ge(m["o_ready"], t + 1)
                wait_if(act, m["on_done"], t - 1)
                act.activation(o[:, k, :], op[:, :], ACT.Copy, scale=SCALE).then_inc(m["o_done"], 1)
                act.activation(sq[:, k, :], op[:, :], ACT.Square, scale=SCALE).then_inc(m["sq_done"], 1)

            front(0, 0)
            k_rows(0, 0)

            def step(t, k, has_next, _):
                if has_next:
                    front(t + 1, 1 - k)
                o_out(t, k)
                if has_next:
                    k_rows(t + 1, 1 - k)

            chunks(act, step)

        @block.vector
        def _(dve):
            for n in range(2):
                dve.memset(blocks[n][:, :], 0.0).then_inc(zeroed, 1)
            dve.memset(S[:, :, :], 0.0).then_inc(m["S_done"], 1)
            dve.sem_inc(m["S_done"], 1)
            dve_stats(dve, x, T, ln)
            for k in range(2):
                dve_normalise(dve, xn[:, k, :], x, ln, k).then_inc(m["xn_ready"], 1)
            dve.wait_ge(w_in, 16 * 8)
            for n in range(2):
                dve.tensor_tensor(b_col[n][:, :], b_raw[n][:, :], core["cols"][:, 1:2], ALU.mult).then_inc(prep, 1)
            dve.tensor_scalar(wo[:, :, :], wo_raw[:, :, :], rms[:, 0:1], None, ALU.mult).then_inc(prep, 1)
            dve.wait_ge(m["S_done"], 2)

            def v_out(t, k):
                dve.wait_ge(m["v_ready"], t + 1)
                wait_if(dve, m["o_ready"], t - 1)
                dve.tensor_copy(v[:, k, :], vp).then_inc(m["v_done"], 1)

            def mask(t, k):
                wait_if(dve, m["o_ready"], t - 1)
                for half in range(2):
                    dve.wait_ge(m["a_ready"], t * 2 + half + 1)
                    dve.tensor_tensor(am[:, k, 4 * half:4 * half + 4, :], ap[half][:, :, :],
                                      keep[:, :].unsqueeze(1).broadcast_to([P, 4, P]), ALU.mult).then_inc(m["masked"], 1)

            def oT_out(t):
                dve.wait_ge(m["oT_ready"], t + 1)
                wait_if(dve, m["y_ready"], t)
                dve.tensor_copy(oT[:, :, :], oTp).then_inc(m["oT_done"], 1)

            def add_y(t):
                dve.wait_ge(m["y_ready"], t + 1)
                dve.tensor_tensor(x[:, t, :], yp, x[:, t, :], ALU.add).then_inc(m["x_done"], 1)

            def add_S(t):
                dve.wait_ge(m["o_ready"], t + 1)
                for j in range(2):
                    r, c = slice(DF * j, DF * j + DF), slice(DV * j, DV * j + DV)
                    new = sp_new.rearrange("p (f n) -> p f n", f=NP)
                    dve.tensor_tensor(S[r, :, c], new[r, :, c], S[r, :, c], ALU.add).then_inc(m["S_done"], 1)

            def norm_a(t, k):
                dve.wait_ge(m["sq_done"], t + 1)
                dve.reduce_sum(ss[:, k, :], sq[:, k, :].rearrange("p (h e) -> p h e", e=DV), AX_X).then_inc(m["ss_done"], 1)
                dve.wait_ge(m["ss_done"], t + 1)
                dve.tensor_scalar(ms[:, k, :], ss[:, k, :], 1.0 / DV, EPS, ALU.mult, ALU.add).then_inc(m["ms_done"], 1)

            def norm_b(t, k):
                dve.wait_ge(m["rs_done"], t + 1)
                dve.tensor_tensor(on[:, k, :].rearrange("p (h e) -> p h e", e=DV),
                                  o[:, k, :].rearrange("p (h e) -> p h e", e=DV),
                                  rs[:, k, :].unsqueeze(2).broadcast_to([P, H, DV]), ALU.mult).then_inc(m["on_done"], 1)

            v_out(0, 0)

            def step(t, k, has_next, has_two):
                first = isinstance(t, int) and t == 0
                mask(t, k)
                if has_two:
                    dve_normalise(dve, xn[:, k, :], x, ln, t + 2).then_inc(m["xn_ready"], 1)
                if not first:
                    oT_out(t - 1)
                if has_next:
                    v_out(t + 1, 1 - k)
                add_S(t)
                if not first:
                    add_y(t - 1)
                norm_a(t, k)
                norm_b(t, k)

            chunks(dve, step)
            oT_out(T - 1)
            add_y(T - 1)


def stage_softmax_attention(nc, core, stage, ins):
    T = core["T"]
    Tok = T * P
    H, HD = 16, 16
    qk_parts = nc.dram_tensor(f"{stage}_qk_parts", (2, 3, H * HD, Tok), BF16, kind="Internal").ap()
    raw_dram = nc.dram_tensor(f"{stage}_raw", (2, HD + 1, H, Tok), F32, kind="Internal").ap()
    with ExitStack() as ctx:
        s = Scope(nc, ctx, stage)
        v_ones = s.sb("v_ones", [P, T, H, HD + 1])
        softmax_project(nc, core, f"{stage}p", ins, qk_parts, v_ones, H, HD)
        softmax_heads(nc, core, f"{stage}h", ins, qk_parts, v_ones, raw_dram, H, HD)
    softmax_output(nc, core, f"{stage}o", ins, raw_dram, H, HD)


def softmax_project(nc, core, stage, ins, qk_parts, v_ones, H, HD):
    T, x = core["T"], core["x"]
    TT = 4
    G = T // TT
    N = TT * P
    with ExitStack() as ctx:
        s = Scope(nc, ctx, stage)
        ln = stats_buffers(s, T)
        w = s.sb("w", [P, DC, 3 * D])
        xn, xT = s.sb("xn", [P, 2, D]), s.sb("xT", [P, 2, DC, N])
        rest = s.sb("rest", [P, 2, N])
        parts = [s.sb(f"parts{j}", [P, 3, N], BF16) for j in range(4)]
        trp = [s.ps(f"trp{k}", [P, DC, P]) for k in range(2)]
        qp = [s.ps(f"qp{j}", [P, N]) for j in range(4)]
        vp = [s.ps(f"vp{k}", [P, H, HD]) for k in range(2)]
        w_in = s.sem("w_in")
        stored = [s.sem(f"stored{j}") for j in range(4)]
        names = ("ones_set", "xn_ready", "tr_done", "xT_done", "q_ready", "part1", "rest_done", "part2", "part3",
                 "v_ready", "v_done")
        m = {n: s.sem(n) for n in names}
        block = ctx.enter_context(nc.Block())
        columns = (0, P, 2 * D, 2 * D + P)

        def groups(eng, step):
            step(0, 0, "first")
            with eng.Fori(0, (G - 2) // 2) as i:
                step(i * 2 + 1, 1, "inside")
                step(i * 2 + 2, 0, "inside")
            step(G - 1, 1, "last")

        @block.sync
        def _(sp):
            sp.dma_start(w[:, :, :], ins["swqvk"].rearrange("p (c n) -> p c n", c=DC)).then_inc(w_in, 16)
            with sp.Fori(0, G) as g:
                for j in range(4):
                    sp.wait_ge(m["part3"], g * 4 + (j + 1))
                    dst = qk_parts[j // 2, :, (j % 2) * P:(j % 2 + 1) * P, bass.ts(g, N)]
                    sp.dma_start(dst.rearrange("a p n -> p a n"), parts[j][:, :, :]).then_inc(stored[j], 16)
            for j in range(4):
                sp.wait_ge(stored[j], 16 * G)

        @block.tensor
        def _(pe):
            pe.wait_ge(w_in, 16)

            def transposes(t, k):
                pe.wait_ge(m["xn_ready"], t + 1)
                wait_if(pe, m["xT_done"], t - 1)
                for c in range(DC):
                    mm = pe.transpose(trp[k][:, c, :], xn[:, k, c * P:(c + 1) * P], core["ident"][:, :])
                mm.then_inc(m["tr_done"], 1)

            for t in range(TT):
                transposes(t, t % 2)

            def step(g, k, position):
                pe.wait_ge(m["xT_done"], g * TT + TT)
                for j in range(4):
                    n = g * 4 + j
                    wait_if(pe, m["rest_done"], n - 3)
                    for c in range(DC):
                        mm = pe.matmul(qp[j][:, :], w[:, c, columns[j]:columns[j] + P], xT[:, k, c, :],
                                       start=(c == 0), stop=(c == DC - 1))
                    mm.then_inc(m["q_ready"], 1)
                    if position != "last":
                        transposes(g * TT + (TT + j), j % 2)
                for j in range(TT):
                    t = g * TT + j
                    wait_if(pe, m["v_done"], t - 1)
                    for c in range(DC):
                        mm = pe.matmul(vp[j % 2][:, :, :].rearrange("p h e -> p (h e)"), xT[:, k, c, j * P:(j + 1) * P],
                                       w[:, c, D:2 * D], start=(c == 0), stop=(c == DC - 1))
                    mm.then_inc(m["v_ready"], 1)

            groups(pe, step)

        @block.scalar
        def _(act):
            act_std(act, ln, core["cols"][:, 0:1])

            def xT_out(t, k, gk, j):
                act.wait_ge(m["tr_done"], t + 1)
                act.activation(xT[:, gk, :, j * P:(j + 1) * P], trp[k][:, :, :], ACT.Copy).then_inc(m["xT_done"], 1)

            def second_part(n, j):
                act.wait_ge(m["rest_done"], n + 1)
                act.activation(parts[j][:, 1, :], rest[:, j % 2, :], ACT.Copy).then_inc(m["part2"], 1)

            for t in range(TT):
                xT_out(t, t % 2, 0, t)

            def step(g, k, position):
                if position != "last":
                    wait_if(act, m["v_ready"], g * TT)
                for j in range(4):
                    n = g * 4 + j
                    act.wait_ge(m["q_ready"], n + 1)
                    wait_if(act, stored[j], g * 16)
                    act.activation(parts[j][:, 0, :], qp[j][:, :], ACT.Copy).then_inc(m["part1"], 1)
                    if position != "last":
                        xT_out(g * TT + (TT + j), j % 2, 1 - k, j)
                    if not (position == "first" and j == 0):
                        second_part(n - 1, (j + 3) % 4)

            groups(act, step)
            second_part(G * 4 - 1, 3)

        @block.vector
        def _(dve):
            dve.memset(v_ones[:, :, :, HD:HD + 1], 1.0).then_inc(m["ones_set"], 1)
            dve_stats(dve, x, T, ln)

            def normalise(t, k):
                wait_if(dve, m["tr_done"], t - 1)
                dve_normalise(dve, xn[:, k, :], x, ln, t).then_inc(m["xn_ready"], 1)

            def third_part(n, j):
                dve.wait_ge(m["part2"], n + 1)
                dve.tensor_tensor(parts[j][:, 2, :], rest[:, j % 2, :], parts[j][:, 1, :],
                                  ALU.subtract).then_inc(m["part3"], 1)

            for t in range(TT):
                normalise(t, t % 2)

            def step(g, k, position):
                if position != "last":
                    normalise(g * TT + TT, 0)
                for j in range(4):
                    n = g * 4 + j
                    dve.wait_ge(m["part1"], n + 1)
                    wait_if(dve, m["part3"], n - 1)
                    dve.tensor_tensor(rest[:, j % 2, :], qp[j][:, :], parts[j][:, 0, :],
                                      ALU.subtract).then_inc(m["rest_done"], 1)
                    if position != "last" and j < TT - 1:
                        normalise(g * TT + (TT + j + 1), (j + 1) % 2)
                    if not (position == "first" and j == 0):
                        third_part(n - 1, (j + 3) % 4)
                for j in range(TT):
                    t = g * TT + j
                    dve.wait_ge(m["v_ready"], t + 1)
                    dve.tensor_copy(v_ones[:, t, :, 0:HD], vp[j % 2][:, :, :]).then_inc(m["v_done"], 1)

            groups(dve, step)
            third_part(G * 4 - 1, 3)


def softmax_heads(nc, core, stage, ins, qk_parts, v_ones, raw_dram, H, HD):
    T = core["T"]
    Tok = T * P
    Q_PARTS, K_PARTS = (0, 0, 0, 1, 1, 2), (0, 1, 2, 0, 1, 0)
    R = HD * len(Q_PARTS)
    TG = 4
    G = T // TG
    N = TG * P
    M = 2 * (HD + 1)
    SCALE = float(D) ** -0.5

    chunks = [(t, c) for t in range(T) for c in range(t // TG + 1)]
    NA = len(chunks) + 1
    units = [(g, p) for g in range(G) for p in range(2 * g + 2)]
    NB = len(units)
    last_unit = [sum(2 * a + 2 for a in range(g + 1)) - 1 for g in range(G)]
    P_RING, RING = 3, 6
    LAG = 4
    FIRST_A, LAST_A = 4, NB - 4
    share = [[] for _ in range(NB)]
    for n in range(NA - 1):
        share[FIRST_A + n * (LAST_A - FIRST_A) // (NA - 1)].append(n)

    def dve_from(u):
        return N + (N // 2 if share[u] else 0)

    def unit_tiles(u):
        g, pair = units[u]
        return [(2 * pair + kk, max(0, 2 * pair + kk - TG * g) * P) for kk in range(2)]

    def unit_columns(u, first=0, end=2 * N):
        (_, lo0), (_, lo1) = unit_tiles(u)
        ranges = [(lo0, 2 * N)] if lo1 == 0 else [(lo0, N), (N + lo1, 2 * N)]
        cut = [(max(lo, first), min(hi, end)) for lo, hi in ranges]
        return [(lo, hi) for lo, hi in cut if lo < hi]

    with ExitStack() as ctx:
        s = Scope(nc, ctx, stage)
        qs = [s.sb(f"qs{k}", [P, Tok], BF16) for k in range(2)]
        ks = [s.sb(f"ks{k}", [P, Tok], BF16) for k in range(2)]
        vh = [s.sb(f"vh{k}", [P, T, M], F32R) for k in range(2)]
        p = [s.sb(f"p{k}", [P, 2 * N]) for k in range(P_RING)]
        p1 = [s.sb(f"p1{k}", [P, 2 * N], F32R) for k in range(RING)]
        p2 = [s.sb(f"p2{k}", [P, 2 * N], F32R) for k in range(RING)]
        top = [s.sb(f"top{k}", [P, T, G]) for k in range(2)]
        neg, rest = s.sb("neg", [P, 2, T]), s.sb("rest", [P, 2, T])
        neg_parts = s.sb("neg_parts", [P, 3 * T], BF16)
        neg_rows = s.sb("neg_rows", [3 * T, P], BF16)
        hide_raw = s.sb("hide_raw", [P, 3, P])
        hide_kq, hide_qk, ident = s.sb("hide_kq", [P, P], BF16), s.sb("hide_qk", [P, P], BF16), s.sb("identb", [P, P], BF16)
        v_head = s.sb("v_head", [P, T, HD + 1])
        raw_o = [s.sb(f"raw_o{k}", [M, N]) for k in range(2)]
        ap = [s.ps(f"ap{k}", [P, N]) for k in range(2)]
        st = [s.ps(f"st{k}", [P, 2 * N]) for k in range(2)]
        op = [s.ps(f"op{k}", [P, N]) for k in range(2)]
        hide_in, const_done, m_in = (s.sem(n) for n in ("hide_in", "const_done", "m_in"))
        qk_in = [s.sem(f"qk_in{k}") for k in range(2)]
        raw_out = [s.sem(f"raw_out{k}") for k in range(2)]
        names = ("a_ready", "a_free", "max_step", "max_parts", "s_ready", "p_ready", "p2_pool", "p2_dve",
                 "pv_done", "vh_step", "vh_ready", "raw_done")
        m = {n: s.sem(n) for n in names}
        block = ctx.enter_context(nc.Block())
        LOAD = 16 * 9

        def heads(eng, step):
            step(0, 0, 0, False, True)
            step(1, 1, 0, True, True)
            with eng.Fori(0, H // 2 - 2) as i:
                step(i * 2 + 2, 0, i + 1, True, True)
                step(i * 2 + 3, 1, i + 1, True, True)
            step(H - 2, 0, H // 2 - 1, True, True)
            step(H - 1, 1, H // 2 - 1, True, False)

        def behind(h, k, has_prev, u, lag):
            if u >= lag:
                return h, k, u - lag
            return (h - 1, 1 - k, NB + u - lag) if has_prev else None

        @block.sync
        def _(sp):
            for k, name in enumerate(("hide_kq", "hide_qk", "ident")):
                sp.dma_start(hide_raw[:, k, :], ins[name]).then_inc(hide_in, 16)

            def load(h, k):
                for n, part in enumerate(Q_PARTS):
                    sp.dma_start(qs[k][n * HD:(n + 1) * HD, :],
                                 qk_parts[0, part, bass.ts(h, HD), :]).then_inc(qk_in[k], 16)
                row = 0
                for count in (3, 2, 1):
                    src = qk_parts[1, 0:count, bass.ts(h, HD), :]
                    sp.dma_start(ks[k][row:row + count * HD, :], src).then_inc(qk_in[k], 16)
                    row += count * HD

            def maxima(h, k):
                sp.wait_ge(m["a_free"], h * NA + (NA + 2))
                sp.dma_start(qs[k][R:R + 3, :].rearrange("a (t p) -> a t p", p=P), neg_rows[:, :]).then_inc(m_in, 16)

            def store(h, g):
                sp.wait_ge(m["raw_done"], h * G + (g + 3))
                dst = raw_dram[:, :, bass.ts(h, 1), g * N:(g + 1) * N]
                sp.dma_start(dst.rearrange("a e h n -> (a e) (h n)"), raw_o[g % 2][:, :]).then_inc(raw_out[g % 2], 16)

            load(0, 0)
            load(1, 1)
            maxima(0, 0)

            def step(h, k, half, has_prev, has_next):
                if has_prev:
                    store(h - 1, G - 1)
                for g in range(G - 1):
                    store(h, g)
                if has_next:
                    maxima(h + 1, 1 - k)
                    if not (isinstance(h, int) and h == H - 2):
                        sp.wait_ge(m["s_ready"], h * NB + NB)
                        load(h + 2, k)

            heads(sp, step)
            store(H - 1, G - 1)
            sp.wait_ge(m_in, 16 * H)
            for k in range(2):
                sp.wait_ge(raw_out[k], 16 * H * G // 2)

        @block.gpsimd
        def _(pool):
            def take_v(h, k, head_before=None):
                pool.tensor_copy(v_head[:, :, :], v_ones[:, :, h, :]).then_inc(m["vh_step"], 1)
                if head_before is not None:
                    pool.wait_ge(m["pv_done"], head_before * NB + (NB + RING))
                pool.wait_ge(m["vh_step"], h * 2 + 1)
                ones = v_head[:, :, HD:HD + 1].broadcast_to([P, T, HD + 1])
                pool.tensor_tensor(vh[k][:, :, 0:HD + 1], v_head[:, :, :], ones,
                                   ALU.mult).then_inc(m["vh_step"], 1)
                pool.wait_ge(m["vh_step"], h * 2 + 2)
                pool.tensor_tensor(vh[k][:, :, HD + 1:M], v_head[:, :, :], vh[k][:, :, 0:HD + 1].bitcast(F32),
                                   ALU.subtract).then_inc(m["vh_ready"], 1)

            take_v(0, 0)

            def step(h, k, half, has_prev, has_next):
                for u in range(NB):
                    b = h * NB + u
                    pool.wait_ge(m["p_ready"], b + 3)
                    for lo, hi in unit_columns(u, 0, dve_from(u)):
                        sub = pool.tensor_tensor(p2[u % RING][:, lo:hi], p[u % P_RING][:, lo:hi],
                                                 p1[u % RING][:, lo:hi].bitcast(F32), ALU.subtract)
                    sub.then_inc(m["p2_pool"], 1)
                    if u == LAG + 3 and has_next:
                        take_v(h + 1, 1 - k, h - 1 if has_prev else None)

            heads(pool, step)

        @block.tensor
        def _(pe):
            def pass_a(h, k, n):
                t, c = chunks[n]
                width = min(N, (t + 1) * P - c * N)
                bank = ap[(k + n) % 2]
                pe.wait_ge(m["a_free"], h * NA + (n + 1))
                diagonal = c == t // TG
                mm = pe.matmul(bank[:, 0:width], qs[k][0:R, t * P:(t + 1) * P], ks[k][0:R, c * N:c * N + width],
                               start=True, stop=not diagonal)
                if diagonal:
                    mm = pe.matmul(bank[:, width - P:width], ident[:, :], hide_qk[:, :], start=False, stop=True)
                mm.then_inc(m["a_ready"], 1)

            def transpose_maxima(h, k):
                pe.wait_ge(m["max_parts"], h + 1)
                pe.wait_ge(m["a_free"], h * NA + NA)
                pe.transpose(ap[(k + NA - 1) % 2][0:3 * T, 0:P // 2].bitcast(BF16), neg_parts[:, :],
                             ident[:, :]).then_inc(m["a_ready"], 1)

            def scores(h, k, u):
                g, pair = units[u]
                pe.wait_ge(m["p_ready"], h * NB + (u + 1))
                for kk, (tile, lo) in enumerate(unit_tiles(u)):
                    diagonal = tile >= TG * g
                    mm = pe.matmul(st[u % 2][:, kk * N + lo:(kk + 1) * N], ks[k][0:R + 3, tile * P:(tile + 1) * P],
                                   qs[k][0:R + 3, g * N + lo:(g + 1) * N], start=True, stop=not diagonal)
                    if diagonal:
                        mm = pe.matmul(st[u % 2][:, kk * N + lo:kk * N + lo + P], ident[:, :], hide_kq[:, :],
                                       start=False, stop=True)
                mm.then_inc(m["s_ready"], 1)

            def values(h, k, u):
                g, pair = units[u]
                if u == 0:
                    pe.wait_ge(m["vh_ready"], h + 1)
                pe.wait_ge(m["p2_pool"], h * NB + (u + (1 + P_RING)))
                pe.wait_ge(m["p2_dve"], h * NB + (u + (1 + P_RING)))
                if pair == 0:
                    pe.wait_ge(m["raw_done"], h * G + (g + 1))
                for n, (tile, lo) in enumerate(unit_tiles(u)):
                    for src in (p1, p2):
                        mm = pe.matmul(op[g % 2][0:M, lo:N], vh[k][:, tile, :], src[u % RING][:, n * N + lo:(n + 1) * N],
                                       start=(pair == 0 and n == 0 and src is p1), stop=(tile >= TG * g),
                                       skip_group_check=True)
                mm.then_inc(m["pv_done"], 1)

            pe.wait_ge(const_done, 7)
            pe.wait_ge(hide_in, 48)
            pe.wait_ge(qk_in[0], LOAD)
            for n in range(NA - 1):
                pass_a(0, 0, n)
            transpose_maxima(0, 0)

            def step(h, k, half, has_prev, has_next):
                pe.wait_ge(m_in, h * 16 + 16)
                for u in range(NB):
                    scores(h, k, u)
                    if has_next:
                        if u == FIRST_A:
                            pe.wait_ge(qk_in[1 - k], (half + 1 + k) * LOAD)
                        for n in share[u][:1]:
                            pass_a(h + 1, 1 - k, n)
                        if u == LAST_A + 2:
                            transpose_maxima(h + 1, 1 - k)
                    if (at := behind(h, k, has_prev, u, LAG)) is not None:
                        values(*at)
                    if has_next:
                        for n in share[u][1:]:
                            pass_a(h + 1, 1 - k, n)

            heads(pe, step)
            for u in range(NB - LAG, NB):
                values(H - 1, 1, u)

        @block.scalar
        def _(act):
            act.wait_ge(hide_in, 48)
            for k, dst in enumerate((hide_kq, hide_qk, ident)):
                act.activation(dst[:, :], hide_raw[:, k, :], ACT.Copy).then_inc(const_done, 1)
            act.sem_inc(m["p_ready"], 2)
            act.sem_inc(m["pv_done"], RING)
            for done in ("p2_pool", "p2_dve"):
                act.sem_inc(m[done], P_RING)

            def step(h, k, half, has_prev, has_next):
                for u in range(NB):
                    b = h * NB + u
                    act.wait_ge(m["s_ready"], b + 1)
                    for done in ("p2_pool", "p2_dve"):
                        act.wait_ge(m[done], b + 1)
                    act.wait_ge(m["pv_done"], b + 1)
                    for dst in (p[u % P_RING], p1[u % RING]):
                        for lo, hi in unit_columns(u):
                            ex = act.activation(dst[:, lo:hi], st[u % 2][:, lo:hi], ACT.Exp, scale=SCALE)
                    ex.then_inc(m["p_ready"], 1)

            heads(act, step)

        @block.vector
        def _(dve):
            for k in range(2):
                dve.memset(ks[k][R:R + 3, :], 1.0).then_inc(const_done, 1)
                dve.memset(top[k][:, :, :], -3.0e38).then_inc(const_done, 1)
            dve.sem_inc(m["a_free"], 2)
            dve.sem_inc(m["raw_done"], 2)
            dve.wait_ge(const_done, 7)

            def reduce(h, k, n):
                t, c = chunks[n]
                width = min(N, (t + 1) * P - c * N)
                dve.wait_ge(m["a_ready"], h * NA + (n + 1))
                dve.reduce_max(top[k][:, t, c:c + 1], ap[(k + n) % 2][:, 0:width], AX_X).then_inc(m["a_free"], 1)

            def split_maxima(h, k):
                step = m["max_step"]
                dve.wait_ge(m["a_free"], h * NA + (NA + 1))
                dve.tensor_reduce(neg[:, 0, :], top[k][:, :, :], AX_X, ALU.max).then_inc(step, 1)
                dve.wait_ge(step, h * 6 + 1)
                dve.tensor_scalar(neg[:, 1, :], neg[:, 0, :], -1.0, None, ALU.mult).then_inc(step, 1)
                src = neg[:, 1, :]
                for k3 in range(2):
                    part = neg_parts[:, k3 * T:(k3 + 1) * T]
                    dve.wait_ge(step, h * 6 + (2 + 2 * k3))
                    dve.tensor_copy(part, src).then_inc(step, 1)
                    dve.wait_ge(step, h * 6 + (3 + 2 * k3))
                    dve.tensor_tensor(rest[:, k3, :], src, part, ALU.subtract).then_inc(step, 1)
                    src = rest[:, k3, :]
                dve.wait_ge(step, h * 6 + 6)
                dve.tensor_copy(neg_parts[:, 2 * T:3 * T], src).then_inc(m["max_parts"], 1)

            def maxima_out(h, k):
                dve.wait_ge(m["a_ready"], h * NA + NA)
                wait_if(dve, m_in, h * 16)
                dve.tensor_copy(neg_rows[:, :], ap[(k + NA - 1) % 2][0:3 * T, 0:P // 2].bitcast(BF16)
                                ).then_inc(m["a_free"], 1)

            def raw_output(h, g):
                dve.wait_ge(m["pv_done"], h * NB + (last_unit[g] + 1 + RING))
                wait_if(dve, raw_out[g % 2], h * (16 * G // 2) + 16 * (g // 2))
                dve.tensor_copy(raw_o[g % 2][:, :], op[g % 2][0:M, :]).then_inc(m["raw_done"], 1)

            def second_parts(h, u):
                dve.wait_ge(m["p_ready"], h * NB + (u + 3))
                for lo, hi in unit_columns(u, dve_from(u)):
                    sub = dve.tensor_tensor(p2[u % RING][:, lo:hi], p[u % P_RING][:, lo:hi],
                                            p1[u % RING][:, lo:hi].bitcast(F32), ALU.subtract)
                sub.then_inc(m["p2_dve"], 1)

            for n in range(NA - 1):
                reduce(0, 0, n)
            split_maxima(0, 0)
            maxima_out(0, 0)

            def step(h, k, half, has_prev, has_next):
                for u in range(NB):
                    if has_next:
                        for n in share[u]:
                            reduce(h + 1, 1 - k, n)
                        if share[u] and share[u][-1] == NA - 2:
                            split_maxima(h + 1, 1 - k)
                        if u == LAST_A + 2:
                            maxima_out(h + 1, 1 - k)
                    if (at := behind(h, k, has_prev, u, 1)) is not None:
                        second_parts(at[0], at[2])
                    if (at := behind(h, k, has_prev, u, LAG)) is not None and at[2] in last_unit:
                        raw_output(at[0], last_unit.index(at[2]))

            heads(dve, step)
            second_parts(H - 1, NB - 1)
            raw_output(H - 1, G - 1)


def softmax_output(nc, core, stage, ins, raw_dram, H, HD):
    T, x = core["T"], core["x"]
    TG = 4
    G = T // TG
    N = TG * P
    with ExitStack() as ctx:
        s = Scope(nc, ctx, stage)
        wo = s.sb("wo", [P, DC, D])
        spread = s.sb("spread", [H, P])
        oT = [s.sb(f"oT{k}", [P, 2, DC, N]) for k in range(2)]
        den = [s.sb(f"den{k}", [H, 2, N]) for k in range(2)]
        den_sum = [s.sb(f"den_sum{k}", [H, N]) for k in range(2)]
        rden = [s.sb(f"rden{k}", [H, N]) for k in range(2)]
        o_sum = [s.sb(f"o_sum{k}", [P, DC, N]) for k in range(2)]
        o = [s.sb(f"o{k}", [P, DC, N]) for k in range(2)]
        rp = [s.ps(f"rp{k}", [P, N]) for k in range(2)]
        yp = [s.ps(f"yp{k}", [P, D]) for k in range(4)]
        w_in = s.sem("w_in")
        oT_in = [s.sem(f"oT_in{k}") for k in range(2)]
        names = ("sum_done", "den_done", "rden_done", "spread_done", "o_done", "y_ready", "x_done")
        m = {n: s.sem(n) for n in names}
        block = ctx.enter_context(nc.Block())

        @block.sync
        def _(sp):
            sp.dma_start(wo[:, :, :], ins["swo"].rearrange("p (c n) -> p c n", c=DC)).then_inc(w_in, 16)
            sp.dma_start(spread[:, :], ins["spread"]).then_inc(w_in, 16)

            def load(g, k):
                for a in range(2):
                    sp.dma_start(den[k][:, a, :], raw_dram[a, HD, :, bass.ts(g, N)]).then_inc(oT_in[k], 16)
                for a in range(2):
                    src = raw_dram[a, 0:HD, :, bass.ts(g, N)].rearrange("(c d) h n -> (d h) c n", c=DC)
                    sp.dma_start(oT[k][:, a, :, :], src).then_inc(oT_in[k], 16)

            load(0, 0)
            load(1, 1)
            with sp.Fori(0, G // 2 - 1) as i:
                for k in range(2):
                    sp.wait_ge(m["sum_done"], i * 2 + (k + 1))
                    sp.wait_ge(m["den_done"], i * 2 + (k + 1))
                    load(i * 2 + (2 + k), k)

        @block.gpsimd
        def _(pool):
            for k in range(2):
                pool.sem_inc(m["o_done"], 1)
            with pool.Fori(0, G // 2) as i:
                for k in range(2):
                    pool.wait_ge(oT_in[k], i * 64 + 64)
                    pool.wait_ge(m["rden_done"], i * 2 + (k + 1))
                    pool.tensor_tensor(den_sum[k][:, :], den[k][:, 0, :], den[k][:, 1, :],
                                       ALU.add).then_inc(m["den_done"], 1)
                    pool.wait_ge(m["o_done"], i * 2 + (k + 1))
                    pool.tensor_tensor(o_sum[k][:, :, :], oT[k][:, 0, :, :], oT[k][:, 1, :, :],
                                       ALU.add).then_inc(m["sum_done"], 1)

        @block.tensor
        def _(pe):
            pe.wait_ge(w_in, 32)
            with pe.Fori(0, G // 2) as i:
                for k in range(2):
                    g = i * 2 + k
                    pe.wait_ge(m["rden_done"], g + 3)
                    pe.matmul(rp[k][:, :], spread[:, :], rden[k][:, :], start=True, stop=True).then_inc(m["spread_done"], 1)
                    pe.wait_ge(m["o_done"], g + 3)
                    for t in range(TG):
                        pe.wait_ge(m["x_done"], g * TG + (t + 1))
                        for c in range(DC):
                            mm = pe.matmul(yp[t][:, :], o[k][:, c, t * P:(t + 1) * P], wo[:, c, :],
                                           start=(c == 0), stop=(c == DC - 1))
                        mm.then_inc(m["y_ready"], 1)

        @block.vector
        def _(dve):
            dve.sem_inc(m["x_done"], TG)
            dve.sem_inc(m["spread_done"], 2)
            dve.sem_inc(m["rden_done"], 2)

            def divide(g, k):
                dve.wait_ge(m["den_done"], g + 1)
                dve.wait_ge(m["spread_done"], g + 1)
                dve.reciprocal(rden[k][:, :], den_sum[k][:, :]).then_inc(m["rden_done"], 1)
                dve.wait_ge(m["sum_done"], g + 1)
                dve.wait_ge(m["spread_done"], g + 3)
                dve.tensor_tensor(o[k][:, :, :], o_sum[k][:, :, :],
                                  rp[k][:, :].unsqueeze(1).broadcast_to([P, DC, N]), ALU.mult).then_inc(m["o_done"], 1)

            def add_y(g):
                for t in range(TG):
                    dve.wait_ge(m["y_ready"], g * TG + (t + 1))
                    dve.tensor_tensor(x[:, g * TG + t, :], yp[t][:, :], x[:, g * TG + t, :],
                                      ALU.add).then_inc(m["x_done"], 1)

            divide(0, 0)
            divide(1, 1)
            add_y(0)
            with dve.Fori(0, G // 2 - 1) as i:
                for k in range(2):
                    divide(i * 2 + (k + 2), k)
                    add_y(i * 2 + (k + 1))
            add_y(G - 1)


STAGES = ['moe', 'lin', 'moe', 'spike', 'soft', 'spike']


def build(nc, ins, out_dram):
    Tok = ins["x"].shape[0]
    T = Tok // P
    with ExitStack() as ctx:
        s = Scope(nc, ctx, "core")
        NE = ins["up"].shape[0]
        core = dict(T=T, x=s.sb("x", [P, T, D]), ident=s.sb("ident", [P, P]), cols=s.sb("cols", [P, 4]),
                    iota8=s.sb("iota8", [P, 8]), comb=s.sb("comb", [P, T, NE]))
        stage_load(nc, core, ins["x"], ins)
        for n, kind in enumerate(STAGES):
            if kind in ("moe", "spike"):
                with ExitStack() as parts:
                    sp = Scope(nc, parts, f"{kind}{n}")
                    x1 = sp.sb("xT1", [P, DC, Tok], F32R)
                    x2 = sp.sb("xT2", [P, DC, Tok], F32R)
                    router = dict(E=NE - 1, w=ins["rw"], b=ins["rb"]) if kind == "moe" else None
                    first, second = (ins["up"][0], ins["dn"][0]) if kind == "moe" else (ins["fc"], ins["proj"])
                    raw1, raw2 = sp.sb("raw1", list(first.shape)), sp.sb("raw2", list(second.shape))
                    stage_norm(nc, core, f"norm{n}", x1, x2, router, [(raw1, first), (raw2, second)])
                    if kind == "moe":
                        stage_experts(nc, core, f"experts{n}", x1, x2, raw1, raw2, ins["up"], ins["dn"], NE)
                    else:
                        stage_spikes(nc, core, f"spikes{n}", x1, x2, raw1, raw2)
            if kind == "lin":
                stage_linear_attention(nc, core, f"lin{n}", ins)
            if kind == "soft":
                stage_softmax_attention(nc, core, f"soft{n}", ins)
        stage_store(nc, core, out_dram)


def kernel(**inputs):
    import numpy as np
    import concourse.bacc as _bacc
    from concourse.bass_utils import run_bass_kernel_spmd as _run

    a = {k: np.asarray(v) for k, v in inputs.items()}

    def by_rows(w):
        r, n = w.shape
        return np.ascontiguousarray(w.reshape(r // P, P, n).transpose(1, 0, 2).reshape(P, -1))

    x = a["L0_attn_x"]
    up = np.concatenate([a["L0_ffn_w_up"], a["L0_ffn_shared_w_up"]])
    dn = np.concatenate([a["L0_ffn_w_down"], a["L0_ffn_shared_w_down"]])
    H0, H1 = 8, 16
    cols = np.zeros((P, 4), np.float32)
    cols[:, 0] = EPS
    sign = np.where((np.arange(P) // 32) % 2 == 0, 1.0, -1.0)
    cols[:, 1] = sign
    cols[:, 2] = 1.0
    cols[:, 3] = -0.5
    k_after_q = np.arange(P)[:, None] > np.arange(P)[None, :]
    spread = np.tile(np.eye(H1, dtype=np.float32), (1, P // H1))
    arrays = {
        "spread": spread,
        "x": x.reshape(-1, D),
        "up": np.stack([by_rows(w.T) for w in up]),
        "dn": np.stack([by_rows(w.T) for w in dn]),
        "rw": by_rows(a["L0_ffn_router_w"].T).reshape(P, DC, -1),
        "rb": np.broadcast_to(a["L0_ffn_router_b"], (P, a["L0_ffn_router_b"].shape[0])),
        "ident": np.eye(P, dtype=np.float32),
        "cols": cols,
        "iota8": np.broadcast_to(np.arange(8, dtype=np.float32), (P, 8)),
        "keep_kq": (~k_after_q).astype(np.float32),
        "hide_kq": np.where(k_after_q, -1e30, 0.0).astype(np.float32),
        "hide_qk": np.where(k_after_q.T, -1e30, 0.0).astype(np.float32),
        "fc": by_rows(a["L1_ffn_W_fc"].T),
        "proj": by_rows(a["L1_ffn_W_proj"].T),
        "lwq": by_rows(a["L0_attn_Wq"]),
        "lwk": by_rows(a["L0_attn_Wk"]),
        "lwv": by_rows(a["L0_attn_Wv"].T),
        "lwo": by_rows(a["L0_attn_Wo"].T),
        "lfq": np.ascontiguousarray(a["L0_attn_fmq_w"].T),
        "lfk": np.ascontiguousarray(a["L0_attn_fmk_w"].T),
        "lbq": np.tile(a["L0_attn_fmq_b"], 4)[:, None],
        "lbk": np.tile(a["L0_attn_fmk_b"], 4)[:, None],
        "lrms": np.tile(a["L0_attn_rms_w"], 4)[:, None],
        "swqvk": by_rows(a["L1_attn_Wqvk"]),
        "swo": by_rows(a["L1_attn_Wo"].reshape(H1, -1, D).transpose(1, 0, 2).reshape(D, D)),
    }
    nc = _bacc.Bacc("TRN2", target_bir_lowering=False, num_devices=1)
    ins = {}
    used = {f"in_{k}": np.ascontiguousarray(v) for k, v in arrays.items()}
    for name, v in arrays.items():
        ins[name] = nc.dram_tensor(f"in_{name}", v.shape, mybir.dt.from_np(v.dtype), kind="ExternalInput").ap()
    out = nc.dram_tensor("out_0", (x.shape[0] * x.shape[1], D), F32, kind="ExternalOutput").ap()
    build(nc, ins, out)
    r = _run(nc, [used], core_ids=[0])
    return r.results[0]["out_0"].reshape(x.shape)
```

```python
from contextlib import ExitStack

import concourse.bass as bass
from concourse import mybir

P = 128
D = 256
DC = D // P
EPS = 1e-5
F32 = mybir.dt.float32
F32R = mybir.dt.float32r
BF16 = mybir.dt.bfloat16
U32 = mybir.dt.uint32
ALU = mybir.AluOpType
ACT = mybir.ActivationFunctionType
AX_X = mybir.AxisListType.X


class Scope:

    def __init__(self, nc, ctx, stage):
        self.nc, self.ctx, self.stage = nc, ctx, stage
        self.sems = []
        ctx.callback(self.release)

    def release(self):
        if self.sems:
            self.nc.clear_and_free_semaphores(self.sems)
            self.nc.all_engine_barrier()

    def sb(self, name, shape, dt=F32):
        return self.ctx.enter_context(self.nc.sbuf_tensor(f"{self.stage}_{name}", shape, dt))

    def ps(self, name, shape, dt=F32):
        return self.ctx.enter_context(self.nc.psum_tensor(f"{self.stage}_{name}", shape, dt))

    def sem(self, name):
        self.sems.append(self.nc.alloc_semaphore(name=f"{self.stage}_{name}"))
        return self.sems[-1]


CONSTANTS = ("ident", "cols", "iota8")


def stats_buffers(s, T):
    return dict(
        raw=s.sb("ln_raw", [P, T, 6]), tmp=s.sb("ln_tmp", [P, 4, T]), mean=s.sb("ln_mean", [P, T]),
        var=s.sb("ln_var", [P, T]), std=s.sb("ln_std", [P, T]), rstd=s.sb("ln_rstd", [P, T]),
        raw_done=s.sem("ln_raw_done"), step=s.sem("ln_step"), var_done=s.sem("ln_var_done"),
        std_done=s.sem("ln_std_done"), rstd_done=s.sem("ln_rstd_done"))


def dve_stats(dve, x, T, ln, arrived=None):
    if arrived:
        share = T // len(arrived)
        for t in range(T):
            if t % share == 0:
                dve.wait_ge(arrived[t // share], 16)
            dve.bn_stats(ln["raw"][:, t, :], x[:, t, :]).then_inc(ln["raw_done"], 1)
    else:
        unroll = 8
        with dve.Fori(0, T // unroll) as i:
            for k in range(unroll):
                dve.bn_stats(ln["raw"][:, i * unroll + k, :], x[:, i * unroll + k, :]).then_inc(ln["raw_done"], 1)
    raw, tmp, step = ln["raw"], ln["tmp"], ln["step"]
    mean_sum, mean_diff, dev_sum, diff_sq = (tmp[:, k, :] for k in range(4))
    dve.wait_ge(ln["raw_done"], T)
    dve.tensor_tensor(mean_sum, raw[:, :, 1], raw[:, :, 4], ALU.add).then_inc(step, 1)
    dve.tensor_tensor(mean_diff, raw[:, :, 1], raw[:, :, 4], ALU.subtract).then_inc(step, 1)
    dve.tensor_tensor(dev_sum, raw[:, :, 2], raw[:, :, 5], ALU.add).then_inc(step, 1)
    dve.wait_ge(step, 3)
    dve.tensor_scalar(ln["mean"][:, :], mean_sum, 0.5, None, ALU.mult).then_inc(step, 1)
    dve.scalar_tensor_tensor(out=diff_sq, in0=mean_diff, scalar=0.25, in1=mean_diff,
                             op0=ALU.mult, op1=ALU.mult).then_inc(step, 1)
    dve.wait_ge(step, 5)
    dve.scalar_tensor_tensor(out=ln["var"][:, :], in0=dev_sum, scalar=1.0 / D, in1=diff_sq,
                             op0=ALU.mult, op1=ALU.add).then_inc(ln["var_done"], 1)
    dve.wait_ge(ln["std_done"], 1)
    dve.reciprocal(ln["rstd"][:, :], ln["std"][:, :]).then_inc(ln["rstd_done"], 1)
    dve.wait_ge(ln["rstd_done"], 1)


def act_std(act, ln, eps_col):
    act.wait_ge(ln["var_done"], 1)
    act.activation(ln["std"][:, :], ln["var"][:, :], ACT.Sqrt, bias=eps_col).then_inc(ln["std_done"], 1)


def dve_normalise(dve, out, x, ln, t):
    return dve.tensor_scalar(out, x[:, t, :], ln["mean"][:, bass.ds(t, 1)], ln["rstd"][:, bass.ds(t, 1)],
                             ALU.subtract, ALU.mult)


def load_x(sp, core, x_dram, x_in, const_dram, const_in):
    T = core["T"]
    share = T // len(x_in)
    xv = x_dram.rearrange("(t p) d -> p t d", p=P)
    for q, arrived in enumerate(x_in):
        sp.dma_start(core["x"][:, q * share:(q + 1) * share, :], xv[:, q * share:(q + 1) * share, :]).then_inc(arrived, 16)
        if q == 0:
            for name in CONSTANTS:
                sp.dma_start(core[name][:, :], const_dram[name]).then_inc(const_in, 16)


def stage_norm(nc, core, stage, x1, x2, router, weights, load=None):
    T, x = core["T"], core["x"]
    RING = 4
    G = T // RING
    with ExitStack() as ctx:
        s = Scope(nc, ctx, stage)
        ln = stats_buffers(s, T)
        xn = s.sb("xn", [P, RING, D])
        tr = [s.ps(f"tr{k}", [P, DC, P]) for k in range(RING)]
        xn_ready, tr_done = s.sem("xn_ready"), s.sem("tr_done")
        x1_done, x2_done = s.sem("x1_done"), s.sem("x2_done")
        if router:
            E = router["E"]
            rw = s.sb("rw", [P, DC, E])
            rb = s.sb("rb", [P, E])
            rw1, rw2 = s.sb("rw1", [P, DC, E], F32R), s.sb("rw2", [P, DC, E], F32R)
            lgT = s.sb("lgT", [E, RING * P])
            lg = s.sb("lg", [P, T, E])
            top = s.sb("top", [P, T, 8])
            top_at = s.sb("top_at", [P, T, 8], U32)
            at_f = s.sb("at_f", [P, T, 2])
            gap = s.sb("gap", [P, T])
            ex = s.sb("ex", [P, T])
            den = s.sb("den", [P, T])
            wt = s.sb("wt", [P, 3, T])
            pick = s.sb("pick", [P, 2, T, E])
            lgTp = s.ps("lgTp", [E, RING * P])
            lgp = s.ps("lgp", [P, T, E])
            rw_in, rw_split, router_done = s.sem("rw_in"), s.sem("rw_split"), s.sem("router_done")
            lgT_done, turned = s.sem("lgT_done"), s.sem("turned")
            lg_done, top_done, at_done = s.sem("lg_done"), s.sem("top_done"), s.sem("at_done")
            gap_done, ex_done, wstep = s.sem("gap_done"), s.sem("ex_done"), s.sem("wstep")
        x_in = [s.sem(f"x_in{q}") for q in range(4)] if load else None
        const_in = s.sem("const_in")
        weights_in, part1_done = [s.sem(f"weights_in{n}") for n in range(len(weights))], s.sem("part1_done")
        block = ctx.enter_context(nc.Block())

        @block.sync
        def _(sp):
            if load:
                load_x(sp, core, load[0], x_in, load[1], const_in)
            if router:
                sp.dma_start(rw[:, :, :], router["w"]).then_inc(rw_in, 16)
                sp.dma_start(rb[:, :], router["b"]).then_inc(rw_in, 16)
            for n, (dst, src, _, _) in enumerate(weights):
                sp.dma_start(dst[:, :], src).then_inc(weights_in[n], 16)

        @block.gpsimd
        def _(pool):
            for n, (raw, _, part1, part2) in enumerate(weights):
                pool.wait_ge(weights_in[n], 16)
                pool.tensor_copy(part1[:, :], raw[:, :]).then_inc(part1_done, 1)
                pool.wait_ge(part1_done, n + 1)
                pool.tensor_tensor(part2[:, :], raw[:, :], part1[:, :].bitcast(F32), ALU.subtract)

        def tiles(eng, step):
            for k in range(RING):
                step(0, k, "first")
            with eng.Fori(0, G - 2) as i:
                for k in range(RING):
                    step(i + 1, k, "inside")
            for k in range(RING):
                step(G - 1, k, "last")

        @block.vector
        def _(dve):
            dve_stats(dve, x, T, ln, x_in)
            if load:
                dve.wait_ge(const_in, 16 * len(CONSTANTS))
            for k in range(RING):
                dve_normalise(dve, xn[:, k, :], x, ln, k).then_inc(xn_ready, 1)

            def step(n, k, position):
                t = n * RING + k
                dve.wait_ge(x1_done, t + 1)
                dve.tensor_tensor(x2[:, :, bass.ts(t, P)], tr[k][:, :, :],
                                  x1[:, :, bass.ts(t, P)].bitcast(F32), ALU.subtract).then_inc(x2_done, 1)
                if position != "last":
                    dve_normalise(dve, xn[:, k, :], x, ln, t + RING).then_inc(xn_ready, 1)

            if router:
                dve.wait_ge(rw_in, 32)
                dve.tensor_copy(rw1[:, :, :], rw[:, :, :]).then_inc(rw_split, 1)
                dve.wait_ge(rw_split, 1)
                dve.tensor_tensor(rw2[:, :, :], rw[:, :, :], rw1[:, :, :].bitcast(F32), ALU.subtract).then_inc(rw_split, 1)
            tiles(dve, step)
            if not router:
                return
            dve.wait_ge(turned, G)
            dve.tensor_tensor(lg[:, :, :], lgp[:, :, :], rb[:, :].unsqueeze(1).broadcast_to([P, T, E]),
                              ALU.add).then_inc(lg_done, 1)
            dve.wait_ge(lg_done, 1)
            for t in range(T):
                dve.max(top[:, t, :], lg[:, t, :]).then_inc(top_done, 1)
            dve.wait_ge(top_done, T)
            for t in range(T):
                dve.max_index(top_at[:, t, :], top[:, t, :], lg[:, t, :]).then_inc(at_done, 1)
            dve.tensor_tensor(gap[:, :], top[:, :, 1], top[:, :, 0], ALU.subtract).then_inc(gap_done, 1)
            dve.wait_ge(at_done, T)
            dve.tensor_copy(at_f[:, :, :], top_at[:, :, 0:2]).then_inc(wstep, 1)
            dve.wait_ge(ex_done, 1)
            dve.tensor_scalar(den[:, :], ex[:, :], 1.0, None, ALU.add).then_inc(wstep, 1)
            dve.wait_ge(wstep, 2)
            dve.reciprocal(wt[:, 2, :], den[:, :]).then_inc(wstep, 1)
            dve.wait_ge(wstep, 3)
            dve.tensor_scalar(wt[:, 0, :], wt[:, 2, :], 0.5, None, ALU.mult).then_inc(wstep, 1)
            dve.wait_ge(wstep, 4)
            dve.tensor_tensor(wt[:, 1, :], ex[:, :], wt[:, 0, :], ALU.mult).then_inc(wstep, 1)
            for k in range(2):
                dve.tensor_tensor(pick[:, k, :, :], core["iota8"][:, :].unsqueeze(1).broadcast_to([P, T, E]),
                                  at_f[:, :, k:k + 1].broadcast_to([P, T, E]), ALU.is_equal).then_inc(wstep, 1)
            dve.wait_ge(wstep, 7)
            for k in range(2):
                dve.tensor_tensor(pick[:, k, :, :], pick[:, k, :, :],
                                  wt[:, k, :].unsqueeze(2).broadcast_to([P, T, E]), ALU.mult).then_inc(wstep, 1)
            dve.wait_ge(wstep, 9)
            dve.tensor_tensor(core["comb"][:, :, 0:E], pick[:, 0, :, :], pick[:, 1, :, :],
                              ALU.add).then_inc(wstep, 1)
            dve.memset(core["comb"][:, :, E:E + 1], 0.5).then_inc(wstep, 1)

        @block.scalar
        def _(act):
            if load:
                act.wait_ge(const_in, 16 * len(CONSTANTS))
            act_std(act, ln, core["cols"][:, 0:1])

            def logits_out(n):
                act.wait_ge(router_done, n + 1)
                wait_if(act, turned, n)
                act.activation(lgT[:, :], lgTp[:, :], ACT.Copy).then_inc(lgT_done, 1)

            def step(n, k, position):
                t = n * RING + k
                act.wait_ge(tr_done, t + 1)
                act.activation(x1[:, :, bass.ts(t, P)], tr[k][:, :, :], ACT.Copy).then_inc(x1_done, 1)
                if router and position != "first" and k == RING - 1:
                    logits_out(n - 1)

            tiles(act, step)
            if router:
                logits_out(G - 1)
            if router:
                act.wait_ge(gap_done, 1)
                act.activation(ex[:, :], gap[:, :], ACT.Exp).then_inc(ex_done, 1)

        @block.tensor
        def _(pe):
            def transposes(t, k):
                pe.wait_ge(xn_ready, t + 1)
                for c in range(DC):
                    mm = pe.transpose(tr[k][:, c, :], xn[:, k, c * P:(c + 1) * P], core["ident"][:, :])
                mm.then_inc(tr_done, 1)

            def logits(n):
                wait_if(pe, lgT_done, n)
                for j, (w, v) in enumerate(((rw1, x1), (rw1, x2), (rw2, x1))):
                    for c in range(DC):
                        mm = pe.matmul(lgTp[:, :], w[:, c, :], v[:, c, bass.ts(n, RING * P)],
                                       start=(j == 0 and c == 0), stop=(j == 2 and c == DC - 1))
                mm.then_inc(router_done, 1)

            def turn(n):
                for j in range(RING):
                    mm = pe.matmul(lgp[:, n * RING + j, :], lgT[:, j * P:(j + 1) * P], core["ident"][0:E, 0:E], start=True, stop=True)
                mm.then_inc(turned, 1)

            if load:
                pe.wait_ge(const_in, 16 * len(CONSTANTS))
            for k in range(RING):
                transposes(k, k)
            if router:
                pe.wait_ge(rw_split, 2)

            def step(n, k, position):
                t = n * RING + k
                pe.wait_ge(x2_done, t + 1)
                if position != "last":
                    transposes(t + RING, k)
                if router and k == RING - 1:
                    logits(n)
                    if position != "first":
                        turn(n - 1)

            tiles(pe, step)
            if router:
                pe.wait_ge(lgT_done, G)
                turn(G - 1)


def stage_experts(nc, core, stage, x1, x2, first_up, first_dn, up_dram, dn_dram, NE):
    T, x, comb = core["T"], core["x"], core["comb"]
    F = up_dram.shape[2] // DC
    FT = F // P
    TT = 4
    G = T // TT
    N = TT * P
    with ExitStack() as ctx:
        s = Scope(nc, ctx, stage)
        (raw_up, _, up1, up2), (raw_dn, _, dn1, dn2) = first_up, first_dn
        h = s.sb("h", [P, FT, N])
        h1, h2 = s.sb("h1", [P, FT, N], F32R), s.sb("h2", [P, FT, N], F32R)
        hp = [s.ps(f"hp{f}", [P, N]) for f in range(FT)]
        yp = [s.ps(f"yp{t}", [P, D]) for t in range(TT)]
        up_in, dn_in = s.sem("up_in"), s.sem("dn_in")
        up1_done, up_split, dn1_done, dn_split = (s.sem(n) for n in ("up1_done", "up_split", "dn1_done", "dn_split"))
        ups_done, hp_ready, act_done, h_split = (s.sem(n) for n in ("ups_done", "hp_ready", "act_done", "h_split"))
        h_used, yp_ready, y_added = s.sem("h_used"), s.sem("yp_ready"), s.sem("y_added")
        block = ctx.enter_context(nc.Block())
        up_parts = ((up1, x1), (up1, x2), (up2, x1))

        @block.sync
        def _(sp):
            with sp.Fori(0, NE - 1) as e:
                sp.wait_ge(up_split, e + 2)
                sp.dma_start(raw_up[:, :], up_dram[e + 1, :, :]).then_inc(up_in, 16)
                sp.wait_ge(dn_split, e + 2)
                sp.dma_start(raw_dn[:, :], dn_dram[e + 1, :, :]).then_inc(dn_in, 16)

        @block.tensor
        def _(pe):
            with pe.Fori(0, NE) as e:
                with pe.Fori(0, G) as g:
                    n = e * G + g
                    pe.wait_ge(up_split, e + 2)
                    for f in range(FT):
                        pe.wait_ge(act_done, n * FT + f + 1)
                        k = 0
                        for w, v in up_parts:
                            for c in range(DC):
                                mm = pe.matmul(hp[f][:, :], w[:, c * F + f * P:c * F + (f + 1) * P],
                                               v[:, c, bass.ts(g, N)], start=(k == 0), stop=(k == 5))
                                k += 1
                        mm.then_inc(hp_ready, 1)
                    pe.sem_inc(ups_done, 1)
                    pe.wait_ge(dn_split, e + 2)
                    for f in range(FT):
                        pe.wait_ge(h_split, n * FT + f + 1 + FT)
                        for t in range(TT):
                            if f == 0:
                                pe.wait_ge(y_added, n * TT + t + 1 + T - TT)
                            for k, (a, b) in enumerate(((h1, dn1), (h1, dn2), (h2, dn1))):
                                mm = pe.matmul(yp[t][:, :], a[:, f, t * P:(t + 1) * P], b[:, f * D:(f + 1) * D],
                                               start=(f == 0 and k == 0), stop=(f == FT - 1 and k == 2))
                            if f == FT - 1:
                                mm.then_inc(yp_ready, 1)
                        if f < FT - 1:
                            mm.then_inc(h_used, 1)
                        else:
                            pe.sem_inc(h_used, 1)

        @block.scalar
        def _(act):
            act.sem_inc(act_done, FT)
            with act.Fori(0, NE) as e:
                with act.Fori(0, G) as g:
                    n = e * G + g
                    for f in range(FT):
                        act.wait_ge(hp_ready, n * FT + f + 1)
                        act.wait_ge(h_split, n * FT + f + 1)
                        act.activation(h[:, f, :], hp[f][:, :], ACT.Silu)
                        act.wait_ge(h_used, n * FT + f + 1)
                        act.activation(h1[:, f, :], hp[f][:, :], ACT.Silu).then_inc(act_done, 1)

        @block.vector
        def _(dve):
            dve.sem_inc(up_split, 2)
            dve.sem_inc(dn_split, 2)
            dve.sem_inc(h_split, FT)
            dve.sem_inc(h_used, FT)
            dve.sem_inc(y_added, T)

            def split_up(e):
                dve.wait_ge(up_in, e * 16)
                dve.tensor_copy(up1[:, :], raw_up[:, :]).then_inc(up1_done, 1)
                dve.wait_ge(up1_done, e)
                dve.tensor_tensor(up2[:, :], raw_up[:, :], up1[:, :].bitcast(F32), ALU.subtract).then_inc(up_split, 1)

            def split_dn(e):
                dve.wait_ge(dn_in, e * 16)
                dve.tensor_copy(dn1[:, :], raw_dn[:, :]).then_inc(dn1_done, 1)
                dve.wait_ge(dn1_done, e)
                dve.tensor_tensor(dn2[:, :], raw_dn[:, :], dn1[:, :].bitcast(F32), ALU.subtract).then_inc(dn_split, 1)

            def group(e, g, last_of_expert):
                n = e * G + g
                for f in range(FT):
                    dve.wait_ge(act_done, n * FT + f + 1 + FT)
                    dve.wait_ge(h_used, n * FT + f + 1)
                    dve.tensor_tensor(h2[:, f, :], h[:, f, :], h1[:, f, :].bitcast(F32),
                                      ALU.subtract).then_inc(h_split, 1)
                if last_of_expert:
                    dve.wait_ge(ups_done, n + 1)
                    split_up(e + 1)
                for t in range(TT):
                    dve.wait_ge(yp_ready, n * TT + t + 1)
                    dve.wait_ge(y_added, n * TT + t + 1)
                    tile = g * TT + t
                    dve.scalar_tensor_tensor(out=x[:, tile, :], in0=yp[t][:, :],
                                             scalar=comb[:, tile, bass.ds(e, 1)], in1=x[:, tile, :],
                                             op0=ALU.mult, op1=ALU.add).then_inc(y_added, 1)
                if last_of_expert:
                    dve.wait_ge(h_used, n * FT + FT + FT)
                    split_dn(e + 1)

            with dve.Fori(0, NE - 1) as e:
                with dve.Fori(0, G - 1) as g:
                    group(e, g, False)
                group(e, G - 1, True)
            with dve.Fori(0, G) as g:
                group(NE - 1, g, False)


def stage_spikes(nc, core, stage, x1, x2, fc, pj, out_dram=None):
    T, x = core["T"], core["x"]
    STEPS, BETA, THRESHOLD = 5, 0.9, 1.0
    F = fc[0].shape[1] // DC
    FT = F // P
    HT = 4
    TT = 4
    G = T // TT
    N = TT * P
    L = 2 + 3 * (STEPS - 1)
    with ExitStack() as ctx:
        s = Scope(nc, ctx, stage)
        (fc1, fc2), (pj1, pj2) = fc[2:], pj[2:]
        r = s.sb("r", [P, 2, N])
        h = s.sb("h", [P, HT, N])
        h1, h2 = s.sb("h1", [P, HT, N], F32R), s.sb("h2", [P, HT, N], F32R)
        y, mem, leak, spk = s.sb("y", [P, TT, D]), s.sb("mem", [P, TT, D]), s.sb("leak", [P, TT, D]), s.sb("spk", [P, TT, D])
        hp = [s.ps(f"hp{f}", [P, N]) for f in range(HT)]
        yp = s.ps("yp", [P, TT, N])
        hp_ready, relu_done, act_done, h_split = (s.sem(n) for n in ("hp_ready", "relu_done", "act_done", "h_split"))
        h_used, yp_ready, y_ready, y_free, neuron = (s.sem(n) for n in ("h_used", "yp_ready", "y_ready", "y_free", "neuron"))
        stored = s.sem("stored")
        block = ctx.enter_context(nc.Block())

        if out_dram is not None:
            @block.sync
            def _(sp):
                ov = out_dram.rearrange("(t p) d -> p t d", p=P)
                with sp.Fori(0, G) as g:
                    sp.wait_ge(neuron, g * L + L)
                    sp.dma_start(ov[:, bass.ts(g, TT), :], x[:, bass.ts(g, TT), :]).then_inc(stored, 16)
                sp.wait_ge(stored, 16 * G)

        @block.tensor
        def _(pe):
            with pe.Fori(0, G) as g:
                for half in range(FT // HT):
                    for f in range(HT):
                        n = g * FT + half * HT + f
                        pe.wait_ge(act_done, n + 1)
                        k = 0
                        for w, v in ((fc1, x1), (fc1, x2), (fc2, x1)):
                            for c in range(DC):
                                at = c * F + (half * HT + f) * P
                                mm = pe.matmul(hp[f][:, :], w[:, at:at + P], v[:, c, bass.ts(g, N)],
                                               start=(k == 0), stop=(k == 5))
                                k += 1
                        mm.then_inc(hp_ready, 1)
                    for f in range(HT):
                        pe.wait_ge(h_split, g * FT + half * HT + f + 1 + HT)
                        if half == 0 and f == 0:
                            pe.wait_ge(y_ready, g + 1)
                        at = (half * HT + f) * D
                        for t in range(TT):
                            for k, (a, b) in enumerate(((h1, pj1), (h1, pj2), (h2, pj1))):
                                mm = pe.matmul(yp[:, t, 0:D], a[:, f, t * P:(t + 1) * P], b[:, at:at + D],
                                               start=(half == 0 and f == 0 and k == 0),
                                               stop=(half == 1 and f == HT - 1 and k == 2))
                        mm.then_inc(h_used, 1)

        @block.scalar
        def _(act):
            act.sem_inc(act_done, HT)
            act.sem_inc(relu_done, 2)
            act.sem_inc(y_ready, 1)

            def copy_y(g):
                act.wait_ge(h_used, g * FT + FT + HT)
                act.wait_ge(y_free, g + 1)
                act.activation(y[:, :, :], yp[:, :, 0:D], ACT.Copy).then_inc(y_ready, 1)

            def half_of(g, half):
                for f in range(HT):
                    n = g * FT + half * HT + f
                    act.wait_ge(hp_ready, n + 1)
                    act.wait_ge(act_done, n + HT - 1)
                    act.activation(r[:, f % 2, :], hp[f][:, :], ACT.Relu).then_inc(relu_done, 1)
                    act.wait_ge(relu_done, n + 3)
                    act.wait_ge(h_split, n + 1)
                    act.activation(h[:, f, :], r[:, f % 2, :], ACT.Square)
                    act.wait_ge(h_used, n + 1)
                    act.activation(h1[:, f, :], r[:, f % 2, :], ACT.Square).then_inc(act_done, 1)

            half_of(0, 0)
            half_of(0, 1)
            with act.Fori(0, G - 1) as i:
                copy_y(i)
                half_of(i + 1, 0)
                half_of(i + 1, 1)
            copy_y(G - 1)

        @block.gpsimd
        def _(pool):
            with pool.Fori(0, G) as g:
                for f in range(FT):
                    n = g * FT + f
                    pool.wait_ge(act_done, n + (1 + HT))
                    pool.wait_ge(h_used, n + 1)
                    pool.tensor_tensor(h2[:, f % HT, :], h[:, f % HT, :], h1[:, f % HT, :].bitcast(F32),
                                       ALU.subtract).then_inc(h_split, 1)

        @block.vector
        def _(dve):
            dve.sem_inc(h_split, HT)
            dve.sem_inc(h_used, HT)
            dve.sem_inc(y_free, 1)
            def first(g):
                dve.wait_ge(y_ready, g + 2)
                return dve.tensor_scalar(spk[:, :, :], y[:, :, :], THRESHOLD, None, ALU.is_gt)

            def decay(src):
                return lambda g: dve.scalar_tensor_tensor(out=leak[:, :, :], in0=src[:, :, :], scalar=BETA,
                                                          in1=y[:, :, :], op0=ALU.mult, op1=ALU.add)

            def reset(src):
                return lambda g: dve.scalar_tensor_tensor(out=mem[:, :, :], in0=src[:, :, :], scalar=THRESHOLD,
                                                          in1=leak[:, :, :], op0=ALU.is_gt, op1=ALU.subtract,
                                                          reverse1=True)

            def count(g):
                return dve.scalar_tensor_tensor(out=spk[:, :, :], in0=mem[:, :, :], scalar=THRESHOLD,
                                                in1=spk[:, :, :], op0=ALU.is_gt, op1=ALU.add)

            def add_to_x(g):
                xg = x[:, bass.ts(g, TT), :]
                return dve.scalar_tensor_tensor(out=xg, in0=spk[:, :, :], scalar=0.5 / STEPS, in1=xg,
                                                op0=ALU.mult, op1=ALU.add)

            chain = [first]
            for k in range(1, STEPS):
                chain += [decay(y if k == 1 else mem), reset(y if k == 1 else mem), count]
            chain.append(add_to_x)

            def neuron_steps(g, todo):
                for k in todo:
                    if k:
                        dve.wait_ge(neuron, g * L + k)
                    chain[k](g).then_inc(neuron, 1)
                if L - 1 in todo:
                    dve.wait_ge(neuron, g * L + L)
                    dve.sem_inc(y_free, 1)

            with dve.Fori(0, G) as i:
                neuron_steps(i, range(L))


def wait_if(eng, sem, value):
    if not isinstance(value, int) or value > 0:
        eng.wait_ge(sem, value)


def stage_linear_attention(nc, core, stage, ins):
    T, x = core["T"], core["x"]
    H, DV, DF = 8, 32, 64
    NP = H // 2
    SCALE = DF ** -0.5
    with ExitStack() as ctx:
        s = Scope(nc, ctx, stage)
        ln = stats_buffers(s, T)
        w_nat = [s.sb(f"w{n}_nat", [P, DC, D]) for n in "qk"]
        blocks = [s.sb(f"fm{n}", [P, P]) for n in "qk"]
        b_raw = [s.sb(f"b{n}_raw", [P, 1]) for n in "qk"]
        b_col = [s.sb(f"b{n}", [P, 1]) for n in "qk"]
        w_feat = [s.sb(f"w{n}_feat", [P, DC, H, 2, 32]) for n in "qk"]
        wv, wo_raw, wo, rms = s.sb("wv", [P, DC, D]), s.sb("wo_raw", [P, DC, D]), s.sb("wo", [P, DC, D]), s.sb("rms", [P, 1])
        keep = s.sb("keep", [P, P])
        xn, xT = s.sb("xn", [P, 2, D]), s.sb("xT", [P, 2, DC, P])
        qf, kf, kt = s.sb("qf", [P, 2, NP, P]), s.sb("kf", [P, 2, NP, P]), s.sb("kt", [P, 2, NP, P])
        v = s.sb("v", [P, 2, D])
        am = s.sb("am", [P, 2, H, P])
        S = s.sb("S", [P, NP, 2 * DV])
        o, sq, on, oT = s.sb("o", [P, 2, D]), s.sb("sq", [P, 2, D]), s.sb("on", [P, 2, D]), s.sb("oT", [P, DC, P])
        ss, ms, rs = s.sb("ss", [P, 2, H]), s.sb("ms", [P, 2, H]), s.sb("rs", [P, 2, H])
        half_neg = s.sb("half_neg", [P, H])
        bank0, bank4 = s.ps("bank0", [P, 512]), s.ps("bank4", [P, 512])
        trp, vp = bank0[:, 0:D].rearrange("p (c q) -> p c q", c=DC), bank0[:, D:2 * D]
        qp, kp = s.ps("qp", [P, NP, P]), s.ps("kp", [P, NP, P])
        ktp = s.ps("ktp", [P, NP, P])
        sp_new = ktp[:, 0:2, :].rearrange("p a q -> p (a q)")
        ap = [s.ps(f"ap{k}", [P, 4, P]) for k in range(2)]
        op = s.ps("op", [P, D])
        oTp, yp = bank4[:, 0:D].rearrange("p (c q) -> p c q", c=DC), bank4[:, D:2 * D]
        w_in, fm_in, zeroed, prep, half_set = (s.sem(n) for n in ("w_in", "fm_in", "zeroed", "prep", "half_set"))
        wf_ready, wf_done = s.sem("wf_ready"), s.sem("wf_done")
        names = ("xn_ready", "tr_done", "xT_done", "q_ready", "k_ready", "v_ready", "q_done", "k_done", "v_done",
                 "kt_ready", "kt_done", "a_ready", "masked", "o_ready", "o_done", "sq_done", "S_done", "ss_done",
                 "ms_done", "rs_done", "on_done", "oT_ready", "oT_done", "y_ready", "x_done")
        m = {n: s.sem(n) for n in names}
        block = ctx.enter_context(nc.Block())

        def chunks(eng, step):
            for t in range(2):
                step(t, t, True, True)
            with eng.Fori(0, (T - 4) // 2) as i:
                for k in range(2):
                    step(i * 2 + (2 + k), k, True, True)
            step(T - 2, 0, True, False)
            step(T - 1, 1, False, False)

        @block.sync
        def _(sp):
            for dst, src in ((w_nat[0], ins["lwq"]), (w_nat[1], ins["lwk"]), (wv, ins["lwv"]), (wo_raw, ins["lwo"])):
                sp.dma_start(dst[:, :, :], src.rearrange("p (c n) -> p c n", c=DC)).then_inc(w_in, 16)
            for dst, src in ((b_raw[0], ins["lbq"]), (b_raw[1], ins["lbk"]), (rms, ins["lrms"]), (keep, ins["keep_kq"])):
                sp.dma_start(dst[:, :], src).then_inc(w_in, 16)
            sp.wait_ge(zeroed, 2)
            for n, src in enumerate((ins["lfq"], ins["lfk"])):
                for j in range(4):
                    sp.dma_start(blocks[n][32 * j:32 * j + 32, 32 * j:32 * j + 32], src).then_inc(fm_in, 16)
            sp.wait_ge(w_in, 16 * 8)
            sp.wait_ge(fm_in, 16 * 2 * 4)

        @block.gpsimd
        def _(pool):
            pool.memset(half_neg[:, :], -0.5).then_inc(half_set, 1)
            pool.wait_ge(half_set, 1)

            def step(t, k, *_):
                pool.wait_ge(m["ms_done"], t + 1)
                wait_if(pool, m["on_done"], t - 1)
                pool.tensor_tensor(rs[:, k, :], ms[:, k, :], half_neg[:, :], ALU.pow).then_inc(m["rs_done"], 1)

            chunks(pool, step)

        @block.tensor
        def _(pe):
            pe.wait_ge(w_in, 16 * 8)
            pe.wait_ge(fm_in, 16 * 2 * 4)
            for n, dst in enumerate((qp, kp)):
                for c in range(DC):
                    for j in range(DC):
                        mm = pe.matmul(dst[:, c * DC + j, :], w_nat[n][:, j, c * P:(c + 1) * P], blocks[n][:, :],
                                       start=True, stop=True)
                mm.then_inc(wf_ready, 1)
            pe.wait_ge(wf_done, 4)

            def x_transposes(t, k):
                pe.wait_ge(m["xn_ready"], t + 1)
                wait_if(pe, m["v_done"], t)
                for c in range(DC):
                    mm = pe.transpose(trp[:, c, :], xn[:, k, c * P:(c + 1) * P], core["ident"][:, :])
                mm.then_inc(m["tr_done"], 1)

            def qk(t, k):
                pe.wait_ge(m["xT_done"], t + 1)
                for n, (dst, read, ready) in enumerate(((qp, "q_done", "q_ready"), (kp, "k_done", "k_ready"))):
                    wait_if(pe, m[read], t)
                    wf = w_feat[n][:, :, :, :, :].rearrange("p c h s e -> p c (h s e)")
                    for f in range(NP):
                        for c in range(DC):
                            mm = pe.matmul(dst[:, f, :], wf[:, c, f * P:(f + 1) * P], xT[:, k, c, :],
                                           start=(c == 0), stop=(c == DC - 1))
                    mm.then_inc(m[ready], 1)

            def values(t, k):
                for c in range(DC):
                    mm = pe.matmul(vp, xT[:, k, c, :], wv[:, c, :], start=(c == 0), stop=(c == DC - 1))
                mm.then_inc(m["v_ready"], 1)

            def k_transposes(t, k):
                pe.wait_ge(m["k_done"], t + 1)
                pe.wait_ge(m["S_done"], t * 2 + 2)
                for f in range(NP):
                    mm = pe.transpose(ktp[:, f, :], kf[:, k, f, :], core["ident"][:, :])
                mm.then_inc(m["kt_ready"], 1)

            def inside(t, k):
                pe.wait_ge(m["q_done"], t + 1)
                pe.wait_ge(m["k_done"], t + 1)
                wait_if(pe, m["masked"], t * 2)
                for f in range(NP):
                    for odd in range(2):
                        r = slice(DF * odd, DF * odd + DF)
                        mm = pe.matmul(ap[odd][:, f, :], kf[r, k, f, :], qf[r, k, f, :], start=True, stop=True)
                        if f == NP - 1:
                            mm.then_inc(m["a_ready"], 1)

            def outputs(t, k):
                pe.wait_ge(m["masked"], t * 2 + 2)
                pe.wait_ge(m["v_done"], t + 1)
                pe.wait_ge(m["kt_done"], t + 1)
                pe.wait_ge(m["S_done"], t * 2 + 2)
                wait_if(pe, m["sq_done"], t)
                for f in range(NP):
                    pe.matmul(op[:, f * 64:(f + 1) * 64], qf[:, k, f, :], S[:, f, :], start=True, stop=True)
                    for j in range(2):
                        h = 2 * f + j
                        pe.matmul(op[:, h * DV:(h + 1) * DV], am[:, k, j * NP + f, :], v[:, k, h * DV:(h + 1) * DV],
                                  start=False, stop=True, skip_group_check=True)
                for f in range(NP):
                    mm = pe.matmul(sp_new[:, f * 64:(f + 1) * 64], kt[:, k, f, :], v[:, k, f * 64:(f + 1) * 64],
                                   start=True, stop=True)
                mm.then_inc(m["o_ready"], 1)

            def o_transposes(t, k):
                pe.wait_ge(m["on_done"], t + 1)
                wait_if(pe, m["x_done"], t)
                for c in range(DC):
                    mm = pe.transpose(oTp[:, c, :], on[:, k, c * P:(c + 1) * P], core["ident"][:, :])
                mm.then_inc(m["oT_ready"], 1)

            def project(t):
                pe.wait_ge(m["oT_done"], t + 1)
                for c in range(DC):
                    mm = pe.matmul(yp, oT[:, c, :], wo[:, c, :], start=(c == 0), stop=(c == DC - 1))
                mm.then_inc(m["y_ready"], 1)

            x_transposes(0, 0)
            qk(0, 0)
            values(0, 0)
            k_transposes(0, 0)

            def step(t, k, has_next, _):
                if has_next:
                    x_transposes(t + 1, 1 - k)
                inside(t, k)
                if has_next:
                    qk(t + 1, 1 - k)
                first = isinstance(t, int) and t == 0
                if not first:
                    o_transposes(t - 1, 1 - k)
                if has_next:
                    values(t + 1, 1 - k)
                outputs(t, k)
                if not first:
                    project(t - 1)
                if has_next:
                    k_transposes(t + 1, 1 - k)

            chunks(pe, step)
            o_transposes(T - 1, 1)
            project(T - 1)

        @block.scalar
        def _(act):
            act_std(act, ln, core["cols"][:, 0:1])
            for n, src in enumerate((qp, kp)):
                act.wait_ge(wf_ready, n + 1)
                act.activation(w_feat[n][:, :, :, 0, :], src[:, :, :].rearrange("p (c j) (h e) -> p c (j h) e", c=DC, e=32),
                               ACT.Copy).then_inc(wf_done, 1)
                act.activation(w_feat[n][:, :, :, 1, :], src[:, :, :].rearrange("p (c j) (h e) -> p c (j h) e", c=DC, e=32),
                               ACT.Copy, scale=-1.0).then_inc(wf_done, 1)
            act.wait_ge(prep, 3)

            def front(t, k):
                act.wait_ge(m["tr_done"], t + 1)
                wait_if(act, m["v_ready"], t - 1)
                act.activation(xT[:, k, :, :], trp, ACT.Copy).then_inc(m["xT_done"], 1)
                wait_if(act, m["o_ready"], t - 1)
                act.wait_ge(m["q_ready"], t + 1)
                act.activation(qf[:, k, :, :], qp[:, :, :], ACT.Exp, bias=b_col[0][:, 0:1]).then_inc(m["q_done"], 1)
                act.wait_ge(m["k_ready"], t + 1)
                act.activation(kf[:, k, :, :], kp[:, :, :], ACT.Exp, bias=b_col[1][:, 0:1]).then_inc(m["k_done"], 1)

            def k_rows(t, k):
                act.wait_ge(m["kt_ready"], t + 1)
                act.activation(kt[:, k, :, :], ktp[:, :, :], ACT.Copy).then_inc(m["kt_done"], 1)

            def o_out(t, k):
                act.wait_ge(m["o_ready"], t + 1)
                wait_if(act, m["on_done"], t - 1)
                act.activation(o[:, k, :], op[:, :], ACT.Copy, scale=SCALE).then_inc(m["o_done"], 1)
                act.activation(sq[:, k, :], op[:, :], ACT.Square, scale=SCALE).then_inc(m["sq_done"], 1)

            front(0, 0)
            k_rows(0, 0)

            def step(t, k, has_next, _):
                if has_next:
                    front(t + 1, 1 - k)
                o_out(t, k)
                if has_next:
                    k_rows(t + 1, 1 - k)

            chunks(act, step)

        @block.vector
        def _(dve):
            for n in range(2):
                dve.memset(blocks[n][:, :], 0.0).then_inc(zeroed, 1)
            dve.memset(S[:, :, :], 0.0).then_inc(m["S_done"], 1)
            dve.sem_inc(m["S_done"], 1)
            dve_stats(dve, x, T, ln)
            for k in range(2):
                dve_normalise(dve, xn[:, k, :], x, ln, k).then_inc(m["xn_ready"], 1)
            dve.wait_ge(w_in, 16 * 8)
            for n in range(2):
                dve.tensor_tensor(b_col[n][:, :], b_raw[n][:, :], core["cols"][:, 1:2], ALU.mult).then_inc(prep, 1)
            dve.tensor_scalar(wo[:, :, :], wo_raw[:, :, :], rms[:, 0:1], None, ALU.mult).then_inc(prep, 1)
            dve.wait_ge(m["S_done"], 2)

            def v_out(t, k):
                dve.wait_ge(m["v_ready"], t + 1)
                wait_if(dve, m["o_ready"], t - 1)
                dve.tensor_copy(v[:, k, :], vp).then_inc(m["v_done"], 1)

            def mask(t, k):
                wait_if(dve, m["o_ready"], t - 1)
                for half in range(2):
                    dve.wait_ge(m["a_ready"], t * 2 + half + 1)
                    dve.tensor_tensor(am[:, k, 4 * half:4 * half + 4, :], ap[half][:, :, :],
                                      keep[:, :].unsqueeze(1).broadcast_to([P, 4, P]), ALU.mult).then_inc(m["masked"], 1)

            def oT_out(t):
                dve.wait_ge(m["oT_ready"], t + 1)
                wait_if(dve, m["y_ready"], t)
                dve.tensor_copy(oT[:, :, :], oTp).then_inc(m["oT_done"], 1)

            def add_y(t):
                dve.wait_ge(m["y_ready"], t + 1)
                dve.tensor_tensor(x[:, t, :], yp, x[:, t, :], ALU.add).then_inc(m["x_done"], 1)

            def add_S(t):
                dve.wait_ge(m["o_ready"], t + 1)
                for j in range(2):
                    r, c = slice(DF * j, DF * j + DF), slice(DV * j, DV * j + DV)
                    new = sp_new.rearrange("p (f n) -> p f n", f=NP)
                    dve.tensor_tensor(S[r, :, c], new[r, :, c], S[r, :, c], ALU.add).then_inc(m["S_done"], 1)

            def norm_a(t, k):
                dve.wait_ge(m["sq_done"], t + 1)
                dve.reduce_sum(ss[:, k, :], sq[:, k, :].rearrange("p (h e) -> p h e", e=DV), AX_X).then_inc(m["ss_done"], 1)
                dve.wait_ge(m["ss_done"], t + 1)
                dve.tensor_scalar(ms[:, k, :], ss[:, k, :], 1.0 / DV, EPS, ALU.mult, ALU.add).then_inc(m["ms_done"], 1)

            def norm_b(t, k):
                dve.wait_ge(m["rs_done"], t + 1)
                dve.tensor_tensor(on[:, k, :].rearrange("p (h e) -> p h e", e=DV),
                                  o[:, k, :].rearrange("p (h e) -> p h e", e=DV),
                                  rs[:, k, :].unsqueeze(2).broadcast_to([P, H, DV]), ALU.mult).then_inc(m["on_done"], 1)

            v_out(0, 0)

            def step(t, k, has_next, has_two):
                first = isinstance(t, int) and t == 0
                mask(t, k)
                if has_two:
                    dve_normalise(dve, xn[:, k, :], x, ln, t + 2).then_inc(m["xn_ready"], 1)
                if not first:
                    oT_out(t - 1)
                if has_next:
                    v_out(t + 1, 1 - k)
                add_S(t)
                if not first:
                    add_y(t - 1)
                norm_a(t, k)
                norm_b(t, k)

            chunks(dve, step)
            oT_out(T - 1)
            add_y(T - 1)


def stage_softmax_attention(nc, core, stage, ins):
    T = core["T"]
    Tok = T * P
    H, HD = 16, 16
    qk_parts = nc.dram_tensor(f"{stage}_qk_parts", (2, 3, H * HD, Tok), BF16, kind="Internal").ap()
    raw_dram = nc.dram_tensor(f"{stage}_raw", (2, HD + 1, H, Tok), F32, kind="Internal").ap()
    with ExitStack() as ctx:
        s = Scope(nc, ctx, stage)
        v_ones = s.sb("v_ones", [P, T, H, HD + 1])
        softmax_project(nc, core, f"{stage}p", ins, qk_parts, v_ones, H, HD)
        softmax_heads(nc, core, f"{stage}h", ins, qk_parts, v_ones, raw_dram, H, HD)
    softmax_output(nc, core, f"{stage}o", ins, raw_dram, H, HD)


def softmax_project(nc, core, stage, ins, qk_parts, v_ones, H, HD):
    T, x = core["T"], core["x"]
    TT = 4
    G = T // TT
    N = TT * P
    with ExitStack() as ctx:
        s = Scope(nc, ctx, stage)
        ln = stats_buffers(s, T)
        w = s.sb("w", [P, DC, 3 * D])
        xn, xT = s.sb("xn", [P, 2, D]), s.sb("xT", [P, 2, DC, N])
        rest = s.sb("rest", [P, 2, N])
        parts = [s.sb(f"parts{j}", [P, 3, N], BF16) for j in range(4)]
        trp = [s.ps(f"trp{k}", [P, DC, P]) for k in range(2)]
        qp = [s.ps(f"qp{j}", [P, N]) for j in range(4)]
        vp = [s.ps(f"vp{k}", [P, H, HD]) for k in range(2)]
        w_in = s.sem("w_in")
        stored = [s.sem(f"stored{j}") for j in range(4)]
        names = ("ones_set", "xn_ready", "tr_done", "xT_done", "q_ready", "part1", "rest_done", "part2", "part3",
                 "v_ready", "v_done")
        m = {n: s.sem(n) for n in names}
        block = ctx.enter_context(nc.Block())
        columns = (0, P, 2 * D, 2 * D + P)

        def groups(eng, step):
            step(0, 0, "first")
            with eng.Fori(0, (G - 2) // 2) as i:
                step(i * 2 + 1, 1, "inside")
                step(i * 2 + 2, 0, "inside")
            step(G - 1, 1, "last")

        @block.sync
        def _(sp):
            sp.dma_start(w[:, :, :], ins["swqvk"].rearrange("p (c n) -> p c n", c=DC)).then_inc(w_in, 16)
            with sp.Fori(0, G) as g:
                for j in range(4):
                    sp.wait_ge(m["part3"], g * 4 + (j + 1))
                    dst = qk_parts[j // 2, :, (j % 2) * P:(j % 2 + 1) * P, bass.ts(g, N)]
                    sp.dma_start(dst.rearrange("a p n -> p a n"), parts[j][:, :, :]).then_inc(stored[j], 16)
            for j in range(4):
                sp.wait_ge(stored[j], 16 * G)

        @block.tensor
        def _(pe):
            pe.wait_ge(w_in, 16)

            def transposes(t, k):
                pe.wait_ge(m["xn_ready"], t + 1)
                wait_if(pe, m["xT_done"], t - 1)
                for c in range(DC):
                    mm = pe.transpose(trp[k][:, c, :], xn[:, k, c * P:(c + 1) * P], core["ident"][:, :])
                mm.then_inc(m["tr_done"], 1)

            for t in range(TT):
                transposes(t, t % 2)

            def step(g, k, position):
                pe.wait_ge(m["xT_done"], g * TT + TT)
                for j in range(4):
                    n = g * 4 + j
                    wait_if(pe, m["rest_done"], n - 3)
                    for c in range(DC):
                        mm = pe.matmul(qp[j][:, :], w[:, c, columns[j]:columns[j] + P], xT[:, k, c, :],
                                       start=(c == 0), stop=(c == DC - 1))
                    mm.then_inc(m["q_ready"], 1)
                    if position != "last":
                        transposes(g * TT + (TT + j), j % 2)
                for j in range(TT):
                    t = g * TT + j
                    wait_if(pe, m["v_done"], t - 1)
                    for c in range(DC):
                        mm = pe.matmul(vp[j % 2][:, :, :].rearrange("p h e -> p (h e)"), xT[:, k, c, j * P:(j + 1) * P],
                                       w[:, c, D:2 * D], start=(c == 0), stop=(c == DC - 1))
                    mm.then_inc(m["v_ready"], 1)

            groups(pe, step)

        @block.scalar
        def _(act):
            act_std(act, ln, core["cols"][:, 0:1])

            def xT_out(t, k, gk, j):
                act.wait_ge(m["tr_done"], t + 1)
                act.activation(xT[:, gk, :, j * P:(j + 1) * P], trp[k][:, :, :], ACT.Copy).then_inc(m["xT_done"], 1)

            def second_part(n, j):
                act.wait_ge(m["rest_done"], n + 1)
                act.activation(parts[j][:, 1, :], rest[:, j % 2, :], ACT.Copy).then_inc(m["part2"], 1)

            for t in range(TT):
                xT_out(t, t % 2, 0, t)

            def step(g, k, position):
                if position != "last":
                    wait_if(act, m["v_ready"], g * TT)
                for j in range(4):
                    n = g * 4 + j
                    act.wait_ge(m["q_ready"], n + 1)
                    wait_if(act, stored[j], g * 16)
                    act.activation(parts[j][:, 0, :], qp[j][:, :], ACT.Copy).then_inc(m["part1"], 1)
                    if position != "last":
                        xT_out(g * TT + (TT + j), j % 2, 1 - k, j)
                    if not (position == "first" and j == 0):
                        second_part(n - 1, (j + 3) % 4)

            groups(act, step)
            second_part(G * 4 - 1, 3)

        @block.vector
        def _(dve):
            dve.memset(v_ones[:, :, :, HD:HD + 1], 1.0).then_inc(m["ones_set"], 1)
            dve_stats(dve, x, T, ln)

            def normalise(t, k):
                wait_if(dve, m["tr_done"], t - 1)
                dve_normalise(dve, xn[:, k, :], x, ln, t).then_inc(m["xn_ready"], 1)

            def third_part(n, j):
                dve.wait_ge(m["part2"], n + 1)
                dve.tensor_tensor(parts[j][:, 2, :], rest[:, j % 2, :], parts[j][:, 1, :],
                                  ALU.subtract).then_inc(m["part3"], 1)

            for t in range(TT):
                normalise(t, t % 2)

            def step(g, k, position):
                if position != "last":
                    normalise(g * TT + TT, 0)
                for j in range(4):
                    n = g * 4 + j
                    dve.wait_ge(m["part1"], n + 1)
                    wait_if(dve, m["part3"], n - 1)
                    dve.tensor_tensor(rest[:, j % 2, :], qp[j][:, :], parts[j][:, 0, :],
                                      ALU.subtract).then_inc(m["rest_done"], 1)
                    if position != "last" and j < TT - 1:
                        normalise(g * TT + (TT + j + 1), (j + 1) % 2)
                    if not (position == "first" and j == 0):
                        third_part(n - 1, (j + 3) % 4)
                for j in range(TT):
                    t = g * TT + j
                    dve.wait_ge(m["v_ready"], t + 1)
                    dve.tensor_copy(v_ones[:, t, :, 0:HD], vp[j % 2][:, :, :]).then_inc(m["v_done"], 1)

            groups(dve, step)
            third_part(G * 4 - 1, 3)


def softmax_heads(nc, core, stage, ins, qk_parts, v_ones, raw_dram, H, HD):
    T = core["T"]
    Tok = T * P
    Q_PARTS, K_PARTS = (0, 0, 0, 1, 1, 2), (0, 1, 2, 0, 1, 0)
    R = HD * len(Q_PARTS)
    TG = 4
    G = T // TG
    N = TG * P
    M = 2 * (HD + 1)
    SCALE = float(D) ** -0.5

    chunks = [(t, c) for t in range(T) for c in range(t // TG + 1)]
    NA = len(chunks) + 1
    units = [(g, p) for g in range(G) for p in range(2 * g + 2)]
    NB = len(units)
    last_unit = [sum(2 * a + 2 for a in range(g + 1)) - 1 for g in range(G)]
    P_RING, RING = 3, 6
    LAG = 4
    FIRST_A, LAST_A = 4, NB - 4
    share = [[] for _ in range(NB)]
    for n in range(NA - 1):
        share[FIRST_A + n * (LAST_A - FIRST_A) // (NA - 1)].append(n)

    def dve_from(u):
        return N + (N // 2 if share[u] else 0)

    def unit_tiles(u):
        g, pair = units[u]
        return [(2 * pair + kk, max(0, 2 * pair + kk - TG * g) * P) for kk in range(2)]

    def unit_columns(u, first=0, end=2 * N):
        (_, lo0), (_, lo1) = unit_tiles(u)
        ranges = [(lo0, 2 * N)] if lo1 == 0 else [(lo0, N), (N + lo1, 2 * N)]
        cut = [(max(lo, first), min(hi, end)) for lo, hi in ranges]
        return [(lo, hi) for lo, hi in cut if lo < hi]

    with ExitStack() as ctx:
        s = Scope(nc, ctx, stage)
        qs = [s.sb(f"qs{k}", [P, Tok], BF16) for k in range(2)]
        ks = [s.sb(f"ks{k}", [P, Tok], BF16) for k in range(2)]
        vh = [s.sb(f"vh{k}", [P, T, M], F32R) for k in range(2)]
        p = [s.sb(f"p{k}", [P, 2 * N]) for k in range(P_RING)]
        p1 = [s.sb(f"p1{k}", [P, 2 * N], F32R) for k in range(RING)]
        p2 = [s.sb(f"p2{k}", [P, 2 * N], F32R) for k in range(RING)]
        top = [s.sb(f"top{k}", [P, T, G]) for k in range(2)]
        neg, rest = s.sb("neg", [P, 2, T]), s.sb("rest", [P, 2, T])
        neg_parts = s.sb("neg_parts", [P, 3 * T], BF16)
        neg_rows = s.sb("neg_rows", [3 * T, P], BF16)
        hide_raw = s.sb("hide_raw", [P, 3, P])
        hide_kq, hide_qk, ident = s.sb("hide_kq", [P, P], BF16), s.sb("hide_qk", [P, P], BF16), s.sb("identb", [P, P], BF16)
        v_head = s.sb("v_head", [P, T, HD + 1])
        raw_o = [s.sb(f"raw_o{k}", [M, N]) for k in range(2)]
        ap = [s.ps(f"ap{k}", [P, N]) for k in range(2)]
        st = [s.ps(f"st{k}", [P, 2 * N]) for k in range(2)]
        op = [s.ps(f"op{k}", [P, N]) for k in range(2)]
        hide_in, const_done, ones_set, m_in = (s.sem(n) for n in ("hide_in", "const_done", "ones_set", "m_in"))
        qk_in = [s.sem(f"qk_in{k}") for k in range(2)]
        raw_out = [s.sem(f"raw_out{k}") for k in range(2)]
        names = ("a_ready", "a_free", "max_step", "max_parts", "s_ready", "p_ready", "p2_pool", "p2_dve",
                 "pv_done", "vh_step", "vh_ready", "raw_done")
        m = {n: s.sem(n) for n in names}
        block = ctx.enter_context(nc.Block())
        LOAD = 16 * 9

        def heads(eng, step):
            step(0, 0, 0, False, True)
            step(1, 1, 0, True, True)
            with eng.Fori(0, H // 2 - 2) as i:
                step(i * 2 + 2, 0, i + 1, True, True)
                step(i * 2 + 3, 1, i + 1, True, True)
            step(H - 2, 0, H // 2 - 1, True, True)
            step(H - 1, 1, H // 2 - 1, True, False)

        def behind(h, k, has_prev, u, lag):
            if u >= lag:
                return h, k, u - lag
            return (h - 1, 1 - k, NB + u - lag) if has_prev else None

        @block.sync
        def _(sp):
            for k, name in enumerate(("hide_kq", "hide_qk", "ident")):
                sp.dma_start(hide_raw[:, k, :], ins[name]).then_inc(hide_in, 16)

            def load(h, k):
                for n, part in enumerate(Q_PARTS):
                    sp.dma_start(qs[k][n * HD:(n + 1) * HD, :],
                                 qk_parts[0, part, bass.ts(h, HD), :]).then_inc(qk_in[k], 16)
                row = 0
                for count in (3, 2, 1):
                    src = qk_parts[1, 0:count, bass.ts(h, HD), :]
                    sp.dma_start(ks[k][row:row + count * HD, :], src).then_inc(qk_in[k], 16)
                    row += count * HD

            def maxima(h, k):
                sp.wait_ge(m["a_free"], h * NA + (NA + 2))
                sp.dma_start(qs[k][R:R + 3, :].rearrange("a (t p) -> a t p", p=P), neg_rows[:, :]).then_inc(m_in, 16)

            def store(h, g):
                sp.wait_ge(m["raw_done"], h * G + (g + 3))
                dst = raw_dram[:, :, bass.ts(h, 1), g * N:(g + 1) * N]
                sp.dma_start(dst.rearrange("a e h n -> (a e) (h n)"), raw_o[g % 2][:, :]).then_inc(raw_out[g % 2], 16)

            load(0, 0)
            load(1, 1)
            maxima(0, 0)

            def step(h, k, half, has_prev, has_next):
                if has_prev:
                    store(h - 1, G - 1)
                for g in range(G - 1):
                    store(h, g)
                if has_next:
                    maxima(h + 1, 1 - k)
                    if not (isinstance(h, int) and h == H - 2):
                        sp.wait_ge(m["s_ready"], h * NB + NB)
                        load(h + 2, k)

            heads(sp, step)
            store(H - 1, G - 1)
            sp.wait_ge(m_in, 16 * H)
            for k in range(2):
                sp.wait_ge(raw_out[k], 16 * H * G // 2)

        def pass_a_bank(k, n, first_head):
            return (ap + op)[n % 4] if first_head else ap[(k + n) % 2]

        @block.gpsimd
        def _(pool):
            def take_v(h, k, head_before=None):
                pool.tensor_copy(v_head[:, :, :], v_ones[:, :, h, :]).then_inc(m["vh_step"], 1)
                if head_before is not None:
                    pool.wait_ge(m["pv_done"], head_before * NB + (NB + RING))
                pool.wait_ge(m["vh_step"], h * 2 + 1)
                ones = v_head[:, :, HD:HD + 1].broadcast_to([P, T, HD + 1])
                pool.tensor_tensor(vh[k][:, :, 0:HD + 1], v_head[:, :, :], ones,
                                   ALU.mult).then_inc(m["vh_step"], 1)
                pool.wait_ge(m["vh_step"], h * 2 + 2)
                pool.tensor_tensor(vh[k][:, :, HD + 1:M], v_head[:, :, :], vh[k][:, :, 0:HD + 1].bitcast(F32),
                                   ALU.subtract).then_inc(m["vh_ready"], 1)

            for k in range(2):
                pool.memset(ks[k][R:R + 3, :], 1.0).then_inc(ones_set, 1)
                pool.wait_ge(ones_set, k + 1)
            take_v(0, 0)

            def step(h, k, half, has_prev, has_next):
                for u in range(NB):
                    b = h * NB + u
                    pool.wait_ge(m["p_ready"], b + 3)
                    for lo, hi in unit_columns(u, 0, dve_from(u)):
                        sub = pool.tensor_tensor(p2[u % RING][:, lo:hi], p[u % P_RING][:, lo:hi],
                                                 p1[u % RING][:, lo:hi].bitcast(F32), ALU.subtract)
                    sub.then_inc(m["p2_pool"], 1)
                    if u == LAG + 3 and has_next:
                        take_v(h + 1, 1 - k, h - 1 if has_prev else None)

            heads(pool, step)

        @block.tensor
        def _(pe):
            def pass_a(h, k, n, first_head=False):
                t, c = chunks[n]
                width = min(N, (t + 1) * P - c * N)
                bank = pass_a_bank(k, n, first_head)
                wait_if(pe, m["a_free"], h * NA + (n + 1) - (2 if first_head else 0))
                diagonal = c == t // TG
                mm = pe.matmul(bank[:, 0:width], qs[k][0:R, t * P:(t + 1) * P], ks[k][0:R, c * N:c * N + width],
                               start=True, stop=not diagonal)
                if diagonal:
                    mm = pe.matmul(bank[:, width - P:width], ident[:, :], hide_qk[:, :], start=False, stop=True)
                mm.then_inc(m["a_ready"], 1)

            def transpose_maxima(h, k):
                pe.wait_ge(m["max_parts"], h + 1)
                pe.wait_ge(m["a_free"], h * NA + NA)
                pe.transpose(ap[(k + NA - 1) % 2][0:3 * T, 0:P // 2].bitcast(BF16), neg_parts[:, :],
                             ident[:, :]).then_inc(m["a_ready"], 1)

            def scores(h, k, u):
                g, pair = units[u]
                pe.wait_ge(m["p_ready"], h * NB + (u + 1))
                for kk, (tile, lo) in enumerate(unit_tiles(u)):
                    diagonal = tile >= TG * g
                    mm = pe.matmul(st[u % 2][:, kk * N + lo:(kk + 1) * N], ks[k][0:R + 3, tile * P:(tile + 1) * P],
                                   qs[k][0:R + 3, g * N + lo:(g + 1) * N], start=True, stop=not diagonal)
                    if diagonal:
                        mm = pe.matmul(st[u % 2][:, kk * N + lo:kk * N + lo + P], ident[:, :], hide_kq[:, :],
                                       start=False, stop=True)
                mm.then_inc(m["s_ready"], 1)

            def values(h, k, u):
                g, pair = units[u]
                if u == 0:
                    pe.wait_ge(m["vh_ready"], h + 1)
                pe.wait_ge(m["p2_pool"], h * NB + (u + (1 + P_RING)))
                pe.wait_ge(m["p2_dve"], h * NB + (u + (1 + P_RING)))
                if pair == 0:
                    pe.wait_ge(m["raw_done"], h * G + (g + 1))
                for n, (tile, lo) in enumerate(unit_tiles(u)):
                    for src in (p1, p2):
                        mm = pe.matmul(op[g % 2][0:M, lo:N], vh[k][:, tile, :], src[u % RING][:, n * N + lo:(n + 1) * N],
                                       start=(pair == 0 and n == 0 and src is p1), stop=(tile >= TG * g),
                                       skip_group_check=True)
                mm.then_inc(m["pv_done"], 1)

            pe.wait_ge(const_done, 5)
            pe.wait_ge(hide_in, 48)
            pe.wait_ge(qk_in[0], LOAD)
            for n in range(NA - 1):
                pass_a(0, 0, n, first_head=True)
            transpose_maxima(0, 0)
            pe.wait_ge(ones_set, 2)

            def step(h, k, half, has_prev, has_next):
                pe.wait_ge(m_in, h * 16 + 16)
                for u in range(NB):
                    scores(h, k, u)
                    if has_next:
                        if u == FIRST_A:
                            pe.wait_ge(qk_in[1 - k], (half + 1 + k) * LOAD)
                        for n in share[u][:1]:
                            pass_a(h + 1, 1 - k, n)
                        if u == LAST_A + 2:
                            transpose_maxima(h + 1, 1 - k)
                    if (at := behind(h, k, has_prev, u, LAG)) is not None:
                        values(*at)
                    if has_next:
                        for n in share[u][1:]:
                            pass_a(h + 1, 1 - k, n)

            heads(pe, step)
            for u in range(NB - LAG, NB):
                values(H - 1, 1, u)

        @block.scalar
        def _(act):
            act.wait_ge(hide_in, 48)
            for k, dst in enumerate((hide_kq, hide_qk, ident)):
                act.activation(dst[:, :], hide_raw[:, k, :], ACT.Copy).then_inc(const_done, 1)
            act.sem_inc(m["p_ready"], 2)
            act.sem_inc(m["pv_done"], RING)
            for done in ("p2_pool", "p2_dve"):
                act.sem_inc(m[done], P_RING)

            def step(h, k, half, has_prev, has_next):
                for u in range(NB):
                    b = h * NB + u
                    act.wait_ge(m["s_ready"], b + 1)
                    for done in ("p2_pool", "p2_dve"):
                        act.wait_ge(m[done], b + 1)
                    act.wait_ge(m["pv_done"], b + 1)
                    for dst in (p[u % P_RING], p1[u % RING]):
                        for lo, hi in unit_columns(u):
                            ex = act.activation(dst[:, lo:hi], st[u % 2][:, lo:hi], ACT.Exp, scale=SCALE)
                    ex.then_inc(m["p_ready"], 1)

            heads(act, step)

        @block.vector
        def _(dve):
            for k in range(2):
                dve.memset(top[k][:, :, :], -3.0e38).then_inc(const_done, 1)
            dve.sem_inc(m["a_free"], 2)
            dve.sem_inc(m["raw_done"], 2)
            dve.wait_ge(const_done, 5)

            def reduce(h, k, n, first_head=False):
                t, c = chunks[n]
                width = min(N, (t + 1) * P - c * N)
                dve.wait_ge(m["a_ready"], h * NA + (n + 1))
                dve.reduce_max(top[k][:, t, c:c + 1], pass_a_bank(k, n, first_head)[:, 0:width], AX_X).then_inc(m["a_free"], 1)

            def split_maxima(h, k):
                step = m["max_step"]
                dve.wait_ge(m["a_free"], h * NA + (NA + 1))
                dve.tensor_reduce(neg[:, 0, :], top[k][:, :, :], AX_X, ALU.max).then_inc(step, 1)
                dve.wait_ge(step, h * 6 + 1)
                dve.tensor_scalar(neg[:, 1, :], neg[:, 0, :], -1.0, None, ALU.mult).then_inc(step, 1)
                src = neg[:, 1, :]
                for k3 in range(2):
                    part = neg_parts[:, k3 * T:(k3 + 1) * T]
                    dve.wait_ge(step, h * 6 + (2 + 2 * k3))
                    dve.tensor_copy(part, src).then_inc(step, 1)
                    dve.wait_ge(step, h * 6 + (3 + 2 * k3))
                    dve.tensor_tensor(rest[:, k3, :], src, part, ALU.subtract).then_inc(step, 1)
                    src = rest[:, k3, :]
                dve.wait_ge(step, h * 6 + 6)
                dve.tensor_copy(neg_parts[:, 2 * T:3 * T], src).then_inc(m["max_parts"], 1)

            def maxima_out(h, k):
                dve.wait_ge(m["a_ready"], h * NA + NA)
                wait_if(dve, m_in, h * 16)
                dve.tensor_copy(neg_rows[:, :], ap[(k + NA - 1) % 2][0:3 * T, 0:P // 2].bitcast(BF16)
                                ).then_inc(m["a_free"], 1)

            def raw_output(h, g):
                dve.wait_ge(m["pv_done"], h * NB + (last_unit[g] + 1 + RING))
                wait_if(dve, raw_out[g % 2], h * (16 * G // 2) + 16 * (g // 2))
                dve.tensor_copy(raw_o[g % 2][:, :], op[g % 2][0:M, :]).then_inc(m["raw_done"], 1)

            def second_parts(h, u):
                dve.wait_ge(m["p_ready"], h * NB + (u + 3))
                for lo, hi in unit_columns(u, dve_from(u)):
                    sub = dve.tensor_tensor(p2[u % RING][:, lo:hi], p[u % P_RING][:, lo:hi],
                                            p1[u % RING][:, lo:hi].bitcast(F32), ALU.subtract)
                sub.then_inc(m["p2_dve"], 1)

            for n in range(NA - 1):
                reduce(0, 0, n, first_head=True)
            split_maxima(0, 0)
            maxima_out(0, 0)

            def step(h, k, half, has_prev, has_next):
                for u in range(NB):
                    if has_next:
                        for n in share[u]:
                            reduce(h + 1, 1 - k, n)
                        if share[u] and share[u][-1] == NA - 2:
                            split_maxima(h + 1, 1 - k)
                        if u == LAST_A + 2:
                            maxima_out(h + 1, 1 - k)
                    if (at := behind(h, k, has_prev, u, 1)) is not None:
                        second_parts(at[0], at[2])
                    if (at := behind(h, k, has_prev, u, LAG)) is not None and at[2] in last_unit:
                        raw_output(at[0], last_unit.index(at[2]))

            heads(dve, step)
            second_parts(H - 1, NB - 1)
            raw_output(H - 1, G - 1)


def softmax_output(nc, core, stage, ins, raw_dram, H, HD):
    T, x = core["T"], core["x"]
    TG = 4
    G = T // TG
    N = TG * P
    with ExitStack() as ctx:
        s = Scope(nc, ctx, stage)
        wo = s.sb("wo", [P, DC, D])
        spread = s.sb("spread", [H, P])
        oT = [s.sb(f"oT{k}", [P, 2, DC, N]) for k in range(2)]
        den = [s.sb(f"den{k}", [H, 2, N]) for k in range(2)]
        den_sum = [s.sb(f"den_sum{k}", [H, N]) for k in range(2)]
        rden = [s.sb(f"rden{k}", [H, N]) for k in range(2)]
        o_sum = [s.sb(f"o_sum{k}", [P, DC, N]) for k in range(2)]
        o = [s.sb(f"o{k}", [P, DC, N]) for k in range(2)]
        rp = [s.ps(f"rp{k}", [P, N]) for k in range(2)]
        yp = [s.ps(f"yp{k}", [P, D]) for k in range(4)]
        w_in = s.sem("w_in")
        oT_in = [s.sem(f"oT_in{k}") for k in range(2)]
        names = ("sum_done", "den_done", "rden_done", "spread_done", "o_done", "y_ready", "x_done")
        m = {n: s.sem(n) for n in names}
        block = ctx.enter_context(nc.Block())

        @block.sync
        def _(sp):
            sp.dma_start(wo[:, :, :], ins["swo"].rearrange("p (c n) -> p c n", c=DC)).then_inc(w_in, 16)
            sp.dma_start(spread[:, :], ins["spread"]).then_inc(w_in, 16)

            def load(g, k):
                for a in range(2):
                    sp.dma_start(den[k][:, a, :], raw_dram[a, HD, :, bass.ts(g, N)]).then_inc(oT_in[k], 16)
                for a in range(2):
                    src = raw_dram[a, 0:HD, :, bass.ts(g, N)].rearrange("(c d) h n -> (d h) c n", c=DC)
                    sp.dma_start(oT[k][:, a, :, :], src).then_inc(oT_in[k], 16)

            load(0, 0)
            load(1, 1)
            with sp.Fori(0, G // 2 - 1) as i:
                for k in range(2):
                    sp.wait_ge(m["sum_done"], i * 2 + (k + 1))
                    sp.wait_ge(m["den_done"], i * 2 + (k + 1))
                    load(i * 2 + (2 + k), k)

        @block.gpsimd
        def _(pool):
            for k in range(2):
                pool.sem_inc(m["o_done"], 1)
            with pool.Fori(0, G // 2) as i:
                for k in range(2):
                    pool.wait_ge(oT_in[k], i * 64 + 64)
                    pool.wait_ge(m["rden_done"], i * 2 + (k + 1))
                    pool.tensor_tensor(den_sum[k][:, :], den[k][:, 0, :], den[k][:, 1, :],
                                       ALU.add).then_inc(m["den_done"], 1)
                    pool.wait_ge(m["o_done"], i * 2 + (k + 1))
                    pool.tensor_tensor(o_sum[k][:, :, :], oT[k][:, 0, :, :], oT[k][:, 1, :, :],
                                       ALU.add).then_inc(m["sum_done"], 1)

        @block.tensor
        def _(pe):
            pe.wait_ge(w_in, 32)

            def spread_rden(g, k):
                pe.wait_ge(m["rden_done"], g + 3)
                pe.wait_ge(m["o_done"], g + 1)
                pe.matmul(rp[k][:, :], spread[:, :], rden[k][:, :], start=True, stop=True).then_inc(m["spread_done"], 1)

            def project(g, k):
                pe.wait_ge(m["o_done"], g + 3)
                for t in range(TG):
                    pe.wait_ge(m["x_done"], g * TG + (t + 1))
                    for c in range(DC):
                        mm = pe.matmul(yp[t][:, :], o[k][:, c, t * P:(t + 1) * P], wo[:, c, :],
                                       start=(c == 0), stop=(c == DC - 1))
                    mm.then_inc(m["y_ready"], 1)

            spread_rden(0, 0)
            with pe.Fori(0, G // 2 - 1) as i:
                for k in range(2):
                    spread_rden(i * 2 + (k + 1), 1 - k)
                    project(i * 2 + k, k)
            spread_rden(G - 1, 1)
            project(G - 2, 0)
            project(G - 1, 1)

        @block.vector
        def _(dve):
            dve.sem_inc(m["x_done"], TG)
            dve.sem_inc(m["spread_done"], 2)
            dve.sem_inc(m["rden_done"], 2)

            def invert(g, k):
                dve.wait_ge(m["den_done"], g + 1)
                dve.wait_ge(m["spread_done"], g + 1)
                dve.reciprocal(rden[k][:, :], den_sum[k][:, :]).then_inc(m["rden_done"], 1)

            def divide(g, k):
                dve.wait_ge(m["sum_done"], g + 1)
                dve.wait_ge(m["spread_done"], g + 3)
                dve.tensor_tensor(o[k][:, :, :], o_sum[k][:, :, :],
                                  rp[k][:, :].unsqueeze(1).broadcast_to([P, DC, N]), ALU.mult).then_inc(m["o_done"], 1)

            def add_y(g):
                for t in range(TG):
                    dve.wait_ge(m["y_ready"], g * TG + (t + 1))
                    dve.tensor_tensor(x[:, g * TG + t, :], yp[t][:, :], x[:, g * TG + t, :],
                                      ALU.add).then_inc(m["x_done"], 1)

            invert(0, 0)
            invert(1, 1)
            divide(0, 0)
            with dve.Fori(0, G // 2 - 1) as i:
                for k in range(2):
                    invert(i * 2 + (k + 2), k)
                    divide(i * 2 + (k + 1), 1 - k)
                    add_y(i * 2 + k)
            divide(G - 1, 1)
            add_y(G - 2)
            add_y(G - 1)


STAGES = ['moe', 'lin', 'moe', 'spike', 'soft', 'spike']


def build(nc, ins, out_dram):
    Tok = ins["x"].shape[0]
    T = Tok // P
    with ExitStack() as ctx:
        s = Scope(nc, ctx, "core")
        NE = ins["up"].shape[0]
        core = dict(T=T, x=s.sb("x", [P, T, D]), ident=s.sb("ident", [P, P]), cols=s.sb("cols", [P, 4]),
                    iota8=s.sb("iota8", [P, 8]), comb=s.sb("comb", [P, T, NE]))
        for n, kind in enumerate(STAGES):
            if kind in ("moe", "spike"):
                with ExitStack() as parts:
                    sp = Scope(nc, parts, f"{kind}{n}")
                    x1 = sp.sb("xT1", [P, DC, Tok], F32R)
                    x2 = sp.sb("xT2", [P, DC, Tok], F32R)
                    router = dict(E=NE - 1, w=ins["rw"], b=ins["rb"]) if kind == "moe" else None
                    first, second = (ins["up"][0], ins["dn"][0]) if kind == "moe" else (ins["fc"], ins["proj"])
                    weights = []
                    for j, src in enumerate((first, second)):
                        shape = list(src.shape)
                        weights.append((sp.sb(f"raw{j}", shape), src, sp.sb(f"first{j}", shape, F32R),
                                        sp.sb(f"second{j}", shape, F32R)))
                    stage_norm(nc, core, f"norm{n}", x1, x2, router, weights, (ins["x"], ins) if n == 0 else None)
                    if kind == "moe":
                        stage_experts(nc, core, f"experts{n}", x1, x2, *weights, ins["up"], ins["dn"], NE)
                    else:
                        stage_spikes(nc, core, f"spikes{n}", x1, x2, *weights,
                                     out_dram=out_dram if n == len(STAGES) - 1 else None)
            if kind == "lin":
                stage_linear_attention(nc, core, f"lin{n}", ins)
            if kind == "soft":
                stage_softmax_attention(nc, core, f"soft{n}", ins)


def kernel(**inputs):
    import numpy as np
    import concourse.bacc as _bacc
    from concourse.bass_utils import run_bass_kernel_spmd as _run

    a = {k: np.asarray(v) for k, v in inputs.items()}

    def by_rows(w):
        r, n = w.shape
        return np.ascontiguousarray(w.reshape(r // P, P, n).transpose(1, 0, 2).reshape(P, -1))

    x = a["L0_attn_x"]
    up = np.concatenate([a["L0_ffn_w_up"], a["L0_ffn_shared_w_up"]])
    dn = np.concatenate([a["L0_ffn_w_down"], a["L0_ffn_shared_w_down"]])
    H0, H1 = 8, 16
    cols = np.zeros((P, 4), np.float32)
    cols[:, 0] = EPS
    sign = np.where((np.arange(P) // 32) % 2 == 0, 1.0, -1.0)
    cols[:, 1] = sign
    cols[:, 2] = 1.0
    cols[:, 3] = -0.5
    k_after_q = np.arange(P)[:, None] > np.arange(P)[None, :]
    spread = np.tile(np.eye(H1, dtype=np.float32), (1, P // H1))
    arrays = {
        "spread": spread,
        "x": x.reshape(-1, D),
        "up": np.stack([by_rows(w.T) for w in up]),
        "dn": np.stack([by_rows(w.T) for w in dn]),
        "rw": by_rows(a["L0_ffn_router_w"].T).reshape(P, DC, -1),
        "rb": np.broadcast_to(a["L0_ffn_router_b"], (P, a["L0_ffn_router_b"].shape[0])),
        "ident": np.eye(P, dtype=np.float32),
        "cols": cols,
        "iota8": np.broadcast_to(np.arange(8, dtype=np.float32), (P, 8)),
        "keep_kq": (~k_after_q).astype(np.float32),
        "hide_kq": np.where(k_after_q, -1e30, 0.0).astype(np.float32),
        "hide_qk": np.where(k_after_q.T, -1e30, 0.0).astype(np.float32),
        "fc": by_rows(a["L1_ffn_W_fc"].T),
        "proj": by_rows(a["L1_ffn_W_proj"].T),
        "lwq": by_rows(a["L0_attn_Wq"]),
        "lwk": by_rows(a["L0_attn_Wk"]),
        "lwv": by_rows(a["L0_attn_Wv"].T),
        "lwo": by_rows(a["L0_attn_Wo"].T),
        "lfq": np.ascontiguousarray(a["L0_attn_fmq_w"].T),
        "lfk": np.ascontiguousarray(a["L0_attn_fmk_w"].T),
        "lbq": np.tile(a["L0_attn_fmq_b"], 4)[:, None],
        "lbk": np.tile(a["L0_attn_fmk_b"], 4)[:, None],
        "lrms": np.tile(a["L0_attn_rms_w"], 4)[:, None],
        "swqvk": by_rows(a["L1_attn_Wqvk"]),
        "swo": by_rows(a["L1_attn_Wo"].reshape(H1, -1, D).transpose(1, 0, 2).reshape(D, D)),
    }
    nc = _bacc.Bacc("TRN2", target_bir_lowering=False, num_devices=1)
    ins = {}
    used = {f"in_{k}": np.ascontiguousarray(v) for k, v in arrays.items()}
    for name, v in arrays.items():
        ins[name] = nc.dram_tensor(f"in_{name}", v.shape, mybir.dt.from_np(v.dtype), kind="ExternalInput").ap()
    out = nc.dram_tensor("out_0", (x.shape[0] * x.shape[1], D), F32, kind="ExternalOutput").ap()
    build(nc, ins, out)
    r = _run(nc, [used], core_ids=[0])
    return r.results[0]["out_0"].reshape(x.shape)
```
